# Optimizing a Trainium2 kernel written in Bass

```python
import numpy as np
import jax
import jax.numpy as jnp

def _softmax(x, axis=-1):
    return jax.nn.softmax(x, axis=axis)

def _gelu(x):
    return jax.nn.gelu(x, approximate=True)

def _silu(x):
    return jax.nn.silu(x)

def _sigmoid(x):
    return jax.nn.sigmoid(x)

def _layernorm(x, axis=-1, eps=1e-05):
    m = jnp.mean(x, axis=axis, keepdims=True)
    v = jnp.var(x, axis=axis, keepdims=True)
    return (x - m) / jnp.sqrt(v + eps)

def _scatter_add(tgt, idx, src, axis=0):
    return tgt.at[idx].add(src)

def _segment_sum(src, seg, n):
    return jax.ops.segment_sum(src, seg, n)
kernel_name = 'mk_gnn_ffn_d2_gnn_r8_909142'

def setup_inputs(seed: int=0):
    np.random.seed(seed)
    _w = jnp.asarray

    def _rec_inputs():
        import jax
        import jax.numpy as jnp
        _gk = jax.random.key(seed)
        x = -0.0002117 + 1 * jax.random.normal(jax.random.fold_in(_gk, 1), (1250, 512), jnp.float32)
        _s = jax.random.randint(jax.random.fold_in(_gk, 2), (20000,), 0, 1250, jnp.int32)
        _d = jax.random.randint(jax.random.fold_in(_gk, 3), (20000,), 0, 1250, jnp.int32)
        _loop = jnp.arange(1250, dtype=jnp.int32)
        src = jnp.concatenate([_s, _d, _loop])
        dst = jnp.concatenate([_d, _s, _loop])
        _o = jnp.argsort(dst, stable=True)
        src = src[_o]
        dst = dst[_o]
        return (x, src, dst)
    x, src, dst = _rec_inputs()

    def _L0_gnn_setup():
        import jax, jax.numpy as jnp
        import numpy as np
        N_NODES = 6250
        N_EDGES = 100000
        HIDDEN = 512
        LAYERS = 3
        key = jax.random.key(seed)
        k1, k2, k3 = jax.random.split(key, 3)
        x = jax.random.normal(k1, (N_NODES, HIDDEN), dtype=jnp.float32)
        edge_index = jax.random.randint(k2, (2, N_EDGES), 0, N_NODES, dtype=jnp.int64)
        W = jax.random.normal(k3, (LAYERS, HIDDEN, HIDDEN), dtype=jnp.float32) / np.float32(np.sqrt(HIDDEN))
        b = jnp.zeros((LAYERS, HIDDEN), dtype=jnp.float32)
        return {'x': x, 'edge_index': edge_index, 'W': W, 'b': b}
    _L0_gnn_all = _L0_gnn_setup()
    _L0_gnn_in = {k: v for k, v in _L0_gnn_all.items() if k in ('W', 'b')}
    del _L0_gnn_all

    def _L0_ffn_setup():
        import jax, jax.numpy as jnp
        import numpy as np
        MARK_AX, OP_ADD, OP_SUB = (0, 1, 2)
        ALU_LO, ALU_HI = (16, 32)
        AX_CARRY_LO, AX_CARRY_HI = (48, 64)
        OPCODE_BASE = 80
        OUTPUT_LO, OUTPUT_HI, CARRY = (128, 144, 160)
        NIB_A, NIB_B, OP_START = (0, 1, 10)
        RESULT, CARRY_OUT = (100, 101)
        GE_POS, GE_DIM = (8, 160)
        OPC_ADD, OPC_SUB = (25, 26)
        B, S, D = (8, 512, 512)

        def _decode_nibble(x, base):
            return jnp.argmax(x[..., base:base + 16] > 0.5, axis=-1).astype(x.dtype)

        def _pipeline(h, W, b):
            for i in range(3):
                h = jnp.einsum('bspd,od->bspo', h, W[i]) + b[i]
                if i < 2:
                    h = jax.nn.relu(h)
            return h
        key = jax.random.key(seed)
        kx, k1, k2, k3, k4 = jax.random.split(key, 5)
        x_bd = jax.random.uniform(kx, (B, S, D), dtype=jnp.float32)
        Wa = jax.random.normal(k1, (3, GE_DIM, GE_DIM), dtype=jnp.float32) * 0.05
        ba = jax.random.normal(k2, (3, GE_DIM), dtype=jnp.float32) * 0.05
        Ws = jax.random.normal(k3, (3, GE_DIM, GE_DIM), dtype=jnp.float32) * 0.05
        bs = jax.random.normal(k4, (3, GE_DIM), dtype=jnp.float32) * 0.05
        return {'x_bd': x_bd, 'Wa': Wa, 'ba': ba, 'Ws': Ws, 'bs': bs}
    _L0_ffn_all = _L0_ffn_setup()
    _L0_ffn_in = {k: v for k, v in _L0_ffn_all.items() if k in ('Wa', 'ba', 'Ws', 'bs')}
    del _L0_ffn_all

    def _L1_gnn_setup():
        import jax, jax.numpy as jnp
        import numpy as np
        N, E, D = (6250, 50000, 512)
        EPS = 1e-05
        key = jax.random.key(seed)
        ks = jax.random.split(key, 5)
        scale = 1.0 / np.sqrt(D)
        x = jax.random.normal(ks[0], (N, D), dtype=jnp.float32)
        edge_index = jax.random.randint(ks[1], (2, E), 0, N, dtype=jnp.int32)
        W_l = jax.random.normal(ks[2], (D, D), dtype=jnp.float32) * scale
        b_l = jnp.zeros((D,), dtype=jnp.float32)
        W_r = jax.random.normal(ks[3], (D, D), dtype=jnp.float32) * scale
        gamma = jnp.ones((D,), dtype=jnp.float32)
        beta = jnp.zeros((D,), dtype=jnp.float32)
        return {'x': x, 'edge_index': edge_index, 'W_l': W_l, 'b_l': b_l, 'W_r': W_r, 'gamma': gamma, 'beta': beta}
    _L1_gnn_all = _L1_gnn_setup()
    _L1_gnn_in = {k: v for k, v in _L1_gnn_all.items() if k in ('W_l', 'b_l', 'W_r', 'gamma', 'beta')}
    del _L1_gnn_all

    def _L1_ffn_setup():
        import jax, jax.numpy as jnp
        import numpy as np
        B, S, D = (4, 256, 512)
        I = 384
        E = 16
        K = 2

        def _inv_softplus(v):
            return float(np.log(np.expm1(v)))

        def swiglu5(h, alpha, gate_scale, up_shift, gate_clamp_raw, up_clamp_raw):
            gate_clamp = jax.nn.softplus(gate_clamp_raw)
            up_clamp = jax.nn.softplus(up_clamp_raw)
            g = jnp.clip(h[..., ::2], -gate_clamp, gate_clamp)
            u = jnp.clip(h[..., 1::2], -up_clamp, up_clamp)
            return g * jax.nn.sigmoid(g * alpha) * gate_scale * (u + up_shift)
        key = jax.random.key(seed)
        ks = jax.random.split(key, 10)
        std = 0.02
        raw = _inv_softplus(7.0)
        act = jnp.array([1.702, 1.0, 1.0, raw, raw], dtype=jnp.float32)
        return {'x': jax.random.normal(ks[0], (B, S, D), dtype=jnp.float32), 'gate_w': jax.random.normal(ks[1], (D, E), dtype=jnp.float32) * 0.01, 'gate_b': jnp.zeros((E,), dtype=jnp.float32), 'shared_w1': jax.random.normal(ks[2], (D, 2 * I), dtype=jnp.float32) * std, 'shared_b1': jnp.zeros((2 * I,), dtype=jnp.float32), 'shared_w2': jax.random.normal(ks[3], (I, D), dtype=jnp.float32) * std, 'shared_b2': jnp.zeros((D,), dtype=jnp.float32), 'shared_act': act, 'expert_w1': jax.random.normal(ks[4], (E, D, 2 * I), dtype=jnp.float32) * std, 'expert_b1': jnp.zeros((E, 2 * I), dtype=jnp.float32), 'expert_w2': jax.random.normal(ks[5], (E, I, D), dtype=jnp.float32) * std, 'expert_b2': jnp.zeros((E, D), dtype=jnp.float32), 'expert_act': jnp.tile(act[None, :], (E, 1))}
    _L1_ffn_all = _L1_ffn_setup()
    _L1_ffn_in = {k: v for k, v in _L1_ffn_all.items() if k in ('gate_w', 'gate_b', 'shared_w1', 'shared_b1', 'shared_w2', 'shared_b2', 'shared_act', 'expert_w1', 'expert_b1', 'expert_w2', 'expert_b2', 'expert_act')}
    del _L1_ffn_all
    return {'x': x, 'src': src, 'dst': dst, 'L0_gnn_W': _L0_gnn_in['W'], 'L0_gnn_b': _L0_gnn_in['b'], 'L0_ffn_Wa': _L0_ffn_in['Wa'], 'L0_ffn_ba': _L0_ffn_in['ba'], 'L0_ffn_Ws': _L0_ffn_in['Ws'], 'L0_ffn_bs': _L0_ffn_in['bs'], 'L1_gnn_W_l': _L1_gnn_in['W_l'], 'L1_gnn_b_l': _L1_gnn_in['b_l'], 'L1_gnn_W_r': _L1_gnn_in['W_r'], 'L1_gnn_gamma': _L1_gnn_in['gamma'], 'L1_gnn_beta': _L1_gnn_in['beta'], 'L1_ffn_gate_w': _L1_ffn_in['gate_w'], 'L1_ffn_gate_b': _L1_ffn_in['gate_b'], 'L1_ffn_shared_w1': _L1_ffn_in['shared_w1'], 'L1_ffn_shared_b1': _L1_ffn_in['shared_b1'], 'L1_ffn_shared_w2': _L1_ffn_in['shared_w2'], 'L1_ffn_shared_b2': _L1_ffn_in['shared_b2'], 'L1_ffn_shared_act': _L1_ffn_in['shared_act'], 'L1_ffn_expert_w1': _L1_ffn_in['expert_w1'], 'L1_ffn_expert_b1': _L1_ffn_in['expert_b1'], 'L1_ffn_expert_w2': _L1_ffn_in['expert_w2'], 'L1_ffn_expert_b2': _L1_ffn_in['expert_b2'], 'L1_ffn_expert_act': _L1_ffn_in['expert_act']}

def reference(x, src, dst, L0_gnn_W, L0_gnn_b, L0_ffn_Wa, L0_ffn_ba, L0_ffn_Ws, L0_ffn_bs, L1_gnn_W_l, L1_gnn_b_l, L1_gnn_W_r, L1_gnn_gamma, L1_gnn_beta, L1_ffn_gate_w, L1_ffn_gate_b, L1_ffn_shared_w1, L1_ffn_shared_b1, L1_ffn_shared_w2, L1_ffn_shared_b2, L1_ffn_shared_act, L1_ffn_expert_w1, L1_ffn_expert_b1, L1_ffn_expert_w2, L1_ffn_expert_b2, L1_ffn_expert_act):
    import jax
    import jax.numpy as jnp

    def _L0_gnn_ref(x, edge_index, W, b):
        import jax, jax.numpy as jnp
        import numpy as np
        N_NODES = 6250
        N_EDGES = 100000
        HIDDEN = 512
        LAYERS = 3
        n = x.shape[0]
        loops = jnp.arange(n, dtype=edge_index.dtype)
        src = jnp.concatenate([edge_index[0], loops])
        dst = jnp.concatenate([edge_index[1], loops])
        deg = jax.ops.segment_sum(jnp.ones_like(dst, dtype=x.dtype), dst, num_segments=n)
        dis = jax.lax.rsqrt(jnp.maximum(deg, 1.0))
        norm = (dis[src] * dis[dst])[:, None]
        for l in range(W.shape[0]):
            h = x @ W[l]
            msg = h[src] * norm
            agg = jax.ops.segment_sum(msg, dst, num_segments=n) + b[l]
            x = jax.nn.relu(agg)
        return x

    def _L0_ffn_ref(x_bd, Wa, ba, Ws, bs):
        import jax, jax.numpy as jnp
        import numpy as np
        MARK_AX, OP_ADD, OP_SUB = (0, 1, 2)
        ALU_LO, ALU_HI = (16, 32)
        AX_CARRY_LO, AX_CARRY_HI = (48, 64)
        OPCODE_BASE = 80
        OUTPUT_LO, OUTPUT_HI, CARRY = (128, 144, 160)
        NIB_A, NIB_B, OP_START = (0, 1, 10)
        RESULT, CARRY_OUT = (100, 101)
        GE_POS, GE_DIM = (8, 160)
        OPC_ADD, OPC_SUB = (25, 26)
        B, S, D = (8, 512, 512)

        def _decode_nibble(x, base):
            return jnp.argmax(x[..., base:base + 16] > 0.5, axis=-1).astype(x.dtype)

        def _pipeline(h, W, b):
            for i in range(3):
                h = jnp.einsum('bspd,od->bspo', h, W[i]) + b[i]
                if i < 2:
                    h = jax.nn.relu(h)
            return h
        x = x_bd
        Bsz, seq, _ = x.shape
        x_ge = jnp.zeros((Bsz, seq, GE_POS, GE_DIM), dtype=x.dtype)
        x_ge = x_ge.at[..., 0, NIB_A].set(_decode_nibble(x, ALU_LO))
        x_ge = x_ge.at[..., 1, NIB_A].set(_decode_nibble(x, ALU_HI))
        x_ge = x_ge.at[..., 0, NIB_B].set(_decode_nibble(x, AX_CARRY_LO))
        x_ge = x_ge.at[..., 1, NIB_B].set(_decode_nibble(x, AX_CARRY_HI))
        x_ge = x_ge.at[..., :, OP_START + OPC_ADD].set(x[..., OPCODE_BASE + OPC_ADD][..., None])
        x_ge = x_ge.at[..., :, OP_START + OPC_SUB].set(x[..., OPCODE_BASE + OPC_SUB][..., None])
        mark = x[..., MARK_AX] > 0.5
        m_add = mark & (x[..., OP_ADD] > 0.5)
        m_sub = mark & ~(x[..., OP_ADD] > 0.5) & (x[..., OP_SUB] > 0.5)
        active = (m_add | m_sub).astype(x.dtype)
        y_add = _pipeline(x_ge, Wa, ba)
        y_sub = _pipeline(x_ge, Ws, bs)
        y = jnp.where(m_add[..., None, None], y_add, jnp.where(m_sub[..., None, None], y_sub, x_ge))
        res_lo = jnp.clip(jnp.round(y[..., 0, RESULT]), 0, 15).astype(jnp.int32)
        res_hi = jnp.clip(jnp.round(y[..., 1, RESULT]), 0, 15).astype(jnp.int32)
        oh_lo = jax.nn.one_hot(res_lo, 16, dtype=x.dtype) * active[..., None]
        oh_hi = jax.nn.one_hot(res_hi, 16, dtype=x.dtype) * active[..., None]
        carry = (jnp.round(y[..., 1, CARRY_OUT]) > 0.5).astype(x.dtype) * active
        out = x
        out = out.at[..., OUTPUT_LO:OUTPUT_LO + 16].add(2.0 * oh_lo)
        out = out.at[..., OUTPUT_HI:OUTPUT_HI + 16].add(2.0 * oh_hi)
        out = out.at[..., CARRY].add(carry)
        return out

    def _L1_gnn_ref(x, edge_index, W_l, b_l, W_r, gamma, beta):
        import jax, jax.numpy as jnp
        import numpy as np
        N, E, D = (6250, 50000, 512)
        EPS = 1e-05
        n = x.shape[0]
        src, dst = (edge_index[0], edge_index[1])
        agg = jax.ops.segment_sum(x[src], dst, num_segments=n)
        cnt = jax.ops.segment_sum(jnp.ones((src.shape[0],), x.dtype), dst, num_segments=n)
        mean_agg = agg / jnp.maximum(cnt, 1.0)[:, None]
        h = mean_agg @ W_l.T + b_l + x @ W_r.T
        mu = jnp.mean(h, axis=0)
        var = jnp.var(h, axis=0)
        h = (h - mu) * jax.lax.rsqrt(var + EPS) * gamma + beta
        return jax.nn.relu(h) + x

    def _L1_ffn_ref(x, gate_w, gate_b, shared_w1, shared_b1, shared_w2, shared_b2, shared_act, expert_w1, expert_b1, expert_w2, expert_b2, expert_act):
        import jax, jax.numpy as jnp
        import numpy as np
        B, S, D = (4, 256, 512)
        I = 384
        E = 16
        K = 2

        def _inv_softplus(v):
            return float(np.log(np.expm1(v)))

        def swiglu5(h, alpha, gate_scale, up_shift, gate_clamp_raw, up_clamp_raw):
            gate_clamp = jax.nn.softplus(gate_clamp_raw)
            up_clamp = jax.nn.softplus(up_clamp_raw)
            g = jnp.clip(h[..., ::2], -gate_clamp, gate_clamp)
            u = jnp.clip(h[..., 1::2], -up_clamp, up_clamp)
            return g * jax.nn.sigmoid(g * alpha) * gate_scale * (u + up_shift)
        shape = x.shape
        xf = x.reshape(-1, shape[-1])
        h = xf @ shared_w1 + shared_b1
        t = swiglu5(h, shared_act[0], shared_act[1], shared_act[2], shared_act[3], shared_act[4])
        z = t @ shared_w2 + shared_b2
        gate_logits = xf @ gate_w + gate_b
        gate_probs = jax.nn.softmax(gate_logits, -1)
        w, idx = jax.lax.top_k(gate_probs, K)
        w = w / jnp.sum(w, axis=-1, keepdims=True)
        cw = jnp.sum(jax.nn.one_hot(idx, E, dtype=xf.dtype) * w[..., None], axis=1)
        he = jnp.einsum('nd,edh->enh', xf, expert_w1) + expert_b1[:, None, :]
        a = expert_act
        te = swiglu5(he, a[:, 0, None, None], a[:, 1, None, None], a[:, 2, None, None], a[:, 3, None, None], a[:, 4, None, None])
        oe = jnp.einsum('enh,ehd->end', te, expert_w2) + expert_b2[:, None, :]
        y = jnp.einsum('ne,end->nd', cw, oe)
        return (y + z).reshape(shape)
    edge_index = jnp.stack([src, dst])
    x = x + _L0_gnn_ref(_layernorm(x, axis=-1), edge_index, L0_gnn_W, L0_gnn_b)
    x = x + _L0_ffn_ref(_layernorm(x, axis=-1)[None], L0_ffn_Wa, L0_ffn_ba, L0_ffn_Ws, L0_ffn_bs)[0]
    x = x + _L1_gnn_ref(_layernorm(x, axis=-1), edge_index, L1_gnn_W_l, L1_gnn_b_l, L1_gnn_W_r, L1_gnn_gamma, L1_gnn_beta)
    x = x + _L1_ffn_ref(_layernorm(x, axis=-1)[None], L1_ffn_gate_w, L1_ffn_gate_b, L1_ffn_shared_w1, L1_ffn_shared_b1, L1_ffn_shared_w2, L1_ffn_shared_b2, L1_ffn_shared_act, L1_ffn_expert_w1, L1_ffn_expert_b1, L1_ffn_expert_w2, L1_ffn_expert_b2, L1_ffn_expert_act)[0]
    return x

_drawn_inputs = setup_inputs


def setup_inputs(seed=0):
    import zlib

    import numpy as np

    out = dict(_drawn_inputs(seed))
    spreads = {'L0_gnn_b': (0.0, 0.1),
     'L1_gnn_b_l': (0.0, 0.8),
     'L1_gnn_gamma': (1.0, 0.2),
     'L1_gnn_beta': (0.0, 0.332),
     'L1_ffn_gate_b': (0.0, 0.329),
     'L1_ffn_shared_b1': (0.0, 0.8),
     'L1_ffn_shared_b2': (0.0, 0.1),
     'L1_ffn_expert_b1': (0.0, 0.8),
     'L1_ffn_expert_b2': (0.0, 0.353)}
    factors = {}
    for name, (base, spread) in spreads.items():
        noise = np.random.default_rng([zlib.crc32(name.encode()), seed]).standard_normal(out[name].shape)
        drawn = base * np.exp(spread * noise) if base else spread * noise
        out[name] = jnp.asarray(drawn.astype(out[name].dtype))
    for name, factor in factors.items():
        out[name] = (out[name] * factor).astype(out[name].dtype)
    return out
```

```python
from contextlib import ExitStack

import concourse.bass as bass
from concourse import mybir

ALU = mybir.AluOpType
ACT = mybir.ActivationFunctionType
AX = mybir.AxisListType
F32 = mybir.dt.float32
F16 = mybir.dt.float16
I32 = mybir.dt.int32

N = 1250
D = 512
E = 41250
NP = 125
NT = N // NP
FT = D // 128
LAYERS = 3
EPS = 1e-5
SPLITS = [(0, 500), (500, 500), (1000, 250)]

CHUNK = 125
CPG = 5
ACTJ = 1
NG = E // (CHUNK * CPG)
WIN = 24
KEYS = NT * WIN
CW = N + WIN
PASSES = (N + WIN - 1) // WIN

GE = 160
GH = GE // 2
FK = 5
POS = 2
ROWS = POS * N
RC = 500
NRC = ROWS // RC
MAGIC = 12582912.0

NEXP = 16
TOPK = 2
INTER = 384
H2 = 2 * INTER
BS = 128
NBE = 36
NBS = 10
NB = NBE + NBS
WBUF = FT * H2 + (INTER // 128) * D + H2 + D
NWB = 3
ASSIGN = TOPK * NT


def build(nc, a, out):
    ctx = ExitStack()
    with ctx:
        def sb(name, shape, dt=F32):
            return ctx.enter_context(nc.sbuf_tensor(name, shape, dt))

        def sem(name):
            return ctx.enter_context(nc.semaphore(name))

        PS = ctx.enter_context(nc.psum_tensor("PS", [128, 8, 512], F32))

        X = sb("X", [128, NT, D])
        XN = sb("XN", [128, NT, D])
        Y = sb("Y", [128, NT, D])
        ZT = sb("ZT", [128, NT * D])
        XT = sb("XT", [128, NT * D])
        BIG = sb("BIG", [128, NT * CW + LAYERS * FT * D])
        CT = BIG[:, 0:NT * CW].rearrange("p (t c) -> p t c", t=NT)
        WG = BIG[:, NT * CW:].rearrange("p (l f n) -> p l f n", l=LAYERS, f=FT)
        zt = ZT[:, 0:FT * N].rearrange("p (f n) -> p f n", f=FT)
        xt = XT[:, 0:FT * N].rearrange("p (f n) -> p f n", f=FT)
        ht = Y[:, :, :].rearrange("p t d -> p (t d)")[:, 0:FT * N].rearrange("p (f n) -> p f n", f=FT)
        h1t = ZT[0:GH, 0:2 * ROWS].rearrange("p (m r) -> p m r", m=2)
        h2t = Y[0:GH, :, :].rearrange("p t d -> p (t d)")[:, 0:2 * ROWS].rearrange("p (m r) -> p m r", m=2)
        ft = XT[0:FK, 0:ROWS]

        at = [0]

        def carve(width, dt=F32):
            w = width if dt is not F16 else (width + 1) // 2
            v = XT[:, at[0]:at[0] + w]
            at[0] += w
            assert at[0] <= NT * D
            return v if dt is F32 else v.bitcast(dt)

        NCH = NG * CPG
        src_i, dst_i = carve(NCH, I32), carve(NCH, I32)
        srcf, dstf, hi, lo, neglo, rel, key = [carve(NCH) for _ in range(7)]
        dist = carve(2 * ACTJ * 128, F16).rearrange("p (b j n) -> p b j n", b=2, j=ACTJ)
        oh_lo = carve(2 * CPG * 128, F16).rearrange("p (b j n) -> p b j n", b=2, j=CPG)
        ohk = [carve(CPG * KEYS, F16).rearrange("p (j n) -> p j n", j=CPG) for _ in range(2)]
        counts = ZT[:, 0:2 * KEYS].rearrange("p (b n) -> p b n", b=2)
        iota_k = sb("iota_k", [128, KEYS], F16)
        wbase = sb("wbase", [128, NG])
        wbase_i = sb("wbase_i", [1, NG], I32)
        bad = sb("bad", [128, 4])
        flag_i = sb("flag_i", [1, 1], I32)

        ident = sb("ident", [128, 128])
        ones = sb("ones", [128, 128])
        below = sb("below", [128, 128])
        stats = sb("stats", [128, NT, 6])
        mv = sb("mv", [128, NT, 2])
        sd = sb("sd", [128, NT])
        rstd = sb("rstd", [128, NT])
        dis = sb("dis", [128, NT])
        invc = sb("invc", [128, N])
        bias = sb("bias", [128, LAYERS, D])
        tmp = sb("tmp", [128, 2, D])

        load = {}

        def loaded(name):
            load[name] = sem("in_" + name)
            return load[name]

        for name in ("x", "edges", "wg", "gb", "ffn", "wlr", "sage", "gate", "acts"):
            loaded(name)
        const_done = sem("const_done")
        step = sem("dve_step")
        var_ready, sd_ready, xn_ready = sem("var_ready"), sem("sd_ready"), sem("xn_ready")
        base_ready, base_read = sem("base_ready"), sem("base_read")
        onehot_ready, group_done = sem("onehot_ready"), sem("group_done")
        lo_ready, dist_ready, onehot_act = sem("lo_ready"), sem("dist_ready"), sem("onehot_act")
        windows_ready, counted, added = sem("windows_ready"), sem("counted"), sem("added")
        bad_ready, bad_sum, flag_ready = sem("bad_ready"), sem("bad_sum"), sem("flag_ready")
        slow_onehot, slow_group = sem("slow_onehot"), sem("slow_group")
        slow_step = sem("slow_step")
        counts_ready = sem("counts_ready")
        deg_ready, deg_copied, degcol_ready = sem("deg_ready"), sem("deg_copied"), sem("degcol_ready")
        y_ready = sem("y_ready")
        agg_ready = sem("agg_ready")
        z_act, z_dve = sem("z_act"), sem("z_dve")
        lin_ready = sem("lin_ready")
        lin_read = sem("lin_read")
        pre_ready = sem("pre_ready")
        feat_ready, feat_t, ft_ready = sem("feat_ready"), sem("feat_t"), sem("ft_ready")
        f1_ready, f2_ready = sem("f1_ready"), sem("f2_ready")
        h1_act, h1_dve, h2_act, h2_dve = sem("h1_act"), sem("h1_dve"), sem("h2_act"), sem("h2_dve")
        f3_ready = sem("f3_ready")
        xtp_ready, xt_act, xt_dve = sem("xtp_ready"), sem("xt_act"), sem("xt_dve")
        minus_ready = sem("minus_ready")
        mean_ps, mean_ready = sem("mean_ps"), sem("mean_ready")
        hp_ready, h_ready = sem("hp_ready"), sem("h_ready")
        hstat, hsd, hscale, hn_ready = sem("hstat"), sem("hsd"), sem("hscale"), sem("hn_ready")
        back_ready, back_read = sem("back_ready"), sem("back_read")
        xn_stored = sem("xn_stored")
        logit_ready, zmax_ready, exp_ready = sem("logit_ready"), sem("zmax_ready"), sem("exp_ready")
        sel_ready, rank_ready = sem("sel_ready"), sem("rank_ready")
        slots_ready, table_ps, tables_ready = sem("slots_ready"), sem("table_ps"), sem("tables_ready")
        sp_ready, sp_exp, sp_one, sp_ln = sem("sp_ready"), sem("sp_exp"), sem("sp_one"), sem("sp_ln")
        gathered = [sem("gathered0"), sem("gathered1")]
        w1_in = [sem("w1_in0"), sem("w1_in1")]
        w2_in = [sem("w2_in0"), sem("w2_in1")]
        xt_ps, xgt_ready = sem("xt_ps"), sem("xgt_ready")
        hb_ready, clip_done, clip_g, gate_sig, t_gs, t_ready = (
            sem("hb_ready"), sem("clip_done"), sem("clip_g"), sem("gate_sig"), sem("t_gs"), sem("t_ready"))
        tt_ps, tt_ready, y_done, yo_ready = sem("tt_ps"), sem("tt_ready"), sem("y_done"), sem("yo_ready")
        stored = [sem("stored0"), sem("stored1")]
        back_in, z_in, sum_ready, out_stored = sem("back_in"), sem("z_in"), sem("sum_ready"), sem("out_stored")

        xn_dram = nc.dram_tensor("xn_dram", [N, D], F32, kind="Internal")
        y_dram = nc.dram_tensor("y_dram", [NB * BS, D], F32, kind="Internal")

        w1f = sb("w1f", [FK, 2, GE])
        w2f = sb("w2f", [GH, 2, 2, GE])
        b2f = sb("b2f", [GH, 2, 2])
        w3f = sb("w3f", [GH, 2, 2, 2])
        b3f = sb("b3f", [128, 2, 2])
        wj = sb("wj", [128, NEXP])
        cj = sb("cj", [128, NEXP])
        fk = sb("fk", [128, NT, 4, 16])
        fm = sb("fm", [128, NT, 4])
        fg = sb("fg", [128, NT, 4])
        feats = sb("feats", [128, POS, NT, FK])
        msk = sb("msk", [128, 8, NT])
        yv = sb("yv", [128, 2, POS * NT, 2])
        res = sb("res", [128, POS * NT, 2])
        oh2 = sb("oh2", [128, NT, 16])
        sage = sb("sage", [128, 3, FT])
        hst = sb("hst", [128, FT, 3, 6])
        hmv = sb("hmv", [128, FT, 2])
        hs = sb("hs", [128, 4, FT])
        gw = sb("gw", [128, FT, NEXP])
        gb = sb("gb", [1, NEXP])
        acts = sb("acts", [128, NEXP + 1, 5])
        clampv = sb("clampv", [128, 5, NEXP + 1, 2])

        bat = [0]

        def bcarve(width):
            v = BIG[:, bat[0]:bat[0] + width]
            bat[0] += width
            assert bat[0] <= NT * CW + LAYERS * FT * D
            return v

        WB = bcarve(NWB * WBUF)
        O_W2 = FT * H2
        O_B1 = O_W2 + (INTER // 128) * D
        O_B2 = O_B1 + H2
        yflat = Y[:, :, :].rearrange("p t d -> p (t d)")
        xg = yflat[:, 0:2 * D].rearrange("p (b d) -> p b d", b=2)
        xgt = yflat[:, 1024:1024 + 2 * D].rearrange("p (b f n) -> p b f n", b=2, f=FT)
        tt = yflat[:, 2048:2048 + 2 * INTER].rearrange("p (b i n) -> p b i n", b=2, i=3)
        yo = yflat[:, 2816:2816 + 2 * D].rearrange("p (b d) -> p b d", b=2)
        gg, uu, ss = [(yflat[:, 3840 + c * INTER:3840 + (c + 1) * INTER], XT[:, c * INTER:(c + 1) * INTER])
                      for c in range(3)]
        tb = ZT[:, 0:2 * INTER].rearrange("p (b i) -> p b i", b=2)
        rat = [2 * INTER]

        def rcarve(*dims):
            n = 1
            for d in dims:
                n *= d
            v = ZT[:, rat[0]:rat[0] + n]
            rat[0] += n
            assert rat[0] <= NT * D, rat[0]
            names = "abcd"[:len(dims)]
            return v if len(dims) == 1 else v.rearrange(
                f"p ({' '.join(names)}) -> p {' '.join(names)}", **{c: d for c, d in zip(names, dims)})

        pr = rcarve(NT, NEXP)
        q = rcarve(NT, NEXP)
        oh = [rcarve(NT, NEXP), rcarve(NT, NEXP)]
        cum = rcarve(NT + 1, NEXP)
        posn = rcarve(NT, NEXP)
        rsmall = rcarve(10, NT)
        blkc = rcarve(6, NEXP)
        thr = rcarve(NT)
        le = rcarve(NEXP, NEXP)
        prod = rcarve(NEXP, NEXP)
        slotf = rcarve(TOPK, NT)
        slotp = rcarve(3, TOPK * NT)
        wsel = rcarve(TOPK, NT)
        nodef = rcarve(NT)
        ohb = rcarve(ASSIGN, 2, NBE)
        cnt_e = rcarve(NBE, NEXP)
        ohr = XT[:, 0:ASSIGN * BS].rearrange("p (a n) -> p a n", a=ASSIGN)
        iota_b = XT[:, ASSIGN * BS:ASSIGN * BS + BS]
        prodb = XT[:, 3000:3000 + NB * NB].rearrange("p (a b) -> p a b", a=NB)
        slot_i = sb("slot_i", [128, TOPK, NT], I32)
        slot_b = sb("slot_b", [128, 2, TOPK * NT], I32)
        idx = sb("idx", [128, 2], I32)
        idx_ready = sem("idx_ready")
        tok = sb("tok", [128, NB], I32)
        wslot = sb("wslot", [128, NB])
        ebf = sb("ebf", [1, 5, NB])
        eb_i = sb("eb_i", [1, 3, NB], I32)

        block = ctx.enter_context(nc.Block())

        def counting(eng, s):
            seen = [0]

            def link(ins):
                seen[0] += 1
                ins.then_inc(s, 1)
                eng.wait_ge(s, seen[0])
            link.seen = seen
            return link

        bank = lambda n: PS[:, n, :]
        CONSTS = 12

        @block.sync
        def _(sp):
            sp.dma_start(src_i[0:CHUNK, :], a["src"]).then_inc(load["edges"], 16)
            sp.dma_start(dst_i[0:CHUNK, :], a["dst"]).then_inc(load["edges"], 16)
            sp.dma_start(X[0:NP, :, :], a["x"].rearrange("(t p) d -> p t d", p=NP)).then_inc(load["x"], 16)
            for l in range(LAYERS):
                sp.dma_start(WG[:, l, :, :], a["W"][l].rearrange("(f p) n -> p f n", p=128)).then_inc(load["wg"], 16)
                sp.dma_start(bias[:, l, :], a["gnn_b"][l:l + 1, :].to_broadcast([128, D])).then_inc(load["gb"], 16)
            for n, (w, b) in enumerate((("WaT", "ba"), ("WsT", "bs"))):
                sp.dma_start(w1f[0:2, n, :], a[w][0, 0:2, :]).then_inc(load["ffn"], 16)
                sp.dma_start(w1f[2:4, n, :], a[w][0, 35:37, :]).then_inc(load["ffn"], 16)
                sp.dma_start(w1f[4:5, n, :], a[b][0:1, :]).then_inc(load["ffn"], 16)
                sp.dma_start(w2f[:, n, :, :], a[w][1].rearrange("(m p) n -> p m n", p=GH)).then_inc(load["ffn"], 16)
                with nc.allow_non_contiguous_dma(reason="small tables"):
                    sp.dma_start(b2f[:, n, :], a[b][1, :].rearrange("(m p) -> p m", p=GH)).then_inc(load["ffn"], 16)
                    sp.dma_start(w3f[:, n, :, :], a[w][2, :, 100:102].rearrange("(m p) n -> p m n", p=GH)).then_inc(load["ffn"], 16)
                sp.dma_start(b3f[:, n, :], a[b][2:3, 100:102].to_broadcast([128, 2])).then_inc(load["ffn"], 16)
            with nc.allow_non_contiguous_dma(reason="small tables"):
                for k, name in enumerate(("b_l", "gamma", "beta")):
                    sp.dma_start(sage[:, k, :], a[name].rearrange("(f p) -> p f", p=128)).then_inc(load["sage"], 16)
            sp.dma_start(gw[:, :, :], a["gate_w"].rearrange("(f p) n -> p f n", p=128)).then_inc(load["gate"], 16)
            sp.dma_start(gb[0:1, :], a["gate_b"].rearrange("(o n) -> o n", o=1)).then_inc(load["gate"], 16)
            sp.dma_start(acts[:, :, :], a["act"].rearrange("(o e) k -> o e k", o=1).to_broadcast([128, NEXP + 1, 5])
                         ).then_inc(load["acts"], 16)
            for l, name in enumerate(("WlT", "WrT")):
                sp.wait_ge(lin_ready, NT * (l + 1))
                sp.dma_start(WG[:, l, :, :], a[name].rearrange("(f p) n -> p f n", p=128)).then_inc(load["wlr"], 16)
            sp.wait_ge(xn_ready, 4 * NT)
            sp.dma_start(xn_dram[:, :].rearrange("(t p) d -> p t d", p=NP), XN[0:NP, :, :]).then_inc(xn_stored, 16)

            sp.wait_ge(tables_ready, 1)

            def load_weights(i, k, b):
                e = sp.value_load(eb_i[0:1, 0, bass.ds(b, 1)], min_val=0, max_val=NEXP)
                off = sp.value_load(eb_i[0:1, 1, bass.ds(b, 1)], min_val=0, max_val=(NWB - 1) * WBUF)
                new = sp.value_load(eb_i[0:1, 2, bass.ds(b, 1)], min_val=0, max_val=1)
                ahead = None
                if not isinstance(b, int):
                    ahead, landed = sp.to_reg(b - NWB + 1), sp.to_reg(i * 32)
                elif b >= NWB:
                    ahead = b - NWB + 1
                if isinstance(b, int) and b >= 2:
                    landed = 32 * i
                sp.wait_ge(tables_ready, 1)
                if not (isinstance(b, int) and b < 2):
                    sp.wait_ge(w1_in[k], landed)
                    sp.wait_ge(w2_in[k], landed)
                if ahead is not None:
                    sp.wait_ge(y_done, ahead)
                w1v = a["w1"][bass.ds(e, 1), :, :].rearrange("o (f p) n -> p (o f) n", p=128)
                sp.dma_start(WB[:, bass.ds(off, FT * H2)].rearrange("p (f n) -> p f n", f=FT), w1v,
                             cond=new).then_inc(w1_in[k], 16)
                sp.dma_start(WB[0:1, bass.ds(off + O_B1, H2)], a["b1"][bass.ds(e, 1), :],
                             cond=new).then_inc(w1_in[k], 16)
                w2v = a["w2"][bass.ds(e, 1), :, :].rearrange("o (f p) n -> p (o f) n", p=128)
                sp.dma_start(WB[:, bass.ds(off + O_W2, (INTER // 128) * D)].rearrange("p (f n) -> p f n", f=INTER // 128),
                             w2v, cond=new).then_inc(w2_in[k], 16)
                sp.dma_start(WB[0:1, bass.ds(off + O_B2, D)], a["b2"][bass.ds(e, 1), :],
                             cond=new).then_inc(w2_in[k], 16)

            for b in range(4):
                load_weights(b // 2, b % 2, b)
            with sp.Fori(2, NB // 2) as i:
                for k in range(2):
                    load_weights(i, k, i * 2 + k)
            sp.wait_ge(stored[0], 16 * (NB // 2))
            sp.wait_ge(stored[1], 16 * (NB // 2))
            sp.dma_start(ZT[0:NP, :].rearrange("p (t d) -> p t d", t=NT),
                         y_dram[NBE * BS:NBE * BS + N, :].rearrange("(t p) d -> p t d", p=NP)).then_inc(z_in, 16)
            for t in range(NT):
                sp.wait_ge(sum_ready, t + 1)
                sp.dma_start(out[t * NP:(t + 1) * NP, :], X[0:NP, t, :]).then_inc(out_stored, 16)
            sp.wait_ge(out_stored, 16 * NT)

        @block.gpsimd
        def _(pool):
            pool.memset(ident[:, :], 0.0).then_inc(const_done, 1)
            pool.memset(ones[:, :], 1.0).then_inc(const_done, 1)
            pool.memset(below[:, :], 1.0).then_inc(const_done, 1)
            pool.iota(iota_k[:, :], pattern=[[1, KEYS]], base=0, channel_multiplier=0,
                      allow_small_or_imprecise_dtypes=True).then_inc(const_done, 1)
            pool.iota(wj[:, :], pattern=[[-1, NEXP]], base=16, channel_multiplier=0,
                      allow_small_or_imprecise_dtypes=True).then_inc(const_done, 1)
            pool.iota(cj[:, :], pattern=[[1, NEXP]], base=0, channel_multiplier=0,
                      allow_small_or_imprecise_dtypes=True).then_inc(const_done, 1)
            pool.wait_ge(const_done, 6)
            pool.affine_select(out=ident[:, :], in_=ident[:, :], compare_op=ALU.not_equal, fill=1.0, base=0,
                               pattern=[[-1, 128]], channel_multiplier=1).then_inc(const_done, 1)
            pool.affine_select(out=below[:, :], in_=below[:, :], compare_op=ALU.is_gt, fill=0.0, base=0,
                               pattern=[[1, 128]], channel_multiplier=-1).then_inc(const_done, 1)
            pool.memset(feats[:, :, :, :], 1.0).then_inc(const_done, 1)
            pool.iota(tok[:, NBE:NB], pattern=[[BS, NBS]], base=0, channel_multiplier=1).then_inc(const_done, 1)
            pool.memset(wslot[:, NBE:NB], 1.0).then_inc(const_done, 1)
            pool.memset(CT[:, :, :], 0.0).then_inc(const_done, 1)

            pool.wait_ge(windows_ready, 1)
            pool.wait_ge(const_done, CONSTS)

            def add_counts(k, g):
                w0 = pool.value_load(wbase_i[0:1, bass.ds(g, 1)], min_val=0, max_val=N - 1)
                pool.wait_ge(counted, g + 1)
                if not isinstance(g, int) or g:
                    pool.wait_ge(added, g)
                dest = CT[0:NP, :, bass.ds(w0, WIN)]
                pool.tensor_tensor(dest, counts[0:NP, k, :].rearrange("p (t w) -> p t w", t=NT), dest, ALU.add
                                   ).then_inc(added, 1)

            add_counts(0, 0)
            add_counts(1, 1)
            with pool.Fori(1, NG // 2) as i:
                for k in range(2):
                    add_counts(k, i * 2 + k)

            pool.wait_ge(hp_ready, FT * len(SPLITS))
            pool.iota(thr[:, :], pattern=[[BS, NT]], base=0, channel_multiplier=0,
                      allow_small_or_imprecise_dtypes=True).then_inc(const_done, 1)
            pool.memset(le[:, :, :], 1.0).then_inc(const_done, 1)
            pool.iota(nodef[:, :], pattern=[[NP, NT]], base=0, channel_multiplier=1,
                      allow_small_or_imprecise_dtypes=True).then_inc(const_done, 1)
            pool.memset(cum[:, 0, :], 0.0).then_inc(const_done, 1)
            pool.iota(cnt_e[:, :, :], pattern=[[1, NBE], [0, NEXP]], base=0, channel_multiplier=0,
                      allow_small_or_imprecise_dtypes=True).then_inc(const_done, 1)
            pool.wait_ge(const_done, CONSTS + 5)
            pool.affine_select(out=le[:, :, :], in_=le[:, :, :], compare_op=ALU.is_ge, fill=0.0, base=0,
                               pattern=[[1, NEXP], [-1, NEXP]], channel_multiplier=0).then_inc(const_done, 1)
            pool.wait_ge(logit_ready, 1)
            pool.iota(iota_b, pattern=[[1, BS]], base=0, channel_multiplier=0,
                      allow_small_or_imprecise_dtypes=True).then_inc(const_done, 1)
            pool.memset(prodb[0:1, :, :], 1.0).then_inc(const_done, 1)
            pool.wait_ge(const_done, CONSTS + 8)
            pool.affine_select(out=prodb[0:1, :, :], in_=prodb[0:1, :, :], compare_op=ALU.is_ge, fill=0.0, base=0,
                               pattern=[[1, NB], [-1, NB]], channel_multiplier=0).then_inc(const_done, 1)

            pool.wait_ge(tables_ready, 1)

            def gather(i, k, b):
                if not (isinstance(b, int) and b < 2):
                    pool.wait_ge(xt_ps, b - 1)
                turn = b + 1 if isinstance(b, int) else pool.to_reg(b + 1)
                pool.tensor_copy(idx[:, k:k + 1], tok[:, bass.ds(b, 1)]).then_inc(idx_ready, 1)
                pool.wait_ge(xn_stored, 16)
                pool.wait_ge(idx_ready, turn)
                pool.indirect_dma_start(xg[:, k, :], None, xn_dram[:, :],
                                        bass.IndirectOffsetOnAxis(idx[:, k:k + 1], 0)
                                        ).then_inc(gathered[k], 16)

            for b in range(2):
                gather(0, b, b)
            with pool.Fori(1, NB // 2) as i:
                for k in range(2):
                    gather(i, k, i * 2 + k)
            pool.wait_ge(stored[0], 16 * (NB // 2))
            pool.wait_ge(stored[1], 16 * (NB // 2))
            for t in range(NT):
                for k, dest in enumerate((XN, Y)):
                    pool.indirect_dma_start(dest[0:NP, t, :], None, y_dram[:, :],
                                            bass.IndirectOffsetOnAxis(slot_i[0:NP, k, t:t + 1], 0)
                                            ).then_inc(back_in, 16)
            pool.wait_ge(back_in, 16 * 2 * NT)

        @block.scalar
        def _(act):
            def sqrt_of_var(k):
                act.wait_ge(var_ready, k + 1)
                nc.scalar.activation(sd[0:NP, :], mv[0:NP, :, 1], ACT.Sqrt).then_inc(sd_ready, 1)

            act.wait_ge(sp_ready, 1)
            nc.scalar.activation(clampv[:, 2, :, :], clampv[:, 1, :, :], ACT.Exp).then_inc(sp_exp, 1)
            act.wait_ge(sp_one, 1)
            nc.scalar.activation(clampv[:, 4, :, :], clampv[:, 3, :, :], ACT.Ln).then_inc(sp_ln, 1)
            act.wait_ge(lo_ready, 1)
            act.wait_ge(const_done, 4)

            def onehots_act(i, k, b):
                for j in range(ACTJ):
                    nc.scalar.activation(dist[0:CHUNK, k, j, 0:NP], iota_k[0:CHUNK, 0:NP], ACT.Abs,
                                         bias=neglo[0:CHUNK, bass.ds(b * CPG + j, 1)]).then_inc(dist_ready, 1)
                for j in range(ACTJ):
                    act.wait_ge(dist_ready, b * ACTJ + (j + 1))
                    ins = nc.scalar.activation(oh_lo[0:CHUNK, k, j, 0:NP], dist[0:CHUNK, k, j, 0:NP], ACT.Relu,
                                               scale=-1.0, bias=ones[0:CHUNK, 0:1])
                ins.then_inc(onehot_act, 1)

            def counts_copy(k, b):
                act.wait_ge(group_done, b + 1)
                if not isinstance(b, int):
                    act.wait_ge(added, b - 1)
                nc.scalar.copy(counts[0:NP, k, :], PS[0:NP, k, 0:KEYS]).then_inc(counted, 1)

            onehots_act(0, 0, 0)
            onehots_act(0, 1, 1)
            counts_copy(0, 0)
            onehots_act(1, 0, 2)
            counts_copy(1, 1)
            onehots_act(1, 1, 3)
            with act.Fori(1, NG // 2 - 1) as i:
                for k in range(2):
                    counts_copy(k, i * 2 + k)
                    onehots_act(i + 1, k, i * 2 + (k + 2))
            for k in range(2):
                act.wait_ge(group_done, NG - 1 + k)
                act.wait_ge(added, NG - 3 + k)
                nc.scalar.copy(counts[0:NP, k, :], PS[0:NP, k, 0:KEYS]).then_inc(counted, 1)
            sqrt_of_var(0)
            act.wait_ge(degcol_ready, 1)
            nc.scalar.activation(dis[0:NP, :], PS[0:NP, 3, 0:NT], ACT.Sqrt).then_inc(sd_ready, 1)

            def z_copy(n, f, c0, w):
                act.wait_ge(agg_ready, n + 1)
                nc.scalar.copy(zt[:, f, c0:c0 + w], PS[:, n % 6, 0:w]).then_inc(z_act, 1)

            n = 0
            for l in range(LAYERS):
                def relu_tiles(tiles):
                    for t in tiles:
                        act.wait_ge(pre_ready, l * NT + t + 1)
                        nc.scalar.activation((XN if l == 0 else Y)[0:NP, t, :], tmp[0:NP, t % 2, :], ACT.Relu,
                                             scale=dis[0:NP, t:t + 1]).then_inc(y_ready, 1)

                for s, (c0, w) in enumerate(SPLITS):
                    for f in range(FT):
                        if f % 2 == 0:
                            z_copy(n, f, c0, w)
                        n += 1
                    if l < LAYERS - 1 and s >= 1:
                        relu_tiles(range(4 * (s - 1), 4 * s))
                if l < LAYERS - 1:
                    relu_tiles(range(8, NT))
            sqrt_of_var(1)

            def h1_copy(c):
                net, r = c // NRC, c % NRC
                act.wait_ge(f1_ready, 2 * c + 1)
                if net:
                    act.wait_ge(f2_ready, 2 * (r + 1))
                nc.scalar.activation(h1t[:, 0, r * RC:(r + 1) * RC], PS[0:GH, 2 * (c % 2), 0:RC], ACT.Relu
                                     ).then_inc(h1_act, 1)

            def h2_copy(c):
                net, r = c // NRC, c % NRC
                act.wait_ge(f2_ready, 2 * c + 1)
                if net:
                    act.wait_ge(f3_ready, r + 1)
                nc.scalar.activation(h2t[:, 0, r * RC:(r + 1) * RC], PS[0:GH, 4, 0:RC], ACT.Relu,
                                     bias=b2f[:, net, 0:1]).then_inc(h2_act, 1)

            h1_copy(0)
            for c in range(2 * NRC):
                if c + 1 < 2 * NRC:
                    h1_copy(c + 1)
                h2_copy(c)
            sqrt_of_var(2)

            def xt_copy(k):
                for s, (c0, w) in enumerate(SPLITS):
                    for f in range(FT):
                        if f % 2 == 0:
                            act.wait_ge(xtp_ready, k * 12 + s * FT + f + 1)
                            nc.scalar.copy(xt[:, f, c0:c0 + w], PS[:, (s * FT + f) % 2, 0:w]).then_inc(xt_act, 1)

            xt_copy(0)
            for n in range(FT * len(SPLITS)):
                f, s = n // len(SPLITS), n % len(SPLITS)
                c0, w = SPLITS[s]
                act.wait_ge(hp_ready, n + 1)
                nc.scalar.activation(ht[:, f, c0:c0 + w], PS[:, 6 + n % 2, 0:w], ACT.Identity,
                                     bias=sage[:, 0, f:f + 1]).then_inc(h_ready, 1)
            act.wait_ge(hstat, 1)
            nc.scalar.activation(hs[:, 1, :], hs[:, 0, :], ACT.Sqrt).then_inc(hsd, 1)
            act.wait_ge(hscale, 1)
            for f in range(FT):
                nc.scalar.activation(ht[:, f, :], ht[:, f, :], ACT.Relu, scale=hs[:, 2, f:f + 1],
                                     bias=hs[:, 3, f:f + 1]).then_inc(hn_ready, 1)
            sqrt_of_var(3)
            xt_copy(1)
            act.wait_ge(zmax_ready, 1)
            nc.scalar.activation(pr[0:NP, :, :], q[0:NP, :, :], ACT.Exp).then_inc(exp_ready, 1)

            act.wait_ge(tables_ready, 1)

            def store(i, k, b):
                act.wait_ge(yo_ready, b + 1)
                act.dma_start(y_dram[bass.ds(b * BS, BS), :], yo[:, k, :]).then_inc(stored[k], 16)

            def turn_t(i, k, b):
                act.wait_ge(tt_ps, b + 1)
                nc.scalar.copy(tt[:, k, :, :], PS[:, 5, 0:INTER].rearrange("p (i n) -> p i n", i=3)
                               ).then_inc(tt_ready, 1)

            def result(i, k, b, first=False):
                act.wait_ge(y_done, b + 1)
                if not first:
                    act.wait_ge(stored[k], 16 * i)
                nc.scalar.activation(yo[:, k, :], PS[:, 6 + k, :], ACT.Copy,
                                     scale=wslot[:, bass.ds(b, 1)]).then_inc(yo_ready, 1)

            def sigmoid(i, k, b):
                e = act.value_load(eb_i[0:1, 0, bass.ds(b, 1)], min_val=0, max_val=NEXP)
                act.wait_ge(clip_g, b + 1)
                if not (isinstance(b, int) and b < 2):
                    act.wait_ge(t_ready, b - 1)
                nc.scalar.activation(ss[k], gg[k], ACT.Sigmoid, scale=acts[:, bass.ds(e, 1), 0]).then_inc(gate_sig, 1)

            sigmoid(0, 0, 0)
            turn_t(0, 0, 0)
            sigmoid(0, 1, 1)
            result(0, 0, 0, first=True)
            with act.Fori(1, NB // 2) as i:
                store(i, 0, i * 2 - 2)
                turn_t(i, 1, i * 2 - 1)
                sigmoid(i, 0, i * 2)
                result(i - 1, 1, i * 2 - 1)
                store(i, 1, i * 2 - 1)
                turn_t(i, 0, i * 2)
                sigmoid(i, 1, i * 2 + 1)
                result(i, 0, i * 2)
            store(0, 0, NB - 2)
            turn_t(0, 1, NB - 1)
            result(NB // 2 - 1, 1, NB - 1)
            store(0, 1, NB - 1)

        @block.tensor
        def _(pe):
            pe.wait_ge(const_done, CONSTS)
            pe.wait_ge(base_ready, 1)
            nc.tensor.matmul(PS[:, 7, 0:NG], ones[0:1, :], dstf[0:1, 0:NCH:CPG],
                             start=True, stop=True).then_inc(base_read, 1)
            pe.wait_ge(bad_ready, 1)
            nc.tensor.matmul(PS[:, 6, 0:1], ones[0:NP, :], bad[0:NP, 0:1], start=True, stop=True).then_inc(bad_sum, 1)

            def group(k, eng_lo, eng_key):
                for j in range(CPG):
                    mm = nc.tensor.matmul(PS[0:NP, k, 0:KEYS], eng_lo[0:CHUNK, k, j, 0:NP], eng_key[0:CHUNK, j, :],
                                          start=(j == 0), stop=(j == CPG - 1))
                return mm

            for k in range(2):
                pe.wait_ge(onehot_act, k + 1)
                pe.wait_ge(onehot_ready, k + 1)
                group(k, oh_lo, ohk[k]).then_inc(group_done, 1)
            with pe.Fori(1, NG // 2) as i:
                for k in range(2):
                    pe.wait_ge(onehot_act, i * 2 + k + 1)
                    pe.wait_ge(onehot_ready, i * 2 + k + 1)
                    pe.wait_ge(counted, i * 2 + k - 1)
                    group(k, oh_lo, ohk[k]).then_inc(group_done, 1)

            pe.wait_ge(flag_ready, 1)
            slow = pe.value_load(flag_i[0:1, 0:1], min_val=0, max_val=1)
            with pe.If(slow > 0):
                with pe.Fori(0, PASSES) as w:
                    with pe.Fori(0, NG) as g:
                        pe.wait_ge(slow_onehot, w * NG + g + 1)
                        group(0, oh_lo, ohk[0]).then_inc(slow_group, 1)

            pe.wait_ge(counts_ready, 1)
            for s, (c0, w) in enumerate(SPLITS):
                for t in range(NT):
                    mm = nc.tensor.matmul(PS[:, s, 0:w], ones[0:NP, :], CT[0:NP, t, c0:c0 + w],
                                          start=(t == 0), stop=(t == NT - 1))
                mm.then_inc(deg_ready, 1)
            pe.wait_ge(deg_copied, 1)
            for t in range(NT):
                mm = nc.tensor.matmul(PS[0:NP, 3, t:t + 1], invc[0:1, t * NP:(t + 1) * NP], ones[0:1, 0:1],
                                      start=True, stop=True)
            mm.then_inc(degcol_ready, 1)

            pe.wait_ge(load["wg"], 16 * LAYERS)
            n_agg = 0
            n_lin = 0

            def aggregate(n, source, f, c0, w):
                if n >= 6:
                    pe.wait_ge(z_act, (n - 6) // 2 + 1) if (n - 6) % 2 == 0 else pe.wait_ge(z_dve, (n - 6) // 2 + 1)
                for t in range(NT):
                    mm = nc.tensor.matmul(PS[:, n % 6, 0:w], source[0:NP, t, f * 128:(f + 1) * 128],
                                          CT[0:NP, t, c0:c0 + w], start=(t == 0), stop=(t == NT - 1))
                return mm

            pe.wait_ge(sd_ready, 2)
            for l in range(LAYERS):
                source = XN if l == 1 else Y

                def linear(tiles, n_z):
                    pe.wait_ge(z_act, n_z // 2)
                    pe.wait_ge(z_dve, n_z // 2)
                    for t in tiles:
                        n = l * NT + t
                        if n >= 2 + NT * (LAYERS - 1):
                            pe.wait_ge(lin_read, n - 1 - NT * (LAYERS - 1))
                        elif n >= 2:
                            pe.wait_ge(pre_ready, n - 1)
                        for f in range(FT):
                            mm = nc.tensor.matmul(PS[0:NP, 6 + n % 2, :], zt[:, f, t * NP:(t + 1) * NP], WG[:, l, f, :],
                                                  start=(f == 0), stop=(f == FT - 1))
                        mm.then_inc(lin_ready, 1)

                pe.wait_ge(y_ready, NT * (l + 1))
                for s, (c0, w) in enumerate(SPLITS):
                    for f in range(FT):
                        aggregate(n_agg, source, f, c0, w).then_inc(agg_ready, 1)
                        n_agg += 1
                    if s >= 1:
                        linear(range(4 * (s - 1), 4 * s), n_agg - FT)
                linear(range(8, NT), n_agg)

            pe.wait_ge(feat_ready, 1)
            pe.wait_ge(load["ffn"], 16 * 14)
            for pos in range(POS):
                for t in range(NT):
                    i = pos * NT + t
                    mm = nc.tensor.transpose(PS[0:FK, i // 4, (i % 4) * NP:(i % 4 + 1) * NP], feats[0:NP, pos, t, :],
                                             ident[0:NP, 0:NP])
            mm.then_inc(feat_t, 1)
            pe.wait_ge(ft_ready, 1)
            def first(c):
                net, r = c // NRC, c % NRC
                for m in range(2):
                    if c >= 2:
                        pe.wait_ge(h1_act if m == 0 else h1_dve, c - 1)
                    nc.tensor.matmul(PS[0:GH, 2 * (c % 2) + m, 0:RC], w1f[:, net, m * GH:(m + 1) * GH],
                                     ft[:, r * RC:(r + 1) * RC], start=True, stop=True).then_inc(f1_ready, 1)

            def second(c):
                net, r = c // NRC, c % NRC
                pe.wait_ge(h1_act, c + 1)
                pe.wait_ge(h1_dve, c + 1)
                for m in range(2):
                    if c >= 1:
                        pe.wait_ge(h2_act if m == 0 else h2_dve, c)
                    for k in range(2):
                        mm = nc.tensor.matmul(PS[0:GH, 4 + m, 0:RC], w2f[:, net, k, m * GH:(m + 1) * GH],
                                              h1t[:, k, r * RC:(r + 1) * RC], start=(k == 0), stop=(k == 1))
                    mm.then_inc(f2_ready, 1)

            def third(c):
                net, r = c // NRC, c % NRC
                pe.wait_ge(h2_act, c + 1)
                pe.wait_ge(h2_dve, c + 1)
                for t in range(4 * r, 4 * r + 4):
                    col = (net * POS * NT + t) * 2
                    for k in range(2):
                        mm = nc.tensor.matmul(PS[0:NP, 6, col:col + 2], h2t[:, k, t * NP:(t + 1) * NP],
                                              w3f[:, net, k, :], start=(k == 0), stop=(k == 1))
                mm.then_inc(f3_ready, 1)

            for c in range(2 * NRC + 2):
                if c < 2 * NRC:
                    first(c)
                if 1 <= c <= 2 * NRC:
                    second(c - 1)
                if c >= 2:
                    third(c - 2)

            def turn_x(k):
                for s, (c0, w) in enumerate(SPLITS):
                    for f in range(FT):
                        n = k * 12 + s * FT + f
                        if n >= 2:
                            pe.wait_ge(xt_act if n % 2 == 0 else xt_dve, n // 2)
                        for j in range(w // NP):
                            t = c0 // NP + j
                            mm = nc.tensor.transpose(PS[:, n % 2, j * NP:(j + 1) * NP],
                                                     XN[0:NP, t, f * 128:(f + 1) * 128], ident[0:NP, 0:NP])
                        mm.then_inc(xtp_ready, 1)

            pe.wait_ge(xn_ready, 3 * NT)
            turn_x(0)
            pe.wait_ge(minus_ready, 1)
            for s, (c0, w) in enumerate(SPLITS):
                for f in range(FT):
                    n = s * FT + f
                    if n >= 4:
                        pe.wait_ge(mean_ready, n - 3)
                    for t in range(NT):
                        mm = nc.tensor.matmul(PS[:, 2 + n % 4, 0:w], XN[0:NP, t, f * 128:(f + 1) * 128],
                                              CT[0:NP, t, c0:c0 + w], start=(t == 0), stop=(t == NT - 1))
                    mm.then_inc(mean_ps, 1)
            pe.wait_ge(mean_ready, FT * len(SPLITS))
            pe.wait_ge(xt_act, 6)
            pe.wait_ge(xt_dve, 6)
            pe.wait_ge(load["wlr"], 32)
            for n in range(FT * len(SPLITS)):
                fo, (c0, w) = n // len(SPLITS), SPLITS[n % len(SPLITS)]
                if n >= 2:
                    pe.wait_ge(h_ready, n - 1)
                for side, rhs in enumerate((zt, xt)):
                    for f in range(FT):
                        mm = nc.tensor.matmul(PS[:, 6 + n % 2, 0:w], WG[:, side, f, fo * 128:(fo + 1) * 128],
                                              rhs[:, f, c0:c0 + w], start=(side == 0 and f == 0),
                                              stop=(side == 1 and f == FT - 1))
                mm.then_inc(hp_ready, 1)
            pe.wait_ge(hn_ready, FT)
            for t in range(NT):
                if t >= 2:
                    pe.wait_ge(back_read, t - 1)
                for f in range(FT):
                    mm = nc.tensor.transpose(PS[0:NP, 2 + t % 2, f * 128:(f + 1) * 128], ht[:, f, t * NP:(t + 1) * NP],
                                             ident[:, :])
                mm.then_inc(back_ready, 1)

            pe.wait_ge(xn_ready, 4 * NT)
            turn_x(1)
            pe.wait_ge(xt_act, 12)
            pe.wait_ge(xt_dve, 12)
            pe.wait_ge(load["gate"], 32)
            for t in range(NT):
                for f in range(FT):
                    nc.tensor.matmul(PS[0:NP, 2, t * NEXP:(t + 1) * NEXP], xt[:, f, t * NP:(t + 1) * NP], gw[:, f, :],
                                     start=(f == 0), stop=False)
                mm = nc.tensor.matmul(PS[0:NP, 2, t * NEXP:(t + 1) * NEXP], ones[0:1, 0:NP], gb[0:1, :],
                                      start=False, stop=True)
            mm.then_inc(logit_ready, 1)
            pe.wait_ge(sel_ready, 1)
            pe.wait_ge(const_done, CONSTS + 9)
            nc.tensor.matmul(PS[0:NP, 3, 0:NT * NEXP], below[0:NP, 0:NP], q[0:NP, :, :].rearrange("p t e -> p (t e)"),
                             start=True, stop=False)
            nc.tensor.matmul(PS[0:NP, 3, 0:NT * NEXP], ones[0:NP, 0:NP],
                             cum[0:NP, 0:NT, :].rearrange("p t e -> p (t e)"), start=False, stop=True)
            nc.tensor.matmul(PS[:, 4, 0:NEXP], ones[0:NP, :], cum[0:NP, NT, :], start=True, stop=True
                             ).then_inc(rank_ready, 1)
            pe.wait_ge(slots_ready, 1)
            for i in range(ASSIGN):
                mm = nc.tensor.matmul(PS[:, 0, 0:2 * NBE], ohr[0:NP, i, :], ohb[0:NP, i, :, :].rearrange("p a b -> p (a b)"),
                                      start=(i == 0), stop=(i == ASSIGN - 1))
            mm.then_inc(table_ps, 1)

            pe.wait_ge(tables_ready, 1)

            def turn_rows(i, k, b):
                pe.wait_ge(gathered[k], 16 * (i + 1))
                for f in range(FT):
                    mm = nc.tensor.transpose(PS[:, 4, f * 128:(f + 1) * 128], xg[:, k, f * 128:(f + 1) * 128], ident[:, :])
                mm.then_inc(xt_ps, 1)

            def up(i, k, b):
                off = pe.value_load(eb_i[0:1, 1, bass.ds(b, 1)], min_val=0, max_val=(NWB - 1) * WBUF)
                pe.wait_ge(w1_in[k], 32 * (i + 1))
                pe.wait_ge(xgt_ready, b + 1)
                if not (isinstance(b, int) and b < 2):
                    pe.wait_ge(clip_done, b - 1)
                for h in range(2):
                    nc.tensor.matmul(PS[:, 2 * k + h, 0:INTER], ones[0:1, :],
                                     WB[0:1, bass.ds(off + (O_B1 + h * INTER), INTER)], start=True, stop=False)
                    for f in range(FT):
                        mm = nc.tensor.matmul(PS[:, 2 * k + h, 0:INTER], xgt[:, k, f, :],
                                              WB[:, bass.ds(off + (f * H2 + h * INTER), INTER)],
                                              start=False, stop=(f == FT - 1))
                mm.then_inc(hb_ready, 1)

            def turn_act(i, k, b):
                pe.wait_ge(t_ready, b + 1)
                for j in range(3):
                    mm = nc.tensor.transpose(PS[:, 5, j * 128:(j + 1) * 128], tb[:, k, j * 128:(j + 1) * 128], ident[:, :])
                mm.then_inc(tt_ps, 1)

            def down(i, k, b):
                off = pe.value_load(eb_i[0:1, 1, bass.ds(b, 1)], min_val=0, max_val=(NWB - 1) * WBUF)
                pe.wait_ge(w2_in[k], 32 * (i + 1))
                pe.wait_ge(tt_ready, b + 1)
                if not (isinstance(b, int) and b < 2):
                    pe.wait_ge(yo_ready, b - 1)
                nc.tensor.matmul(PS[:, 6 + k, :], ones[0:1, :], WB[0:1, bass.ds(off + O_B2, D)], start=True, stop=False)
                for j in range(3):
                    mm = nc.tensor.matmul(PS[:, 6 + k, :], tt[:, k, j, :], WB[:, bass.ds(off + (O_W2 + j * D), D)],
                                          start=False, stop=(j == 2))
                mm.then_inc(y_done, 1)

            turn_rows(0, 0, 0)
            up(0, 0, 0)
            pe.wait_ge(xgt_ready, 1)
            turn_rows(0, 1, 1)
            up(0, 1, 1)
            turn_act(0, 0, 0)
            turn_rows(1, 0, 2)
            down(0, 0, 0)
            with pe.Fori(1, NB // 2) as i:
                up(i, 0, i * 2)
                turn_act(i - 1, 1, i * 2 - 1)
                turn_rows(i, 1, i * 2 + 1)
                down(i - 1, 1, i * 2 - 1)
                up(i, 1, i * 2 + 1)
                turn_act(i, 0, i * 2)
                with pe.If(i < NB // 2 - 1):
                    turn_rows(i + 1, 0, i * 2 + 2)
                down(i, 0, i * 2)
            turn_act(NB // 2 - 1, 1, NB - 1)
            down(NB // 2 - 1, 1, NB - 1)

        @block.vector
        def _(dve):
            v = nc.vector
            link = counting(dve, step)

            dve.wait_ge(load["acts"], 16)
            link(v.tensor_scalar(clampv[:, 0, :, :], acts[:, :, 3:5], -1.0, None, ALU.mult))
            v.tensor_tensor(clampv[:, 1, :, :], clampv[:, 0, :, :], acts[:, :, 3:5], ALU.min).then_inc(sp_ready, 1)
            dve.wait_ge(sp_exp, 1)
            v.tensor_scalar(clampv[:, 3, :, :], clampv[:, 2, :, :], 1.0, None, ALU.add).then_inc(sp_one, 1)
            dve.wait_ge(sp_ln, 1)
            link(v.tensor_scalar(clampv[:, 2, :, :], acts[:, :, 3:5], 0.0, None, ALU.max))
            link(v.tensor_tensor(clampv[:, 0, :, :], clampv[:, 2, :, :], clampv[:, 4, :, :], ALU.add))
            link(v.tensor_scalar(clampv[:, 1, :, :], clampv[:, 0, :, :], -1.0, None, ALU.mult))

            def layer_norm(k):
                for t in range(NT):
                    ins = v.bn_stats(stats[0:NP, t, :], X[0:NP, t, :])
                link(ins)
                for t in range(NT):
                    ins = v.bn_aggr(mv[0:NP, t, :], stats[0:NP, t, :])
                link(ins)
                v.tensor_scalar(mv[0:NP, :, 1], mv[0:NP, :, 1], EPS, None, ALU.add).then_inc(var_ready, 1)
                dve.wait_ge(sd_ready, k + 1 if k == 0 else k + 2)
                link(v.reciprocal(rstd[0:NP, :], sd[0:NP, :]))
                for t in range(NT):
                    v.tensor_scalar(XN[0:NP, t, :], X[0:NP, t, :], mv[0:NP, t, 0:1], rstd[0:NP, t:t + 1],
                                    ALU.subtract, ALU.mult).then_inc(xn_ready, 1)
                dve.wait_ge(xn_ready, (k + 1) * NT)

            dve.wait_ge(load["edges"], 32)
            v.tensor_copy(dstf[0:CHUNK, :], dst_i[0:CHUNK, :]).then_inc(base_ready, 1)
            link(v.tensor_copy(srcf[0:CHUNK, :], src_i[0:CHUNK, :]))
            link(v.tensor_scalar(hi[0:CHUNK, :], srcf[0:CHUNK, :], -62.0, 1.0 / NP, ALU.add, ALU.mult))
            link(v.tensor_scalar(rel[0:CHUNK, :], hi[0:CHUNK, :], MAGIC, None, ALU.add))
            link(v.tensor_scalar(hi[0:CHUNK, :], rel[0:CHUNK, :], -MAGIC, None, ALU.add))
            link(v.scalar_tensor_tensor(out=lo[0:CHUNK, :], in0=hi[0:CHUNK, :], scalar=-float(NP),
                                        in1=srcf[0:CHUNK, :], op0=ALU.mult, op1=ALU.add))
            v.tensor_scalar(neglo[0:CHUNK, :], lo[0:CHUNK, :], -1.0, None, ALU.mult).then_inc(lo_ready, 1)
            dve.wait_ge(base_read, 1)
            v.tensor_copy(wbase_i[0:1, :], PS[0:1, 7, 0:NG]).then_inc(windows_ready, 1)
            link(v.tensor_copy(wbase[:, :], PS[:, 7, 0:NG]))
            three = lambda m: m[0:CHUNK, :].rearrange("p (g j) -> p g j", j=CPG)

            def make_keys(link_to):
                link_to(v.tensor_tensor(three(rel), three(dstf),
                                        wbase[0:CHUNK, :].rearrange("p (g o) -> p g o", o=1).to_broadcast([CHUNK, NG, CPG]),
                                        ALU.subtract))
                link_to(v.tensor_scalar(srcf[0:CHUNK, :], rel[0:CHUNK, :], 0.0, None, ALU.is_ge))
                link_to(v.scalar_tensor_tensor(out=srcf[0:CHUNK, :], in0=rel[0:CHUNK, :], scalar=float(WIN),
                                               in1=srcf[0:CHUNK, :], op0=ALU.is_lt, op1=ALU.mult))
                link_to(v.scalar_tensor_tensor(out=rel[0:CHUNK, :], in0=hi[0:CHUNK, :], scalar=float(WIN),
                                               in1=rel[0:CHUNK, :], op0=ALU.mult, op1=ALU.add))
                link_to(v.scalar_tensor_tensor(out=key[0:CHUNK, :], in0=rel[0:CHUNK, :], scalar=1.0,
                                               in1=srcf[0:CHUNK, :], op0=ALU.add, op1=ALU.mult))
                link_to(v.tensor_scalar(key[0:CHUNK, :], key[0:CHUNK, :], -1.0, None, ALU.add))

            make_keys(link)
            link(v.tensor_reduce(bad[0:CHUNK, 1:2], srcf[0:CHUNK, :], AX.X, ALU.min))
            v.tensor_scalar(bad[0:CHUNK, 0:1], bad[0:CHUNK, 1:2], -1.0, 1.0, ALU.mult, ALU.add).then_inc(bad_ready, 1)
            dve.wait_ge(bad_sum, 1)
            link(v.tensor_scalar(bad[:, 2:3], PS[:, 6, 0:1], 0.5, None, ALU.is_ge))
            v.tensor_copy(flag_i[0:1, 0:1], bad[0:1, 2:3]).then_inc(flag_ready, 1)

            dve.wait_ge(const_done, 4)

            def onehots(k, c, first=0):
                for j in range(CPG):
                    if j >= first:
                        v.tensor_scalar(oh_lo[0:CHUNK, k, j, 0:NP], iota_k[0:CHUNK, 0:NP], lo[0:CHUNK, bass.ds(c + j, 1)],
                                        None, ALU.is_equal)
                    ins = v.tensor_scalar(ohk[k][0:CHUNK, j, :], iota_k[0:CHUNK, :], key[0:CHUNK, bass.ds(c + j, 1)],
                                          None, ALU.is_equal)
                return ins

            for k in range(2):
                onehots(k, k * CPG, ACTJ).then_inc(onehot_ready, 1)
            with dve.Fori(1, NG // 2) as i:
                for k in range(2):
                    dve.wait_ge(group_done, i * 2 + k - 1)
                    onehots(k, (i * 2 + k) * CPG, ACTJ).then_inc(onehot_ready, 1)

            dve.wait_ge(load["x"], 16)
            layer_norm(0)
            dve.wait_ge(added, NG)

            slow = dve.value_load(flag_i[0:1, 0:1], min_val=0, max_val=1)
            with dve.If(slow > 0):
                SLOW0, SLOWK = 2, 7
                v.memset(CT[0:NP, :, :], 0.0).then_inc(slow_step, 1)
                v.memset(wbase[:, :], 0.0).then_inc(slow_step, 1)
                dve.wait_ge(slow_step, SLOW0)
                with dve.Fori(0, PASSES) as w:
                    done = [0]

                    def slow_link(ins):
                        done[0] += 1
                        at = dve.to_reg(w * (SLOWK + NG) + (SLOW0 + done[0]))
                        ins.then_inc(slow_step, 1)
                        dve.wait_ge(flag_ready, 1)
                        dve.wait_ge(slow_step, at)

                    make_keys(slow_link)
                    slow_link(v.tensor_scalar(wbase[:, :], wbase[:, :], float(WIN), None, ALU.add))
                    with dve.Fori(0, NG) as g:
                        onehots(0, g * CPG).then_inc(slow_onehot, 1)
                        dve.wait_ge(slow_group, w * NG + g + 1)
                        dest = CT[0:NP, :, bass.ds(w * WIN, WIN)]
                        v.tensor_tensor(dest, PS[0:NP, 0, 0:KEYS].rearrange("p (t w) -> p t w", t=NT), dest, ALU.add
                                        ).then_inc(slow_step, 1)
                        dve.wait_ge(slow_step, w * (SLOWK + NG) + g + (SLOW0 + SLOWK + 1))

            for t in range(NT):
                dest = CT[0:NP, t, t * NP:(t + 1) * NP]
                ins = v.tensor_tensor(dest, dest, ident[0:NP, 0:NP], ALU.add)
            ins.then_inc(counts_ready, 1)

            for s, (c0, w) in enumerate(SPLITS):
                dve.wait_ge(deg_ready, s + 1)
                ins = v.tensor_copy(invc[:, c0:c0 + w], PS[:, s, 0:w])
            ins.then_inc(deg_copied, 1)
            dve.wait_ge(sd_ready, 2)
            link(v.reciprocal(dis[0:NP, :], dis[0:NP, :]))
            for t in range(NT):
                v.tensor_scalar(Y[0:NP, t, :], XN[0:NP, t, :], dis[0:NP, t:t + 1], None, ALU.mult).then_inc(y_ready, 1)
            dve.wait_ge(degcol_ready, 1)
            link(v.tensor_scalar(invc[:, :], invc[:, :], -1.0, 1.0, ALU.add, ALU.max))
            link(v.reciprocal(invc[:, :], invc[:, :]))
            dve.wait_ge(load["gb"], 16 * LAYERS)

            n = 0
            for l in range(LAYERS):
                def finish(tiles):
                    for t in tiles:
                        m = l * NT + t
                        dve.wait_ge(lin_ready, m + 1)
                        if l < LAYERS - 1 and m >= 2:
                            dve.wait_ge(y_ready, NT + m - 1)
                        if l == LAYERS - 1 and t < 2:
                            dve.wait_ge(y_ready, NT * LAYERS)
                        ins = v.scalar_tensor_tensor(out=tmp[0:NP, t % 2, :], in0=PS[0:NP, 6 + m % 2, :],
                                                     scalar=dis[0:NP, t:t + 1], in1=bias[0:NP, l, :],
                                                     op0=ALU.mult, op1=ALU.add)
                        if l < LAYERS - 1:
                            ins.then_inc(pre_ready, 1)
                        else:
                            ins.then_inc(lin_read, 1)
                            dve.wait_ge(lin_read, t + 1)
                            link(v.scalar_tensor_tensor(out=X[0:NP, t, :], in0=tmp[0:NP, t % 2, :], scalar=0.0,
                                                        in1=X[0:NP, t, :], op0=ALU.max, op1=ALU.add))

                for s, (c0, w) in enumerate(SPLITS):
                    for f in range(FT):
                        if f % 2 == 1:
                            dve.wait_ge(agg_ready, n + 1)
                            v.tensor_copy(zt[:, f, c0:c0 + w], PS[:, n % 6, 0:w]).then_inc(z_dve, 1)
                        n += 1
                    if s >= 1:
                        finish(range(4 * (s - 1), 4 * s))
                finish(range(8, NT))

            layer_norm(1)
            nib = XN[0:NP, :, 16:80].rearrange("p t (g j) -> p t g j", j=16)
            link(v.tensor_scalar(fk[0:NP, :, :, :], nib, 0.5, None, ALU.is_gt))
            wjb = wj[0:NP, :].rearrange("p (a j) -> p a j", a=1)
            link(v.tensor_tensor(fk[0:NP, :, :, :].rearrange("p t g j -> p (t g) j"),
                                 fk[0:NP, :, :, :].rearrange("p t g j -> p (t g) j"),
                                 wjb.to_broadcast([NP, NT * 4, 16]), ALU.mult))
            link(v.tensor_reduce(fm[0:NP, :, :], fk[0:NP, :, :, :], AX.X, ALU.max))
            link(v.tensor_scalar(fg[0:NP, :, :], fm[0:NP, :, :], -1.0, 16.0, ALU.mult, ALU.add))
            link(v.scalar_tensor_tensor(out=fg[0:NP, :, :], in0=fm[0:NP, :, :], scalar=0.0, in1=fg[0:NP, :, :],
                                        op0=ALU.is_gt, op1=ALU.mult))
            for pos in range(POS):
                v.tensor_copy(feats[0:NP, pos, :, 0], fg[0:NP, :, pos])
                v.tensor_copy(feats[0:NP, pos, :, 1], fg[0:NP, :, 2 + pos])
                ins = v.tensor_copy(feats[0:NP, pos, :, 2:4], XN[0:NP, :, 105:107])
            ins.then_inc(feat_ready, 1)
            for c in range(3):
                ins = v.tensor_scalar(msk[0:NP, c, :], XN[0:NP, :, c], 0.5, None, ALU.is_gt)
            link(ins)
            v.tensor_tensor(msk[0:NP, 3, :], msk[0:NP, 0, :], msk[0:NP, 1, :], ALU.mult)
            link(v.tensor_tensor(msk[0:NP, 4, :], msk[0:NP, 0, :], msk[0:NP, 2, :], ALU.mult))
            link(v.tensor_tensor(msk[0:NP, 7, :], msk[0:NP, 4, :], msk[0:NP, 1, :], ALU.mult))
            link(v.tensor_tensor(msk[0:NP, 5, :], msk[0:NP, 4, :], msk[0:NP, 7, :], ALU.subtract))
            link(v.tensor_tensor(msk[0:NP, 6, :], msk[0:NP, 3, :], msk[0:NP, 5, :], ALU.add))
            for c in range(NRC):
                w = min(4, POS * NT - 4 * c) * NP
                dve.wait_ge(feat_t, 1)
                ins = v.tensor_copy(ft[:, c * RC:c * RC + w], PS[0:FK, c, 0:w])
            ins.then_inc(ft_ready, 1)
            def h1_copy(c):
                net, r = c // NRC, c % NRC
                dve.wait_ge(f1_ready, 2 * c + 2)
                if net:
                    dve.wait_ge(f2_ready, 2 * (r + 1))
                v.tensor_scalar(h1t[:, 1, r * RC:(r + 1) * RC], PS[0:GH, 2 * (c % 2) + 1, 0:RC], 0.0, None, ALU.max
                                ).then_inc(h1_dve, 1)

            def h2_copy(c):
                net, r = c // NRC, c % NRC
                dve.wait_ge(f2_ready, 2 * c + 2)
                if net:
                    dve.wait_ge(f3_ready, r + 1)
                v.tensor_scalar(h2t[:, 1, r * RC:(r + 1) * RC], PS[0:GH, 5, 0:RC], b2f[:, net, 1:2], 0.0,
                                ALU.add, ALU.max).then_inc(h2_dve, 1)

            h1_copy(0)
            for c in range(2 * NRC):
                if c + 1 < 2 * NRC:
                    h1_copy(c + 1)
                h2_copy(c)
                v.tensor_tensor(X[0:NP, c, :], X[0:NP, c, :], XN[0:NP, c, :], ALU.add)
            dve.wait_ge(f3_ready, 2 * NRC)
            for net in range(2):
                o = net * POS * NT * 2
                link(v.tensor_tensor(yv[0:NP, net, :, :],
                                     PS[0:NP, 6, o:o + POS * NT * 2].rearrange("p (t c) -> p t c", c=2),
                                     b3f[0:NP, net, :].rearrange("p (a c) -> p a c", a=1).to_broadcast([NP, POS * NT, 2]),
                                     ALU.add))
                m = msk[0:NP, 3 if net == 0 else 5, :].rearrange("p (t o) -> p t o", o=1).to_broadcast([NP, NT, 2])
                for pos in range(POS):
                    view = yv[0:NP, net, pos * NT:(pos + 1) * NT, :]
                    ins = v.tensor_tensor(view, view, m, ALU.mult)
                link(ins)
            link(v.tensor_tensor(res[0:NP, :, :], yv[0:NP, 0, :, :], yv[0:NP, 1, :, :], ALU.add))
            link(v.tensor_scalar(msk[0:NP, 7, :], res[0:NP, NT:2 * NT, 1], 0.5, None, ALU.is_gt))
            link(v.tensor_tensor(msk[0:NP, 7, :], msk[0:NP, 7, :], msk[0:NP, 6, :], ALU.mult))
            link(v.tensor_scalar(res[0:NP, :, :], res[0:NP, :, :], 0.0, 15.0, ALU.max, ALU.min))
            link(v.tensor_scalar(res[0:NP, :, :], res[0:NP, :, :], MAGIC, None, ALU.add))
            link(v.tensor_scalar(res[0:NP, :, :], res[0:NP, :, :], -MAGIC, None, ALU.add))
            link(v.tensor_scalar(msk[0:NP, 6, :], msk[0:NP, 6, :], 2.0, None, ALU.mult))
            wide = lambda m: m.rearrange("p (t o) -> p t o", o=1).to_broadcast([NP, NT, 16])
            cjb = cj[0:NP, :].rearrange("p (a j) -> p a j", a=1).to_broadcast([NP, NT, 16])
            for pos in range(POS):
                link(v.tensor_tensor(oh2[0:NP, :, :], cjb,
                                     res[0:NP, pos * NT:(pos + 1) * NT, 0:1].to_broadcast([NP, NT, 16]), ALU.is_equal))
                link(v.tensor_tensor(oh2[0:NP, :, :], oh2[0:NP, :, :], wide(msk[0:NP, 6, :]), ALU.mult))
                view = X[0:NP, :, 128 + 16 * pos:144 + 16 * pos]
                link(v.tensor_tensor(view, view, oh2[0:NP, :, :], ALU.add))
            link(v.tensor_tensor(X[0:NP, :, 160], X[0:NP, :, 160], msk[0:NP, 7, :], ALU.add))

            for t in range(NT):
                dest = CT[0:NP, t, t * NP:(t + 1) * NP]
                ins = v.tensor_tensor(dest, dest, ident[0:NP, 0:NP], ALU.subtract)
            ins.then_inc(minus_ready, 1)
            layer_norm(2)

            def xt_copy(k):
                for s, (c0, w) in enumerate(SPLITS):
                    for f in range(FT):
                        if f % 2 == 1:
                            dve.wait_ge(xtp_ready, k * 12 + s * FT + f + 1)
                            v.tensor_copy(xt[:, f, c0:c0 + w], PS[:, (s * FT + f) % 2, 0:w]).then_inc(xt_dve, 1)

            xt_copy(0)
            for s, (c0, w) in enumerate(SPLITS):
                for f in range(FT):
                    n = s * FT + f
                    dve.wait_ge(mean_ps, n + 1)
                    v.tensor_tensor(zt[:, f, c0:c0 + w], PS[:, 2 + n % 4, 0:w], invc[:, c0:c0 + w], ALU.mult
                                    ).then_inc(mean_ready, 1)
            for n in range(FT * len(SPLITS)):
                f, s = n // len(SPLITS), n % len(SPLITS)
                c0, w = SPLITS[s]
                dve.wait_ge(h_ready, n + 1)
                ins = v.bn_stats(hst[:, f, s, :], ht[:, f, c0:c0 + w])
            link(ins)
            for f in range(FT):
                ins = v.bn_aggr(hmv[:, f, :], hst[:, f, :, :].rearrange("p s k -> p (s k)"))
            link(ins)
            v.tensor_scalar(hs[:, 0, :], hmv[:, :, 1], EPS, None, ALU.add).then_inc(hstat, 1)
            dve.wait_ge(hsd, 1)
            dve.wait_ge(load["sage"], 48)
            link(v.reciprocal(hs[:, 2, :], hs[:, 1, :]))
            link(v.tensor_tensor(hs[:, 2, :], hs[:, 2, :], sage[:, 1, :], ALU.mult))
            link(v.tensor_tensor(hs[:, 3, :], hmv[:, :, 0], hs[:, 2, :], ALU.mult))
            v.tensor_tensor(hs[:, 3, :], sage[:, 2, :], hs[:, 3, :], ALU.subtract).then_inc(hscale, 1)
            for t in range(NT):
                dve.wait_ge(back_ready, t + 1)
                v.tensor_tensor(tmp[0:NP, t % 2, :], PS[0:NP, 2 + t % 2, :], XN[0:NP, t, :], ALU.add
                                ).then_inc(back_read, 1)
                dve.wait_ge(back_read, t + 1)
                ins = v.tensor_tensor(X[0:NP, t, :], X[0:NP, t, :], tmp[0:NP, t % 2, :], ALU.add)
            link(ins)

            layer_norm(3)
            xt_copy(1)
            R = lambda m: m[0:NP, :, :]
            col = lambda c: rsmall[0:NP, c, :]
            over = lambda m: m.rearrange("p (t o) -> p t o", o=1).to_broadcast([NP, NT, NEXP])
            wjt = wj[0:NP, :].rearrange("p (a j) -> p a j", a=1).to_broadcast([NP, NT, NEXP])
            dve.wait_ge(logit_ready, 1)
            dve.wait_ge(const_done, CONSTS + 9)
            logits = PS[0:NP, 2, 0:NT * NEXP].rearrange("p (t e) -> p t e", t=NT)
            link(v.tensor_reduce(col(0), logits, AX.X, ALU.max))
            v.tensor_tensor(R(q), logits, over(col(0)), ALU.subtract).then_inc(zmax_ready, 1)
            dve.wait_ge(exp_ready, 1)
            link(v.tensor_reduce(col(1), R(pr), AX.X, ALU.add))
            link(v.reciprocal(col(1), col(1)))
            link(v.tensor_tensor(R(pr), R(pr), over(col(1)), ALU.mult))
            for k in range(TOPK):
                link(v.tensor_reduce(col(2 + k), R(pr), AX.X, ALU.max))
                link(v.tensor_tensor(R(q), R(pr), over(col(2 + k)), ALU.is_equal))
                link(v.tensor_tensor(R(q), R(q), wjt, ALU.mult))
                link(v.tensor_reduce(col(4), R(q), AX.X, ALU.max))
                link(v.tensor_tensor(R(oh[k]), wjt, over(col(4)), ALU.is_equal))
                if k == 0:
                    link(v.scalar_tensor_tensor(out=R(pr), in0=R(oh[0]), scalar=-4.0, in1=R(pr),
                                                op0=ALU.mult, op1=ALU.add))
            link(v.tensor_tensor(col(5), col(2), col(3), ALU.add))
            link(v.reciprocal(col(5), col(5)))
            v.tensor_tensor(wsel[0:NP, 0, :], col(2), col(5), ALU.mult)
            v.tensor_tensor(wsel[0:NP, 1, :], col(3), col(5), ALU.mult)
            link(v.tensor_tensor(R(q), R(oh[0]), R(oh[1]), ALU.add))
            for t in range(NT):
                ins = v.tensor_tensor(cum[0:NP, t + 1, :], cum[0:NP, t, :], q[0:NP, t, :], ALU.add)
                if t < NT - 1:
                    link(ins)
            ins.then_inc(sel_ready, 1)
            dve.wait_ge(rank_ready, 1)
            BC = lambda c: blkc[:, c, :]
            link(v.tensor_copy(BC(0), PS[:, 4, 0:NEXP]))
            link(v.tensor_tensor(prod[:, :, 0:NT], BC(0).rearrange("p (e o) -> p e o", o=1).to_broadcast([128, NEXP, NT]),
                                 thr[:, :].rearrange("p (o k) -> p o k", o=1).to_broadcast([128, NEXP, NT]), ALU.is_gt))
            link(v.tensor_reduce(BC(1), prod[:, :, 0:NT], AX.X, ALU.add))
            link(v.tensor_tensor(prod[:, :, :], BC(1).rearrange("p (o e) -> p o e", o=1).to_broadcast([128, NEXP, NEXP]),
                                 le[:, :, :], ALU.mult))
            link(v.tensor_reduce(BC(2), prod[:, :, :], AX.X, ALU.add))
            link(v.tensor_tensor(BC(3), BC(2), BC(1), ALU.subtract))
            link(v.tensor_scalar(BC(3), BC(3), float(BS), None, ALU.mult))
            link(v.tensor_tensor(R(posn), PS[0:NP, 3, 0:NT * NEXP].rearrange("p (t e) -> p t e", t=NT),
                                 blkc[0:NP, 3, :].rearrange("p (o e) -> p o e", o=1).to_broadcast([NP, NT, NEXP]), ALU.add))
            for k in range(TOPK):
                link(v.tensor_tensor(R(pr), R(oh[k]), R(posn), ALU.mult))
                link(v.tensor_reduce(slotf[0:NP, k, :], R(pr), AX.X, ALU.add))
            link(v.tensor_copy(slot_i[0:NP, :, :], slotf[0:NP, :, :]))
            flat = slot_i[0:NP, :, :].rearrange("p k t -> p (k t)")
            v.tensor_scalar(slot_b[0:NP, 0, :], flat, 7, None, ALU.logical_shift_right)
            link(v.tensor_scalar(slot_b[0:NP, 1, :], flat, BS - 1, None, ALU.bitwise_and))
            link(v.tensor_copy(slotp[0:NP, 0:2, :], slot_b[0:NP, :, :]))
            A2 = [NP, ASSIGN, BS]
            v.tensor_tensor(ohr[0:NP, :, :], iota_b[0:NP, :].rearrange("p (o n) -> p o n", o=1).to_broadcast(A2),
                            slotp[0:NP, 1, :].rearrange("p (a o) -> p a o", o=1).to_broadcast(A2), ALU.is_equal)
            A3 = [NP, ASSIGN, NBE]
            link(v.tensor_tensor(ohb[0:NP, :, 1, :], iota_b[0:NP, 0:NBE].rearrange("p (o n) -> p o n", o=1).to_broadcast(A3),
                                 slotp[0:NP, 0, :].rearrange("p (a o) -> p a o", o=1).to_broadcast(A3), ALU.is_equal))
            for k in range(TOPK):
                rows = slice(k * NT, (k + 1) * NT)
                link(v.tensor_tensor(ohb[0:NP, rows, 0, :], ohb[0:NP, rows, 1, :],
                                     nodef[0:NP, :].rearrange("p (a o) -> p a o", o=1).to_broadcast([NP, NT, NBE]), ALU.mult))
            ins = v.tensor_tensor(ohb[0:NP, :, 1, :], ohb[0:NP, :, 1, :],
                                  wsel[0:NP, :, :].rearrange("p k (t o) -> p (k t) o", o=1).to_broadcast(A3), ALU.mult)
            ins.then_inc(slots_ready, 1)
            one = lambda c: ebf[0:1, c, :]
            link(v.tensor_tensor(cnt_e[0:1, :, :], cnt_e[0:1, :, :],
                                 blkc[0:1, 2, :].rearrange("p (o e) -> p o e", o=1).to_broadcast([1, NBE, NEXP]), ALU.is_ge))
            link(v.tensor_reduce(ebf[0:1, 0, 0:NBE], cnt_e[0:1, :, :], AX.X, ALU.add))
            link(v.tensor_scalar(ebf[0:1, 0, 0:NBE], ebf[0:1, 0, 0:NBE], float(NEXP - 1), None, ALU.min))
            link(v.memset(ebf[0:1, 0, NBE:NB], float(NEXP)))
            link(v.memset(ebf[0:1, 1, 0:1], 1.0))
            link(v.tensor_tensor(ebf[0:1, 1, 1:NB], ebf[0:1, 0, 1:NB], ebf[0:1, 0, 0:NB - 1], ALU.not_equal))
            link(v.tensor_tensor(prodb[0:1, :, :], prodb[0:1, :, :],
                                 one(1).rearrange("p (o b) -> p o b", o=1).to_broadcast([1, NB, NB]), ALU.mult))
            link(v.tensor_reduce(one(2), prodb[0:1, :, :], AX.X, ALU.add))
            link(v.tensor_scalar(one(3), one(2), -1.0, 1.0 / NWB, ALU.add, ALU.mult))
            link(v.tensor_scalar(one(3), one(3), MAGIC, None, ALU.add))
            link(v.tensor_scalar(one(3), one(3), -MAGIC, None, ALU.add))
            link(v.scalar_tensor_tensor(out=one(4), in0=one(3), scalar=-float(NWB), in1=one(2), op0=ALU.mult, op1=ALU.add))
            link(v.tensor_scalar(one(4), one(4), float(WBUF), None, ALU.mult))
            v.tensor_copy(eb_i[0:1, 0, :], one(0))
            v.tensor_copy(eb_i[0:1, 1, :], one(4))
            link(v.tensor_copy(eb_i[0:1, 2, :], one(1)))
            link(v.tensor_scalar(tok[:, NBE:NB], tok[:, NBE:NB], float(N - 1), None, ALU.min))
            dve.wait_ge(table_ps, 1)
            v.tensor_copy(tok[:, 0:NBE], PS[:, 0, 0:NBE])
            v.tensor_copy(wslot[:, 0:NBE], PS[:, 0, NBE:2 * NBE]).then_inc(tables_ready, 1)

            dve.wait_ge(tables_ready, 1)

            def rows_copy(i, k, b):
                dve.wait_ge(xt_ps, b + 1)
                v.tensor_copy(xgt[:, k, :, :], PS[:, 4, :].rearrange("p (f n) -> p f n", f=FT)).then_inc(xgt_ready, 1)

            def units(i, k, b, then=None):
                e = dve.value_load(eb_i[0:1, 0, bass.ds(b, 1)], min_val=0, max_val=NEXP)
                dve.wait_ge(hb_ready, b + 1)
                pair = lambda m: m.rearrange("p (h c) -> p h c", h=2)
                gate = PS[:, 2 * k:2 * k + 2, 0:INTER:2]
                upv = PS[:, 2 * k:2 * k + 2, 1:INTER:2]
                hi_g, lo_g = clampv[:, 0, bass.ds(e, 1), 0], clampv[:, 1, bass.ds(e, 1), 0]
                hi_u, lo_u = clampv[:, 0, bass.ds(e, 1), 1], clampv[:, 1, bass.ds(e, 1), 1]
                if not (isinstance(b, int) and b < 2):
                    dve.wait_ge(t_ready, b - 1)
                v.tensor_scalar(pair(gg[k]), gate, lo_g, hi_g, ALU.max, ALU.min).then_inc(clip_g, 1)
                v.tensor_scalar(pair(uu[k]), upv, lo_u, hi_u, ALU.max, ALU.min).then_inc(clip_done, 1)
                if then is not None:
                    then()
                dve.wait_ge(gate_sig, b + 1)
                v.scalar_tensor_tensor(out=ss[k], in0=gg[k], scalar=acts[:, bass.ds(e, 1), 1], in1=ss[k],
                                       op0=ALU.mult, op1=ALU.mult).then_inc(t_gs, 1)
                dve.wait_ge(t_gs, b + 1)
                if not (isinstance(b, int) and b < 2):
                    dve.wait_ge(tt_ps, b - 1)
                v.scalar_tensor_tensor(out=tb[:, k, :], in0=uu[k], scalar=acts[:, bass.ds(e, 1), 2], in1=ss[k],
                                       op0=ALU.add, op1=ALU.mult).then_inc(t_ready, 1)

            rows_copy(0, 0, 0)
            rows_copy(0, 1, 1)
            units(0, 0, 0)
            units(0, 1, 1, lambda: rows_copy(1, 0, 2))
            with dve.Fori(1, NB // 2) as i:
                units(i, 0, i * 2, lambda: rows_copy(i, 1, i * 2 + 1))
                more = i < NB // 2 - 1

                def next_rows():
                    with dve.If(more):
                        rows_copy(i + 1, 0, i * 2 + 2)
                units(i, 1, i * 2 + 1, next_rows)

            dve.wait_ge(z_in, 16)
            dve.wait_ge(back_in, 16 * 2 * NT)
            zrow = ZT[0:NP, :].rearrange("p (t d) -> p t d", t=NT)
            for t in range(NT):
                link(v.tensor_tensor(XN[0:NP, t, :], XN[0:NP, t, :], Y[0:NP, t, :], ALU.add))
                link(v.tensor_tensor(XN[0:NP, t, :], XN[0:NP, t, :], zrow[:, t, :], ALU.add))
                v.tensor_tensor(X[0:NP, t, :], X[0:NP, t, :], XN[0:NP, t, :], ALU.add).then_inc(sum_ready, 1)


def kernel(**inputs):
    import numpy as np
    import concourse.bacc as bacc
    from concourse.bass_utils import run_bass_kernel_spmd

    g = {k: np.asarray(v) for k, v in inputs.items()}
    edges = lambda e: e.reshape(NG * CPG, CHUNK).T
    arrays = {
        "x": g["x"], "src": edges(g["src"]), "dst": edges(g["dst"]),
        "W": g["L0_gnn_W"], "gnn_b": g["L0_gnn_b"],
        "WaT": g["L0_ffn_Wa"].transpose(0, 2, 1), "ba": g["L0_ffn_ba"],
        "WsT": g["L0_ffn_Ws"].transpose(0, 2, 1), "bs": g["L0_ffn_bs"],
        "WlT": g["L1_gnn_W_l"].T, "WrT": g["L1_gnn_W_r"].T, "b_l": g["L1_gnn_b_l"],
        "gamma": g["L1_gnn_gamma"], "beta": g["L1_gnn_beta"],
        "gate_w": g["L1_ffn_gate_w"], "gate_b": g["L1_ffn_gate_b"],
        "w1": np.concatenate([g["L1_ffn_expert_w1"], g["L1_ffn_shared_w1"][None]]),
        "b1": np.concatenate([g["L1_ffn_expert_b1"], g["L1_ffn_shared_b1"][None]]),
        "w2": np.concatenate([g["L1_ffn_expert_w2"], g["L1_ffn_shared_w2"][None]]),
        "b2": np.concatenate([g["L1_ffn_expert_b2"], g["L1_ffn_shared_b2"][None]]),
        "act": np.concatenate([g["L1_ffn_expert_act"], g["L1_ffn_shared_act"][None]]),
    }
    arrays = {k: np.ascontiguousarray(v) for k, v in arrays.items()}
    nc = bacc.Bacc("TRN2", target_bir_lowering=False, num_devices=1)
    aps = {k: nc.dram_tensor("in_" + k, v.shape, mybir.dt.from_np(v.dtype), kind="ExternalInput").ap()
           for k, v in arrays.items()}
    out = nc.dram_tensor("out", (N, D), F32, kind="ExternalOutput").ap()
    build(nc, aps, out)
    r = run_bass_kernel_spmd(nc, [{"in_" + k: v for k, v in arrays.items()}], core_ids=[0])
    return r.results[0]["out"]
```

```python
from contextlib import ExitStack

import concourse.bass as bass
from concourse import mybir

ALU = mybir.AluOpType
ACT = mybir.ActivationFunctionType
AX = mybir.AxisListType
F32 = mybir.dt.float32
F16 = mybir.dt.float16
F32R = mybir.dt.float32r
I32 = mybir.dt.int32

N = 1250
D = 512
E = 41250
NP = 125
NT = N // NP
FT = D // 128
LAYERS = 3
EPS = 1e-5
SPLITS = [(0, 500), (500, 500), (1000, 250)]

CHUNK = 125
CPG = 5
ACTJ = 1
NG = E // (CHUNK * CPG)
WIN = 24
KEYS = NT * WIN
CW = N + WIN
PASSES = (N + WIN - 1) // WIN

GE = 160
GH = GE // 2
FK = 5
POS = 2
ROWS = POS * N
RC = 500
NRC = ROWS // RC
EXACT = 4096
APART = EXACT // (CHUNK * CPG)
MAGIC = 12582912.0

NEXP = 16
TOPK = 2
INTER = 384
H2 = 2 * INTER
BS = 128
NB = 36
O_W2 = FT * H2
O_B1 = O_W2 + (INTER // 128) * D
WBUF = O_B1 + H2
EARLY = 6
NWB = 3
ASSIGN = TOPK * NT


def build(nc, a, out):
    ctx = ExitStack()
    with ctx:
        def sb(name, shape, dt=F32):
            return ctx.enter_context(nc.sbuf_tensor(name, shape, dt))

        def sem(name):
            return ctx.enter_context(nc.semaphore(name))

        PS = ctx.enter_context(nc.psum_tensor("PS", [128, 8, 512], F32))

        ROWB = NT * D * 4
        WB_BYTES = FT * D * 4
        CTB = (NT * CW * 4 + 31) // 32 * 32
        BASE = (nc.sbuf_base + 31) // 32 * 32
        nc.alloc_sbuf_tensor("arena", [128, (BASE - nc.sbuf_base + 6 * ROWB + CTB + 2 * WB_BYTES) // 4], F32)

        def at(name, offset, shape, dt=F32):
            return nc.alloc_sbuf_tensor_at(name, shape, dt, offset=BASE + offset)

        R_X, R_XN, R_YH, R_YL, R_ZH, R_ZL, R_CT = [k * ROWB for k in range(7)]
        R_WH = R_CT + CTB
        R_WL = R_WH + WB_BYTES

        X = at("X", R_X, [128, NT, D])
        XN = at("XN", R_XN, [128, NT, D])
        WNEXT = at("WNEXT", R_XN, [128, 2, FT, D])
        val = at("val", R_XN + 2 * WB_BYTES, [128, 2, D])
        CTR = at("CTR", R_CT, [128, NT, CW], F32R)
        CT = at("CT", R_CT, [128, NT, CW])
        YH = at("YH", R_YH, [128, NT, D], F32R)
        YL = at("YL", R_YL, [128, NT, D], F32R)
        ZH = at("ZH", R_ZH, [128, FT, N], F32R)
        ZL = at("ZL", R_ZL, [128, FT, N], F32R)
        WH = at("WH", R_WH, [128, FT, D], F32R)
        WL = at("WL", R_WL, [128, FT, D], F32R)
        WRAW = at("WRAW", R_WL, [128, FT, D])
        ht = at("HT", R_XN, [128, FT, N])
        h1t = at("H1T", R_ZH, [GH, 2, ROWS])
        h2t = at("H2T", R_YH, [GH, 2, ROWS])
        ft = at("FTT", R_ZL, [FK, ROWS])
        assert ROWS * 4 <= ROWB // 2 and FT * N * 4 <= ROWB
        FS = at("FS", R_ZL + ROWB // 2, [128, 2560])
        f32 = lambda m: m.bitcast(F32)
        ET = at("ET", R_YH, [128, 2 * NT * D])
        XT = at("XTF", R_ZH, [128, NT * D])
        xt = XT[:, 0:FT * N].rearrange("p (f n) -> p f n", f=FT)
        YF = at("YF", R_YH, [128, NT * D])
        RT = at("RT", R_YL, [128, NT * D])
        QX = at("QX", R_XN, [128, NT * D])
        WB = at("WB", R_ZL, [128, NWB * WBUF])
        R_SW = R_WL + WB_BYTES - WBUF * 4
        SW = at("SW", R_SW, [128, WBUF])
        assert R_ZL + NWB * WBUF * 4 <= R_SW and 2 * ROWB <= NWB * WBUF * 4
        GA, GB = [at(n, r, [128, NT, D]) for n, r in (("GA", R_ZL), ("GB", R_ZL + ROWB))]

        used = [0]

        def carve(width, dt=F32):
            w = width if dt is not F16 else (width + 1) // 2
            v = ET[:, used[0]:used[0] + w]
            used[0] += w
            assert used[0] <= 2 * NT * D
            return v if dt is F32 else v.bitcast(dt)

        NCH = NG * CPG
        src_i, dst_i = carve(NCH, I32), carve(NCH, I32)
        srcf, dstf, hi, lo, neglo, rel, key = [carve(NCH) for _ in range(7)]
        dist = carve(2 * ACTJ * 128, F16).rearrange("p (b j n) -> p b j n", b=2, j=ACTJ)
        oh_lo = carve(2 * CPG * 128, F16).rearrange("p (b j n) -> p b j n", b=2, j=CPG)
        ohk = [carve(CPG * KEYS, F16).rearrange("p (j n) -> p j n", j=CPG) for _ in range(2)]
        counts = carve(2 * KEYS).rearrange("p (b n) -> p b n", b=2)
        iota_k = carve(KEYS, F16)
        wbase = sb("wbase", [128, NG])
        wbase_i = sb("wbase_i", [1, NG], I32)
        bad = sb("bad", [128, 4])
        flag_i = sb("flag_i", [1, 1], I32)
        apart = carve(2 * NG).rearrange("p (a g) -> p a g", a=2)

        ident = sb("ident", [128, 128])
        ones = sb("ones", [128, 128])
        below = sb("below", [128, 128])
        stats = sb("stats", [128, NT, 6])
        mv = sb("mv", [128, NT, 2])
        sd = sb("sd", [128, NT])
        rstd = sb("rstd", [128, NT])
        dis = sb("dis", [128, NT])
        rdis = sb("rdis", [128, NT])
        invc = sb("invc", [128, N])
        bias = sb("bias", [128, LAYERS, D])
        tmp = sb("tmp", [128, 2, D])

        load = {}

        def loaded(name):
            load[name] = sem("in_" + name)
            return load[name]

        for name in ("sw", "b2", "x", "edges", "w0", "w12", "wl", "wr", "gb", "ffn", "sage", "gate", "acts"):
            loaded(name)
        const_done = sem("const_done")
        step = sem("dve_step")
        var_ready, sd_ready, xn_ready = sem("var_ready"), sem("sd_ready"), sem("xn_ready")
        base_ready, base_read = sem("base_ready"), sem("base_read")
        onehot_ready, group_done = sem("onehot_ready"), sem("group_done")
        lo_ready, dist_ready, onehot_act = sem("lo_ready"), sem("dist_ready"), sem("onehot_act")
        windows_ready, counted, added = sem("windows_ready"), sem("counted"), sem("added")
        bad_ready, bad_sum, flag_ready = sem("bad_ready"), sem("bad_sum"), sem("flag_ready")
        slow_onehot, slow_group = sem("slow_onehot"), sem("slow_group")
        slow_step = sem("slow_step")
        counts_ready = sem("counts_ready")
        deg_ready, deg_copied, degcol_ready = sem("deg_ready"), sem("deg_copied"), sem("degcol_ready")
        y_ready = sem("y_ready")
        agg_ready = sem("agg_ready")
        zh_ready, zl_ready = sem("zh_ready"), sem("zl_ready")
        val_ready, yh_ready = sem("val_ready"), sem("yh_ready")
        wh_ready, w_ready = sem("wh_ready"), sem("w_ready")
        xn_added = sem("xn_added")
        lin_ready = sem("lin_ready")
        lin_read = sem("lin_read")
        pre_ready = sem("pre_ready")
        feat_ready, feat_t, ft_ready = sem("feat_ready"), sem("feat_t"), sem("ft_ready")
        f1_ready, f2_ready = sem("f1_ready"), sem("f2_ready")
        h1_act, h1_dve, h2_act, h2_dve = sem("h1_act"), sem("h1_dve"), sem("h2_act"), sem("h2_dve")
        f3_ready = sem("f3_ready")
        xtp_ready, xt_act, xt_dve = sem("xtp_ready"), sem("xt_act"), sem("xt_dve")
        sxt_ps, sxt_hi, sxt_ready = sem("sxt_ps"), sem("sxt_hi"), sem("sxt_ready")
        minus_ready = sem("minus_ready")
        mean_ps, mean_f32 = sem("mean_ps"), sem("mean_f32")
        mean_hi, mean_ready = sem("mean_hi"), sem("mean_ready")
        hr_ps, hr_ready = sem("hr_ps"), sem("hr_ready")
        hp_ready, h_ready = sem("hp_ready"), sem("h_ready")
        hstat, hsd, hscale, hn_ready = sem("hstat"), sem("hsd"), sem("hscale"), sem("hn_ready")
        back_ready, back_read = sem("back_ready"), sem("back_read")
        xn_stored = sem("xn_stored")
        logit_ready, zmax_ready, exp_ready = sem("logit_ready"), sem("zmax_ready"), sem("exp_ready")
        sel_ready, rank_ready = sem("sel_ready"), sem("rank_ready")
        slots_ready, table_ps, tables_ready = sem("slots_ready"), sem("table_ps"), sem("tables_ready")
        sp_ready, sp_exp, sp_one, sp_ln = sem("sp_ready"), sem("sp_exp"), sem("sp_one"), sem("sp_ln")
        gathered = [sem("gathered0"), sem("gathered1")]
        w1_in = [sem("w1_in0"), sem("w1_in1")]
        w2_in = [sem("w2_in0"), sem("w2_in1")]
        xt_ps, xgt_ready = sem("xt_ps"), sem("xgt_ready")
        hb_ready, clip_done, clip_g, gate_sig, t_gs, t_ready = (
            sem("hb_ready"), sem("clip_done"), sem("clip_g"), sem("gate_sig"), sem("t_gs"), sem("t_ready"))
        clip_u = sem("clip_u")
        tt_ps, tt_ready, y_done, yo_ready = sem("tt_ps"), sem("tt_ready"), sem("y_done"), sem("yo_ready")
        stored = [sem("stored0"), sem("stored1")]
        zeroed = sem("zeroed")
        z_added = sem("z_added")
        cw_ps, cwt_ready = sem("cw_ps"), sem("cwt_ready")
        back_in = [sem(f"back_in{g}") for g in range(NT // 2)]
        sum_ready, out_stored = sem("sum_ready"), sem("out_stored")

        xn_dram = nc.dram_tensor("xn_dram", [N, D], F32, kind="Internal")
        y_dram = nc.dram_tensor("y_dram", [NB * BS, D], F32, kind="Internal")

        w1f = FS[0:FK, 1040:1360].rearrange("p (a n) -> p a n", a=2)
        w2f = FS[0:GH, 1360:2000].rearrange("p (a m n) -> p a m n", a=2, m=2)
        b2f = sb("b2f", [GH, 2, 2])
        w3f = sb("w3f", [GH, 2, 2, 2])
        b3f = sb("b3f", [128, 2, 2])
        wj = sb("wj", [128, NEXP])
        cj = sb("cj", [128, NEXP])
        fk = FS[:, 0:NT * 64].rearrange("p (t g j) -> p t g j", t=NT, g=4)
        fm = FS[:, 960:1000].rearrange("p (t g) -> p t g", g=4)
        fg = FS[:, 1000:1040].rearrange("p (t g) -> p t g", g=4)
        feats = sb("feats", [128, POS, NT, FK])
        msk = sb("msk", [128, 8, NT])
        yv = FS[:, 640:640 + 80].rearrange("p (a t c) -> p a t c", a=2, c=2)
        res = FS[:, 720:720 + 40].rearrange("p (t c) -> p t c", c=2)
        oh2 = FS[:, 800:800 + 160].rearrange("p (t j) -> p t j", j=16)
        sage = sb("sage", [128, 3, FT])
        hst = sb("hst", [128, FT, 3, 6])
        hmv = sb("hmv", [128, FT, 2])
        hs = sb("hs", [128, 4, FT])
        gw = sb("gw", [128, FT, NEXP])
        gb = sb("gb", [1, NEXP])
        acts = sb("acts", [128, NEXP + 1, 5])
        clampv = sb("clampv", [128, 5, NEXP + 1, 2])

        xg = YF[:, 0:2 * D].rearrange("p (b d) -> p b d", b=2)
        xgt = YF[:, 1024:1024 + 2 * D].rearrange("p (b f n) -> p b f n", b=2, f=FT)
        tt = YF[:, 2048:2048 + 2 * INTER].rearrange("p (b i n) -> p b i n", b=2, i=3)
        yo = YF[:, 2816:2816 + 2 * D].rearrange("p (b d) -> p b d", b=2)
        spare = bias[:, :, :].rearrange("p l n -> p (l n)")
        hb = [YF[:, 3840:3840 + H2], spare[:, 0:H2]]
        ss = [YF[:, 3840 + H2:3840 + H2 + INTER], spare[:, H2:H2 + INTER]]
        tb = RT[:, 0:2 * INTER].rearrange("p (b i) -> p b i", b=2)
        b2m = invc[0:NEXP + 1, 0:D]
        cw = invc[:, D:D + NT * (NEXP + 1)].rearrange("p (t e) -> p t e", t=NT)
        rat = [2 * INTER]

        def rcarve(*dims):
            n = 1
            for d in dims:
                n *= d
            v = RT[:, rat[0]:rat[0] + n]
            rat[0] += n
            assert rat[0] <= NT * D, rat[0]
            names = "abcd"[:len(dims)]
            return v if len(dims) == 1 else v.rearrange(
                f"p ({' '.join(names)}) -> p {' '.join(names)}", **{c: d for c, d in zip(names, dims)})

        pr = rcarve(NT, NEXP)
        q = rcarve(NT, NEXP)
        oh = [rcarve(NT, NEXP), rcarve(NT, NEXP)]
        cum = rcarve(NT + 1, NEXP)
        posn = rcarve(NT, NEXP)
        rsmall = rcarve(10, NT)
        blkc = rcarve(6, NEXP)
        thr = rcarve(NT)
        le = rcarve(NEXP, NEXP)
        prod = rcarve(NEXP, NEXP)
        slotf = rcarve(TOPK, NT)
        slotp = rcarve(3, TOPK * NT)
        wsel = rcarve(TOPK, NT)
        nodef = rcarve(NT)
        ohb = rcarve(ASSIGN, 2, NB)
        cnt_e = rcarve(NB, NEXP)
        iota_b = rcarve(BS)
        ohr = QX[:, 0:ASSIGN * BS].rearrange("p (a n) -> p a n", a=ASSIGN)
        prodb = QX[:, 2560:2560 + NB * NB].rearrange("p (a b) -> p a b", a=NB)
        cwt = QX[0:NEXP + 1, 3860:3860 + N]
        slot_i = sb("slot_i", [128, TOPK, NT], I32)
        slot_b = sb("slot_b", [128, 2, TOPK * NT], I32)
        idx = sb("idx", [128, 2], I32)
        idx_ready = sem("idx_ready")
        tok = sb("tok", [128, NB], I32)
        wslot = sb("wslot", [128, NB])
        ebf = rcarve(5, NB)
        eb_i = sb("eb_i", [1, 4, NB], I32)

        block = ctx.enter_context(nc.Block())

        def counting(eng, s):
            seen = [0]

            def link(ins):
                seen[0] += 1
                ins.then_inc(s, 1)
                eng.wait_ge(s, seen[0])
            link.seen = seen
            return link

        bank = lambda n: PS[:, n, :]
        CONSTS = 11
        SURE = TOPK * N // BS

        def last_pair(eng):
            return eng.value_load(eb_i[0:1, 3, 0:1], min_val=(SURE + 1) // 2 - 1, max_val=NB // 2 - 1)

        CWT_BANKS = ((6, 0), (7, 0), (4, 200))
        SF = [(s, f) for s in range(len(SPLITS)) for f in range(FT)]

        @block.sync
        def _(sp):
            sp.dma_start(src_i[0:CHUNK, :], a["src"]).then_inc(load["edges"], 16)
            sp.dma_start(dst_i[0:CHUNK, :], a["dst"]).then_inc(load["edges"], 16)
            sp.dma_start(X[0:NP, :, :], a["x"].rearrange("(t p) d -> p t d", p=NP)).then_inc(load["x"], 16)
            sp.dma_start(WRAW[:, :, :], a["W"][0].rearrange("(f p) n -> p f n", p=128)).then_inc(load["w0"], 16)
            for l in range(LAYERS):
                if l:
                    sp.dma_start(WNEXT[:, l - 1, :, :], a["W"][l].rearrange("(f p) n -> p f n", p=128)
                                 ).then_inc(load["w12"], 16)
                sp.dma_start(bias[:, l, :], a["gnn_b"][l:l + 1, :].to_broadcast([128, D])).then_inc(load["gb"], 16)
            with nc.allow_non_contiguous_dma(reason="small tables"):
                for k, name in enumerate(("b_l", "gamma", "beta")):
                    sp.dma_start(sage[:, k, :], a[name].rearrange("(f p) -> p f", p=128)).then_inc(load["sage"], 16)
            sp.dma_start(gw[:, :, :], a["gate_w"].rearrange("(f p) n -> p f n", p=128)).then_inc(load["gate"], 16)
            sp.dma_start(gb[0:1, :], a["gate_b"].rearrange("(o n) -> o n", o=1)).then_inc(load["gate"], 16)
            sp.dma_start(acts[:, :, :], a["act"].rearrange("(o e) k -> o e k", o=1).to_broadcast([128, NEXP + 1, 5])
                         ).then_inc(load["acts"], 16)
            sp.wait_ge(const_done, 5)
            sp.dma_start(y_dram[SURE * BS:NB * BS, :].rearrange("(b p) d -> p b d", p=BS),
                         XT[:, 0:D].rearrange("p (o d) -> p o d", o=1).to_broadcast([128, NB - SURE, D])
                         ).then_inc(zeroed, 16)
            sp.wait_ge(lin_ready, NT * LAYERS)
            for n, (w, b) in enumerate((("WaT", "ba"), ("WsT", "bs"))):
                sp.dma_start(w1f[0:2, n, :], a[w][0, 0:2, :]).then_inc(load["ffn"], 16)
                sp.dma_start(w1f[2:4, n, :], a[w][0, 35:37, :]).then_inc(load["ffn"], 16)
                sp.dma_start(w1f[4:5, n, :], a[b][0:1, :]).then_inc(load["ffn"], 16)
                sp.dma_start(w2f[:, n, :, :], a[w][1].rearrange("(m p) n -> p m n", p=GH)).then_inc(load["ffn"], 16)
                with nc.allow_non_contiguous_dma(reason="small tables"):
                    sp.dma_start(b2f[:, n, :], a[b][1, :].rearrange("(m p) -> p m", p=GH)).then_inc(load["ffn"], 16)
                    sp.dma_start(w3f[:, n, :, :], a[w][2, :, 100:102].rearrange("(m p) n -> p m n", p=GH)).then_inc(load["ffn"], 16)
                sp.dma_start(b3f[:, n, :], a[b][2:3, 100:102].to_broadcast([128, 2])).then_inc(load["ffn"], 16)
            sp.dma_start(WRAW[:, :, :], a["WrT"].rearrange("(f p) n -> p f n", p=128)).then_inc(load["wr"], 16)
            sp.wait_ge(hr_ps, FT * len(SPLITS))
            sp.dma_start(WRAW[:, :, :], a["WlT"].rearrange("(f p) n -> p f n", p=128)).then_inc(load["wl"], 16)
            sp.wait_ge(mean_ready, FT * len(SPLITS))
            sp.dma_start(b2m, a["b2"]).then_inc(load["b2"], 16)
            sp.wait_ge(hp_ready, FT * len(SPLITS))
            sp.dma_start(SW[:, 0:O_W2].rearrange("p (f n) -> p f n", f=FT),
                         a["w1"][NEXP].rearrange("(f p) n -> p f n", p=128)).then_inc(load["sw"], 16)
            sp.dma_start(SW[:, O_W2:O_B1].rearrange("p (f n) -> p f n", f=INTER // 128),
                         a["w2"][NEXP].rearrange("(f p) n -> p f n", p=128)).then_inc(load["sw"], 16)
            sp.dma_start(SW[:, O_B1:WBUF], a["b1"][NEXP:NEXP + 1, :].to_broadcast([128, H2])).then_inc(load["sw"], 16)
            sp.wait_ge(xn_ready, 3 * NT)
            sp.dma_start(xn_dram[:, :].rearrange("(t p) d -> p t d", p=NP), XN[0:NP, :, :]).then_inc(xn_stored, 16)

            sp.wait_ge(tables_ready, 1)

            def load_weights(i, k, b):
                e = sp.value_load(eb_i[0:1, 0, bass.ds(b, 1)], min_val=0, max_val=NEXP)
                off = sp.value_load(eb_i[0:1, 1, bass.ds(b, 1)], min_val=0, max_val=(NWB - 1) * WBUF)
                new = sp.value_load(eb_i[0:1, 2, bass.ds(b, 1)], min_val=0, max_val=1)
                if isinstance(b, int):
                    ahead, landed1, landed2 = b + EARLY - NWB + 1, 32 * i, 16 * i
                else:
                    ahead, landed1, landed2 = sp.to_reg(b + (EARLY - NWB + 1)), sp.to_reg(i * 32), sp.to_reg(i * 16)
                sp.wait_ge(tables_ready, 1)
                if not (isinstance(b, int) and b < 2):
                    sp.wait_ge(w1_in[k], landed1)
                    sp.wait_ge(w2_in[k], landed2)
                if not (isinstance(b, int) and b < NWB):
                    sp.wait_ge(y_done, ahead)
                w1v = a["w1"][bass.ds(e, 1), :, :].rearrange("o (f p) n -> p (o f) n", p=128)
                sp.dma_start(WB[:, bass.ds(off, FT * H2)].rearrange("p (f n) -> p f n", f=FT), w1v,
                             cond=new).then_inc(w1_in[k], 16)
                sp.dma_start(WB[:, bass.ds(off + O_B1, H2)], a["b1"][bass.ds(e, 1), :].to_broadcast([128, H2]),
                             cond=new).then_inc(w1_in[k], 16)
                w2v = a["w2"][bass.ds(e, 1), :, :].rearrange("o (f p) n -> p (o f) n", p=128)
                sp.dma_start(WB[:, bass.ds(off + O_W2, (INTER // 128) * D)].rearrange("p (f n) -> p f n", f=INTER // 128),
                             w2v, cond=new).then_inc(w2_in[k], 16)

            last = last_pair(sp)
            for b in range(4):
                load_weights(b // 2, b % 2, b)
            with sp.Fori(2, NB // 2) as i:
                with sp.If(i < last + 1):
                    for k in range(2):
                        load_weights(i, k, i * 2 + k)
            for t in range(NT):
                sp.wait_ge(sum_ready, t + 1)
                sp.dma_start(out[t * NP:(t + 1) * NP, :], X[0:NP, t, :]).then_inc(out_stored, 16)
            sp.wait_ge(out_stored, 16 * NT)

        @block.gpsimd
        def _(pool):
            pool.memset(ident[:, :], 0.0).then_inc(const_done, 1)
            pool.memset(ones[:, :], 1.0).then_inc(const_done, 1)
            pool.memset(below[:, :], 1.0).then_inc(const_done, 1)
            pool.iota(iota_k[:, :], pattern=[[1, KEYS]], base=0, channel_multiplier=0,
                      allow_small_or_imprecise_dtypes=True).then_inc(const_done, 1)
            pool.memset(XT[:, 0:D], 0.0).then_inc(const_done, 1)
            pool.iota(wj[:, :], pattern=[[-1, NEXP]], base=16, channel_multiplier=0,
                      allow_small_or_imprecise_dtypes=True).then_inc(const_done, 1)
            pool.iota(cj[:, :], pattern=[[1, NEXP]], base=0, channel_multiplier=0,
                      allow_small_or_imprecise_dtypes=True).then_inc(const_done, 1)
            pool.wait_ge(const_done, 7)
            pool.affine_select(out=ident[:, :], in_=ident[:, :], compare_op=ALU.not_equal, fill=1.0, base=0,
                               pattern=[[-1, 128]], channel_multiplier=1).then_inc(const_done, 1)
            pool.affine_select(out=below[:, :], in_=below[:, :], compare_op=ALU.is_gt, fill=0.0, base=0,
                               pattern=[[1, 128]], channel_multiplier=-1).then_inc(const_done, 1)
            pool.memset(feats[:, :, :, :], 1.0).then_inc(const_done, 1)
            pool.memset(f32(CTR[:, :, :]), 0.0).then_inc(const_done, 1)

            pool.wait_ge(windows_ready, 1)
            pool.wait_ge(const_done, CONSTS)

            def add_counts(k, g):
                w0 = pool.value_load(wbase_i[0:1, bass.ds(g, 1)], min_val=0, max_val=N - 1)
                pool.wait_ge(counted, g + 1)
                if not isinstance(g, int) or g:
                    pool.wait_ge(added, g)
                dest = CTR[0:NP, :, bass.ds(w0, WIN)]
                pool.tensor_tensor(dest, counts[0:NP, k, :].rearrange("p (t w) -> p t w", t=NT), f32(dest), ALU.add
                                   ).then_inc(added, 1)

            add_counts(0, 0)
            add_counts(1, 1)
            with pool.Fori(1, NG // 2) as i:
                for k in range(2):
                    add_counts(k, i * 2 + k)

            pool.wait_ge(hp_ready, FT * len(SPLITS))
            pool.iota(thr[:, :], pattern=[[BS, NT]], base=0, channel_multiplier=0,
                      allow_small_or_imprecise_dtypes=True).then_inc(const_done, 1)
            pool.memset(le[:, :, :], 1.0).then_inc(const_done, 1)
            pool.iota(nodef[:, :], pattern=[[NP, NT]], base=0, channel_multiplier=1,
                      allow_small_or_imprecise_dtypes=True).then_inc(const_done, 1)
            pool.memset(cum[:, 0, :], 0.0).then_inc(const_done, 1)
            pool.iota(cnt_e[:, :, :], pattern=[[1, NB], [0, NEXP]], base=0, channel_multiplier=0,
                      allow_small_or_imprecise_dtypes=True).then_inc(const_done, 1)
            pool.wait_ge(const_done, CONSTS + 5)
            pool.affine_select(out=le[:, :, :], in_=le[:, :, :], compare_op=ALU.is_ge, fill=0.0, base=0,
                               pattern=[[1, NEXP], [-1, NEXP]], channel_multiplier=0).then_inc(const_done, 1)
            pool.wait_ge(logit_ready, 1)
            pool.wait_ge(xn_stored, 16)
            pool.iota(iota_b, pattern=[[1, BS]], base=0, channel_multiplier=0,
                      allow_small_or_imprecise_dtypes=True).then_inc(const_done, 1)
            pool.memset(prodb[0:1, :, :], 1.0).then_inc(const_done, 1)
            pool.wait_ge(const_done, CONSTS + 8)
            pool.affine_select(out=prodb[0:1, :, :], in_=prodb[0:1, :, :], compare_op=ALU.is_ge, fill=0.0, base=0,
                               pattern=[[1, NB], [-1, NB]], channel_multiplier=0).then_inc(const_done, 1)

            pool.wait_ge(tables_ready, 1)

            def gather(i, k, b):
                if not (isinstance(b, int) and b < 2):
                    pool.wait_ge(xt_ps, b - 1)
                turn = b + 1 if isinstance(b, int) else pool.to_reg(b + 1)
                pool.tensor_copy(idx[:, k:k + 1], tok[:, bass.ds(b, 1)]).then_inc(idx_ready, 1)
                pool.wait_ge(xn_stored, 16)
                pool.wait_ge(idx_ready, turn)
                pool.indirect_dma_start(xg[:, k, :], None, xn_dram[:, :],
                                        bass.IndirectOffsetOnAxis(idx[:, k:k + 1], 0)
                                        ).then_inc(gathered[k], 16)

            for b in range(2):
                gather(0, b, b)
            last = last_pair(pool)
            with pool.Fori(1, NB // 2) as i:
                with pool.If(i < last + 1):
                    for k in range(2):
                        gather(i, k, i * 2 + k)
            all_stored = pool.to_reg(last * 16 + 16)
            pool.wait_ge(tables_ready, 1)
            pool.wait_ge(stored[0], all_stored)
            pool.wait_ge(stored[1], all_stored)
            for t in range(NT):
                for k, dest in enumerate((GA, GB)):
                    pool.indirect_dma_start(dest[0:NP, t, :], None, y_dram[:, :],
                                            bass.IndirectOffsetOnAxis(slot_i[0:NP, k, t:t + 1], 0)
                                            ).then_inc(back_in[t // 2], 16)
            for g in range(NT // 2):
                pool.wait_ge(back_in[g], 16 * 4)

        @block.scalar
        def _(act):
            def sqrt_of_var(k):
                act.wait_ge(var_ready, k + 1)
                nc.scalar.activation(sd[0:NP, :], mv[0:NP, :, 1], ACT.Sqrt).then_inc(sd_ready, 1)

            act.wait_ge(sp_ready, 1)
            nc.scalar.activation(clampv[:, 2, :, :], clampv[:, 1, :, :], ACT.Exp).then_inc(sp_exp, 1)
            act.wait_ge(sp_one, 1)
            nc.scalar.activation(clampv[:, 4, :, :], clampv[:, 3, :, :], ACT.Ln).then_inc(sp_ln, 1)
            act.wait_ge(lo_ready, 1)
            act.wait_ge(const_done, 4)

            def onehots_act(i, k, b):
                for j in range(ACTJ):
                    nc.scalar.activation(dist[0:CHUNK, k, j, 0:NP], iota_k[0:CHUNK, 0:NP], ACT.Abs,
                                         bias=neglo[0:CHUNK, bass.ds(b * CPG + j, 1)]).then_inc(dist_ready, 1)
                for j in range(ACTJ):
                    act.wait_ge(dist_ready, b * ACTJ + (j + 1))
                    ins = nc.scalar.activation(oh_lo[0:CHUNK, k, j, 0:NP], dist[0:CHUNK, k, j, 0:NP], ACT.Relu,
                                               scale=-1.0, bias=ones[0:CHUNK, 0:1])
                ins.then_inc(onehot_act, 1)

            def counts_copy(k, b):
                act.wait_ge(group_done, b + 1)
                if not isinstance(b, int):
                    act.wait_ge(added, b - 1)
                nc.scalar.copy(counts[0:NP, k, :], PS[0:NP, k, 0:KEYS]).then_inc(counted, 1)

            onehots_act(0, 0, 0)
            onehots_act(0, 1, 1)
            counts_copy(0, 0)
            onehots_act(1, 0, 2)
            counts_copy(1, 1)
            onehots_act(1, 1, 3)
            with act.Fori(1, NG // 2 - 1) as i:
                for k in range(2):
                    counts_copy(k, i * 2 + k)
                    onehots_act(i + 1, k, i * 2 + (k + 2))
            for k in range(2):
                act.wait_ge(group_done, NG - 1 + k)
                act.wait_ge(added, NG - 3 + k)
                nc.scalar.copy(counts[0:NP, k, :], PS[0:NP, k, 0:KEYS]).then_inc(counted, 1)
            sqrt_of_var(0)
            act.wait_ge(degcol_ready, 1)
            nc.scalar.activation(dis[0:NP, :], PS[0:NP, 3, 0:NT], ACT.Sqrt).then_inc(sd_ready, 1)

            def split_weight(k, raw, name, count):
                act.wait_ge(load[name], count)
                nc.scalar.copy(WH[:, :, :], raw).then_inc(wh_ready, 1)

            act.wait_ge(zeroed, 16)
            act.wait_ge(deg_ready, len(SPLITS))
            split_weight(0, WRAW[:, :, :], "w0", 16)
            act.wait_ge(load["w12"], 32)
            for t in range(NT):
                act.wait_ge(val_ready, t + 1)
                nc.scalar.copy(YH[0:NP, t, :], val[0:NP, t % 2, :]).then_inc(yh_ready, 1)

            n = 0
            for l in range(LAYERS):
                def relu_tiles(tiles):
                    for t in tiles:
                        m = (l + 1) * NT + t
                        act.wait_ge(pre_ready, l * NT + t + 1)
                        if t < 2:
                            act.wait_ge(agg_ready, FT * len(SPLITS) * (l + 1))
                        act.wait_ge(y_ready, m - 1)
                        nc.scalar.activation(val[0:NP, t % 2, :], tmp[0:NP, t % 2, :], ACT.Relu,
                                             scale=dis[0:NP, t:t + 1]).then_inc(val_ready, 1)
                        act.wait_ge(val_ready, m + 1)
                        nc.scalar.copy(YH[0:NP, t, :], val[0:NP, t % 2, :]).then_inc(yh_ready, 1)

                if l:
                    act.wait_ge(lin_ready, NT * l)
                    split_weight(l, WNEXT[:, l - 1, :, :], "w12", 32)
                for s, (c0, w) in enumerate(SPLITS):
                    for f in range(FT):
                        act.wait_ge(agg_ready, n + 1)
                        if s == 0 and l:
                            act.wait_ge(lin_ready, NT * l)
                        nc.scalar.copy(ZH[:, f, c0:c0 + w], PS[:, n % 6, 0:w]).then_inc(zh_ready, 1)
                        n += 1
                if l < LAYERS - 1:
                    relu_tiles(range(NT))
            sqrt_of_var(1)

            def h1_copy(c):
                net, r = c // NRC, c % NRC
                act.wait_ge(f1_ready, 2 * c + 1)
                if net:
                    act.wait_ge(f2_ready, 2 * (r + 1))
                nc.scalar.activation(h1t[:, 0, r * RC:(r + 1) * RC], PS[0:GH, 2 * (c % 2), 0:RC], ACT.Relu
                                     ).then_inc(h1_act, 1)

            def h2_copy(c):
                net, r = c // NRC, c % NRC
                act.wait_ge(f2_ready, 2 * c + 1)
                if net:
                    act.wait_ge(f3_ready, r + 1)
                nc.scalar.activation(h2t[:, 0, r * RC:(r + 1) * RC], PS[0:GH, 4, 0:RC], ACT.Relu,
                                     bias=b2f[:, net, 0:1]).then_inc(h2_act, 1)

            h1_copy(0)
            for c in range(2 * NRC):
                if c + 1 < 2 * NRC:
                    h1_copy(c + 1)
                h2_copy(c)
            sqrt_of_var(2)
            split_weight(3, WRAW[:, :, :], "wr", 16)
            for t in range(NT):
                act.wait_ge(xn_ready, NT + t + 1)
                nc.scalar.copy(YH[0:NP, t, :], XN[0:NP, t, :]).then_inc(yh_ready, 1)
            for n, (s, f) in enumerate(SF):
                c0, w = SPLITS[s]
                act.wait_ge(sxt_ps, n + 1)
                nc.scalar.copy(ZH[:, f, c0:c0 + w], PS[:, n % 4, 0:w]).then_inc(sxt_hi, 1)
            act.wait_ge(y_ready, NT * (LAYERS + 1))
            act.wait_ge(xn_added, NT)
            for n in range(FT * len(SPLITS)):
                f, s = n // len(SPLITS), n % len(SPLITS)
                c0, w = SPLITS[s]
                act.wait_ge(hr_ps, n + 1)
                nc.scalar.activation(ht[:, f, c0:c0 + w], PS[:, 4 + n % 4, 0:w], ACT.Identity,
                                     bias=sage[:, 0, f:f + 1]).then_inc(hr_ready, 1)
            split_weight(4, WRAW[:, :, :], "wl", 16)
            for n, (s, f) in enumerate(SF):
                c0, w = SPLITS[s]
                act.wait_ge(mean_f32, n + 1)
                nc.scalar.copy(ZH[:, f, c0:c0 + w], tmp[:, n % 2, 0:w]).then_inc(mean_hi, 1)
            act.wait_ge(hstat, 1)
            nc.scalar.activation(hs[:, 1, :], hs[:, 0, :], ACT.Sqrt).then_inc(hsd, 1)
            act.wait_ge(hscale, 1)
            for f in range(FT):
                nc.scalar.activation(ht[:, f, :], ht[:, f, :], ACT.Relu, scale=hs[:, 2, f:f + 1],
                                     bias=hs[:, 3, f:f + 1]).then_inc(hn_ready, 1)
            sqrt_of_var(3)
            for n, (s, f) in enumerate(SF):
                c0, w = SPLITS[s]
                if f % 2 == 0:
                    act.wait_ge(xtp_ready, n + 1)
                    nc.scalar.copy(xt[:, f, c0:c0 + w], PS[:, n % 2, 0:w]).then_inc(xt_act, 1)
            act.wait_ge(zmax_ready, 1)
            nc.scalar.activation(pr[0:NP, :, :], q[0:NP, :, :], ACT.Exp).then_inc(exp_ready, 1)

            act.wait_ge(cw_ps, 1)
            act.wait_ge(xn_stored, 16)
            for s, (c0, w) in enumerate(SPLITS):
                ins = nc.scalar.copy(cwt[:, c0:c0 + w], PS[0:NEXP + 1, CWT_BANKS[s][0], CWT_BANKS[s][1]:CWT_BANKS[s][1] + w])
            ins.then_inc(cwt_ready, 1)

            def turn_t(k, p, rows=128):
                act.wait_ge(tt_ps, p + 1)
                nc.scalar.copy(tt[:, k, :, 0:rows], PS[:, 5, 0:INTER].rearrange("p (i n) -> p i n", i=3)[:, :, 0:rows]
                               ).then_inc(tt_ready, 1)

            def sigmoid(k, p, b=None):
                shared = b is None
                if not shared:
                    e = act.value_load(eb_i[0:1, 0, bass.ds(b, 1)], min_val=0, max_val=NEXP - 1)
                    alpha, rows = acts[:, bass.ds(e, 1), 0], 128
                else:
                    alpha, rows = acts[0:NP, NEXP:NEXP + 1, 0], NP
                act.wait_ge(clip_g, p + 1)
                if not (isinstance(p, int) and p < 2):
                    act.wait_ge(t_ready, p - 1)
                nc.scalar.activation(ss[k][0:rows], hb[k][0:rows, 0:H2:2], ACT.Sigmoid, scale=alpha).then_inc(gate_sig, 1)

            def store(i, k, b):
                act.wait_ge(yo_ready, b + 1)
                act.dma_start(y_dram[bass.ds(b * BS, BS), :], yo[:, k, :]).then_inc(stored[k], 16)

            def result(i, k, b, first=False):
                act.wait_ge(y_done, b + (EARLY + 1))
                if not first:
                    act.wait_ge(stored[k], i * 16)
                nc.scalar.activation(yo[:, k, :], PS[:, 6 + k, :], ACT.Copy,
                                     scale=wslot[:, bass.ds(b, 1)]).then_inc(yo_ready, 1)

            sigmoid(0, 0)
            for p in range(1, EARLY):
                turn_t((p - 1) % 2, p - 1, NP)
                sigmoid(p % 2, p)
            act.wait_ge(tables_ready, 1)
            last = last_pair(act)
            turn_t(1, EARLY - 1, NP)
            sigmoid(0, EARLY, 0)
            turn_t(0, EARLY)
            sigmoid(1, EARLY + 1, 1)
            result(0, 0, 0, first=True)
            with act.Fori(1, NB // 2) as i:
                with act.If(i < last + 1):
                    store(i, 0, i * 2 - 2)
                    turn_t(1, i * 2 + (EARLY - 1))
                    sigmoid(0, i * 2 + EARLY, i * 2)
                    with act.If(i < 2):
                        result(0, 1, 1, first=True)
                    with act.If(i > 1):
                        result(i - 1, 1, i * 2 - 1)
                    store(i, 1, i * 2 - 1)
                    turn_t(0, i * 2 + EARLY)
                    sigmoid(1, i * 2 + (EARLY + 1), i * 2 + 1)
                    result(i, 0, i * 2)
            store(0, 0, last * 2)
            turn_t(1, last * 2 + (EARLY + 1))
            sigmoid(0, last * 2 + (EARLY + 2))
            result(last, 1, last * 2 + 1)
            store(0, 1, last * 2 + 1)
            for j in range(NT - EARLY):
                turn_t(j % 2, last * 2 + (EARLY + 2 + j), NP)
                if j + 1 < NT - EARLY:
                    sigmoid((j + 1) % 2, last * 2 + (EARLY + j + 3))

        @block.tensor
        def _(pe):
            pe.wait_ge(const_done, 4)
            pe.wait_ge(base_ready, 1)
            nc.tensor.matmul(PS[:, 7, 0:NG], ones[0:1, :], dstf[0:1, 0:NCH:CPG],
                             start=True, stop=True).then_inc(base_read, 1)
            pe.wait_ge(bad_ready, 1)
            nc.tensor.matmul(PS[:, 6, 0:1], ones[0:NP, :], bad[0:NP, 0:1], start=True, stop=True).then_inc(bad_sum, 1)

            def group(k, eng_lo, eng_key):
                for j in range(CPG):
                    mm = nc.tensor.matmul(PS[0:NP, k, 0:KEYS], eng_lo[0:CHUNK, k, j, 0:NP], eng_key[0:CHUNK, j, :],
                                          start=(j == 0), stop=(j == CPG - 1))
                return mm

            for k in range(2):
                pe.wait_ge(onehot_act, k + 1)
                pe.wait_ge(onehot_ready, k + 1)
                group(k, oh_lo, ohk[k]).then_inc(group_done, 1)
            with pe.Fori(1, NG // 2) as i:
                for k in range(2):
                    pe.wait_ge(onehot_act, i * 2 + k + 1)
                    pe.wait_ge(onehot_ready, i * 2 + k + 1)
                    pe.wait_ge(counted, i * 2 + k - 1)
                    group(k, oh_lo, ohk[k]).then_inc(group_done, 1)

            pe.wait_ge(const_done, CONSTS)
            pe.wait_ge(flag_ready, 1)
            slow = pe.value_load(flag_i[0:1, 0:1], min_val=0, max_val=1)
            with pe.If(slow > 0):
                with pe.Fori(0, PASSES) as w:
                    with pe.Fori(0, NG) as g:
                        pe.wait_ge(slow_onehot, w * NG + g + 1)
                        group(0, oh_lo, ohk[0]).then_inc(slow_group, 1)

            pe.wait_ge(counts_ready, 1)

            def degrees(unit, table):
                for s, (c0, w) in enumerate(SPLITS):
                    for t in range(NT):
                        mm = nc.tensor.matmul(PS[:, s, 0:w], unit, table[0:NP, t, c0:c0 + w],
                                              start=(t == 0), stop=(t == NT - 1))
                    mm.then_inc(deg_ready, 1)

            with pe.If(slow < 1):
                degrees(WH[0:NP, 0, 0:128], CTR)
            with pe.If(slow > 0):
                degrees(ones[0:NP, :], CT)
            pe.wait_ge(deg_copied, 1)
            for t in range(NT):
                mm = nc.tensor.matmul(PS[0:NP, 3, t:t + 1], invc[0:1, t * NP:(t + 1) * NP], ones[0:1, 0:1],
                                      start=True, stop=True)
            mm.then_inc(degcol_ready, 1)

            def aggregate(dest, f, c0, w, exact, tile_wait=None):
                for t in range(NT):
                    if tile_wait is not None:
                        tile_wait(t)
                    for h, part in enumerate((YH, YL)):
                        lhs, rhs = part[0:NP, t, f * 128:(f + 1) * 128], CTR[0:NP, t, c0:c0 + w]
                        if not exact:
                            lhs, rhs = f32(lhs), CT[0:NP, t, c0:c0 + w]
                        mm = nc.tensor.matmul(dest, lhs, rhs, start=(t == 0 and h == 0),
                                              stop=(t == NT - 1 and h == 1))
                return mm

            PRODUCTS = ((ZH, WH), (ZH, WL), (ZL, WH))

            def gcn(exact):
                n_agg = 0
                for l in range(LAYERS):
                    for s, (c0, w) in enumerate(SPLITS):
                        for f in range(FT):
                            if n_agg >= 6:
                                pe.wait_ge(zl_ready, n_agg - 5)
                            tile_wait = None
                            if s == 0 and f == 0:
                                tile_wait = lambda t: pe.wait_ge(y_ready, NT * l + t + 1)
                            aggregate(PS[:, n_agg % 6, 0:w], f, c0, w, exact, tile_wait).then_inc(agg_ready, 1)
                            n_agg += 1
                    pe.wait_ge(w_ready, l + 1)
                    for t in range(NT):
                        n = l * NT + t
                        pe.wait_ge(zl_ready, n_agg - FT * (2 - min(t // 4, 2)))
                        if n >= 2 + NT * (LAYERS - 1):
                            pe.wait_ge(lin_read, n - 1 - NT * (LAYERS - 1))
                        elif n >= 2:
                            pe.wait_ge(pre_ready, n - 1)
                        for f in range(FT):
                            for h, (z, w) in enumerate(PRODUCTS):
                                mm = nc.tensor.matmul(PS[0:NP, 6 + n % 2, :], z[:, f, t * NP:(t + 1) * NP], w[:, f, :],
                                                      start=(f == 0 and h == 0), stop=(f == FT - 1 and h == 2))
                        mm.then_inc(lin_ready, 1)

            with pe.If(slow < 1):
                gcn(True)
            with pe.If(slow > 0):
                gcn(False)

            pe.wait_ge(feat_ready, 1)
            pe.wait_ge(load["ffn"], 16 * 14)
            for pos in range(POS):
                for t in range(NT):
                    i = pos * NT + t
                    mm = nc.tensor.transpose(PS[0:FK, i // 4, (i % 4) * NP:(i % 4 + 1) * NP], feats[0:NP, pos, t, :],
                                             ident[0:NP, 0:NP])
            mm.then_inc(feat_t, 1)
            pe.wait_ge(ft_ready, 1)
            def first(c):
                net, r = c // NRC, c % NRC
                for m in range(2):
                    if c >= 2:
                        pe.wait_ge(h1_act if m == 0 else h1_dve, c - 1)
                    nc.tensor.matmul(PS[0:GH, 2 * (c % 2) + m, 0:RC], w1f[:, net, m * GH:(m + 1) * GH],
                                     ft[:, r * RC:(r + 1) * RC], start=True, stop=True).then_inc(f1_ready, 1)

            def second(c):
                net, r = c // NRC, c % NRC
                pe.wait_ge(h1_act, c + 1)
                pe.wait_ge(h1_dve, c + 1)
                for m in range(2):
                    if c >= 1:
                        pe.wait_ge(h2_act if m == 0 else h2_dve, c)
                    for k in range(2):
                        mm = nc.tensor.matmul(PS[0:GH, 4 + m, 0:RC], w2f[:, net, k, m * GH:(m + 1) * GH],
                                              h1t[:, k, r * RC:(r + 1) * RC], start=(k == 0), stop=(k == 1))
                    mm.then_inc(f2_ready, 1)

            def third(c):
                net, r = c // NRC, c % NRC
                pe.wait_ge(h2_act, c + 1)
                pe.wait_ge(h2_dve, c + 1)
                for t in range(4 * r, 4 * r + 4):
                    col = (net * POS * NT + t) * 2
                    for k in range(2):
                        mm = nc.tensor.matmul(PS[0:NP, 6, col:col + 2], h2t[:, k, t * NP:(t + 1) * NP],
                                              w3f[:, net, k, :], start=(k == 0), stop=(k == 1))
                mm.then_inc(f3_ready, 1)

            for c in range(2 * NRC + 2):
                if c < 2 * NRC:
                    first(c)
                if 1 <= c <= 2 * NRC:
                    second(c - 1)
                if c >= 2:
                    third(c - 2)

            pe.wait_ge(xn_ready, 2 * NT)
            pe.wait_ge(f3_ready, 2 * NRC)
            for n, (s, f) in enumerate(SF):
                c0, w = SPLITS[s]
                if n >= 4:
                    pe.wait_ge(sxt_ready, n - 3)
                for j in range(w // NP):
                    mm = nc.tensor.transpose(PS[:, n % 4, j * NP:(j + 1) * NP],
                                             XN[0:NP, c0 // NP + j, f * 128:(f + 1) * 128], ident[0:NP, 0:NP])
                mm.then_inc(sxt_ps, 1)

            def sage_linear(banks, wait, signal):
                for n in range(FT * len(SPLITS)):
                    fo, (c0, w) = n // len(SPLITS), SPLITS[n % len(SPLITS)]
                    if n >= 4:
                        pe.wait_ge(wait, n - 3)
                    for f in range(FT):
                        for h, (z, wt) in enumerate(PRODUCTS):
                            mm = nc.tensor.matmul(PS[:, banks + n % 4, 0:w], wt[:, f, fo * 128:(fo + 1) * 128],
                                                  z[:, f, c0:c0 + w], start=(f == 0 and h == 0),
                                                  stop=(f == FT - 1 and h == 2))
                    mm.then_inc(signal, 1)

            pe.wait_ge(sxt_ready, FT * len(SPLITS))
            pe.wait_ge(w_ready, LAYERS + 1)
            sage_linear(4, hr_ready, hr_ps)
            pe.wait_ge(minus_ready, 1)
            pe.wait_ge(y_ready, NT * (LAYERS + 1))

            def sage_sums(exact):
                for n, (s, f) in enumerate(SF):
                    c0, w = SPLITS[s]
                    if n >= 4:
                        pe.wait_ge(mean_f32, n - 3)
                    aggregate(PS[:, n % 4, 0:w], f, c0, w, exact).then_inc(mean_ps, 1)

            with pe.If(slow < 1):
                sage_sums(True)
            with pe.If(slow > 0):
                sage_sums(False)
            pe.wait_ge(mean_ready, FT * len(SPLITS))
            pe.wait_ge(hr_ready, FT * len(SPLITS))
            pe.wait_ge(w_ready, LAYERS + 2)
            sage_linear(4, h_ready, hp_ready)
            pe.wait_ge(hn_ready, FT)
            for t in range(NT):
                if t >= 2:
                    pe.wait_ge(back_read, t - 1)
                for f in range(FT):
                    mm = nc.tensor.transpose(PS[0:NP, 2 + t % 2, f * 128:(f + 1) * 128], ht[:, f, t * NP:(t + 1) * NP],
                                             ident[:, :])
                mm.then_inc(back_ready, 1)

            pe.wait_ge(xn_ready, 3 * NT)
            for n, (s, f) in enumerate(SF):
                c0, w = SPLITS[s]
                if n >= 2:
                    pe.wait_ge(xt_act if n % 2 == 0 else xt_dve, n // 2)
                for j in range(w // NP):
                    mm = nc.tensor.transpose(PS[:, n % 2, j * NP:(j + 1) * NP],
                                             XN[0:NP, c0 // NP + j, f * 128:(f + 1) * 128], ident[0:NP, 0:NP])
                mm.then_inc(xtp_ready, 1)
            pe.wait_ge(xt_act, 6)
            pe.wait_ge(xt_dve, 6)
            pe.wait_ge(load["gate"], 32)
            for t in range(NT):
                for f in range(FT):
                    nc.tensor.matmul(PS[0:NP, 5, t * NEXP:(t + 1) * NEXP], xt[:, f, t * NP:(t + 1) * NP], gw[:, f, :],
                                     start=(f == 0), stop=False)
                mm = nc.tensor.matmul(PS[0:NP, 5, t * NEXP:(t + 1) * NEXP], ones[0:1, 0:NP], gb[0:1, :],
                                      start=False, stop=True)
            mm.then_inc(logit_ready, 1)
            def turn_rows(i, k, b):
                pe.wait_ge(gathered[k], i * 16 + 16)
                for f in range(FT):
                    mm = nc.tensor.transpose(PS[:, 4, f * 128:(f + 1) * 128], xg[:, k, f * 128:(f + 1) * 128], ident[:, :])
                mm.then_inc(xt_ps, 1)

            def up_bank_free(p):
                if not (isinstance(p, int) and p < 2):
                    pe.wait_ge(clip_done, p - 1)

            def shared_up(k, p, t):
                up_bank_free(p)
                for h in range(2):
                    for f in range(FT):
                        mm = nc.tensor.matmul(PS[0:NP, 2 * k + h, 0:INTER], xt[:, f, t * NP:(t + 1) * NP],
                                              SW[:, f * H2 + h * INTER:f * H2 + (h + 1) * INTER],
                                              start=(f == 0), stop=(f == FT - 1))
                mm.then_inc(hb_ready, 1)

            def up(i, k, b):
                off = pe.value_load(eb_i[0:1, 1, bass.ds(b, 1)], min_val=0, max_val=(NWB - 1) * WBUF)
                pe.wait_ge(w1_in[k], i * 32 + 32)
                pe.wait_ge(xgt_ready, b + 1)
                up_bank_free(b + EARLY)
                for h in range(2):
                    for f in range(FT):
                        mm = nc.tensor.matmul(PS[:, 2 * k + h, 0:INTER], xgt[:, k, f, :],
                                              WB[:, bass.ds(off + (f * H2 + h * INTER), INTER)],
                                              start=(f == 0), stop=(f == FT - 1))
                mm.then_inc(hb_ready, 1)

            def turn_act(k, p, rows=128):
                pe.wait_ge(t_ready, p + 1)
                if not (isinstance(p, int) and p < 1):
                    pe.wait_ge(tt_ready, p)
                for j in range(3):
                    mm = nc.tensor.transpose(PS[:, 5, j * 128:j * 128 + rows], tb[0:rows, k, j * 128:(j + 1) * 128],
                                             ident[0:rows, 0:rows])
                mm.then_inc(tt_ps, 1)

            def shared_down(k, p, t):
                pe.wait_ge(tt_ready, p + 1)
                for j in range(3):
                    nc.tensor.matmul(PS[0:NP, 6 + k, :], tt[:, k, j, 0:NP], SW[:, O_W2 + j * D:O_W2 + (j + 1) * D],
                                     start=(j == 0), stop=False)
                nc.tensor.matmul(PS[0:NP, 6 + k, :], cwt[:, t * NP:(t + 1) * NP], b2m, start=False, stop=True
                                 ).then_inc(y_done, 1)

            def down(i, k, b):
                off = pe.value_load(eb_i[0:1, 1, bass.ds(b, 1)], min_val=0, max_val=(NWB - 1) * WBUF)
                pe.wait_ge(w2_in[k], i * 16 + 16)
                pe.wait_ge(tt_ready, b + (EARLY + 1))
                if isinstance(b, int) and b < 2:
                    pe.wait_ge(z_added, EARLY - 1 + b)
                else:
                    pe.wait_ge(yo_ready, b - 1)
                for j in range(3):
                    mm = nc.tensor.matmul(PS[:, 6 + k, :], tt[:, k, j, :], WB[:, bass.ds(off + (O_W2 + j * D), D)],
                                          start=(j == 0), stop=(j == 2))
                mm.then_inc(y_done, 1)

            pe.wait_ge(load["sw"], 48)
            shared_up(0, 0, 0)
            shared_up(1, 1, 1)
            pe.wait_ge(sel_ready, 1)
            pe.wait_ge(const_done, CONSTS + 9)
            nc.tensor.matmul(PS[0:NP, 4, 0:NT * NEXP], below[0:NP, 0:NP], q[0:NP, :, :].rearrange("p t e -> p (t e)"),
                             start=True, stop=False)
            nc.tensor.matmul(PS[0:NP, 4, 0:NT * NEXP], ones[0:NP, 0:NP],
                             cum[0:NP, 0:NT, :].rearrange("p t e -> p (t e)"), start=False, stop=True)
            nc.tensor.matmul(PS[:, 4, NT * NEXP:(NT + 1) * NEXP], ones[0:NP, :], cum[0:NP, NT, :], start=True, stop=True
                             ).then_inc(rank_ready, 1)
            for t in range(NT):
                s = min(t // 4, 2)
                n, o = CWT_BANKS[s]
                mm = nc.tensor.transpose(PS[0:NEXP + 1, n, o + t * NP - SPLITS[s][0]:o + (t + 1) * NP - SPLITS[s][0]],
                                         cw[0:NP, t, :], ident[0:NP, 0:NP])
            mm.then_inc(cw_ps, 1)
            pe.wait_ge(load["b2"], 16)
            turn_act(0, 0, NP)
            pe.wait_ge(cwt_ready, 1)
            shared_down(0, 0, 0)
            for p in range(2, EARLY):
                shared_up(p % 2, p, p)
                if p == EARLY - 3:
                    pe.wait_ge(slots_ready, 1)
                    for i in range(ASSIGN):
                        mm = nc.tensor.matmul(PS[:, 4, 0:2 * NB], ohr[0:NP, i, :],
                                              ohb[0:NP, i, :, :].rearrange("p a b -> p (a b)"),
                                              start=(i == 0), stop=(i == ASSIGN - 1))
                    mm.then_inc(table_ps, 1)
                turn_act((p - 1) % 2, p - 1, NP)
                if p >= 3:
                    pe.wait_ge(z_added, p - 2)
                shared_down((p - 1) % 2, p - 1, p - 1)

            pe.wait_ge(tables_ready, 1)
            last = last_pair(pe)
            turn_rows(0, 0, 0)
            up(0, 0, 0)
            turn_act(1, EARLY - 1, NP)
            turn_rows(0, 1, 1)
            pe.wait_ge(z_added, EARLY - 2)
            shared_down(1, EARLY - 1, EARLY - 1)
            up(0, 1, 1)
            turn_act(0, EARLY)
            pe.wait_ge(xgt_ready, 2)
            turn_rows(1, 0, 2)
            down(0, 0, 0)
            with pe.Fori(1, NB // 2) as i:
                with pe.If(i < last + 1):
                    up(i, 0, i * 2)
                    turn_act(1, i * 2 + (EARLY - 1))
                    turn_rows(i, 1, i * 2 + 1)
                    with pe.If(i < 2):
                        down(0, 1, 1)
                    with pe.If(i > 1):
                        down(i - 1, 1, i * 2 - 1)
                    up(i, 1, i * 2 + 1)
                    turn_act(0, i * 2 + EARLY)
                    with pe.If(i < last):
                        turn_rows(i + 1, 0, i * 2 + 2)
                    down(i, 0, i * 2)
            shared_up(0, last * 2 + (EARLY + 2), EARLY)
            turn_act(1, last * 2 + (EARLY + 1))
            down(last, 1, last * 2 + 1)
            for j in range(NT - EARLY):
                if j + 1 < NT - EARLY:
                    shared_up((j + 1) % 2, last * 2 + (EARLY + j + 3), EARLY + j + 1)
                turn_act(j % 2, last * 2 + (EARLY + 2 + j), NP)
                if j < 2:
                    pe.wait_ge(yo_ready, last * 2 + (j + 1))
                else:
                    pe.wait_ge(z_added, EARLY + j - 1)
                shared_down(j % 2, last * 2 + (EARLY + 2 + j), EARLY + j)

        @block.vector
        def _(dve):
            v = nc.vector
            link = counting(dve, step)

            dve.wait_ge(load["acts"], 16)
            link(v.tensor_scalar(clampv[:, 0, :, :], acts[:, :, 3:5], -1.0, None, ALU.mult))
            v.tensor_tensor(clampv[:, 1, :, :], clampv[:, 0, :, :], acts[:, :, 3:5], ALU.min).then_inc(sp_ready, 1)
            dve.wait_ge(sp_exp, 1)
            v.tensor_scalar(clampv[:, 3, :, :], clampv[:, 2, :, :], 1.0, None, ALU.add).then_inc(sp_one, 1)
            dve.wait_ge(sp_ln, 1)
            link(v.tensor_scalar(clampv[:, 2, :, :], acts[:, :, 3:5], 0.0, None, ALU.max))
            link(v.tensor_tensor(clampv[:, 0, :, :], clampv[:, 2, :, :], clampv[:, 4, :, :], ALU.add))
            link(v.tensor_scalar(clampv[:, 1, :, :], clampv[:, 0, :, :], -1.0, None, ALU.mult))

            def layer_norm(k, stats_done=False):
                if not stats_done:
                    for t in range(NT):
                        ins = v.bn_stats(stats[0:NP, t, :], X[0:NP, t, :])
                    link(ins)
                for t in range(NT):
                    ins = v.bn_aggr(mv[0:NP, t, :], stats[0:NP, t, :])
                link(ins)
                v.tensor_scalar(mv[0:NP, :, 1], mv[0:NP, :, 1], EPS, None, ALU.add).then_inc(var_ready, 1)
                dve.wait_ge(sd_ready, k + 1 if k == 0 else k + 2)
                link(v.reciprocal(rstd[0:NP, :], sd[0:NP, :]))
                if k == 0:
                    return
                for t in range(NT):
                    v.tensor_scalar(XN[0:NP, t, :], X[0:NP, t, :], mv[0:NP, t, 0:1], rstd[0:NP, t:t + 1],
                                    ALU.subtract, ALU.mult).then_inc(xn_ready, 1)
                dve.wait_ge(xn_ready, k * NT)

            dve.wait_ge(load["edges"], 32)
            v.tensor_copy(dstf[0:CHUNK, :], dst_i[0:CHUNK, :]).then_inc(base_ready, 1)
            link(v.tensor_copy(srcf[0:CHUNK, :], src_i[0:CHUNK, :]))
            link(v.tensor_scalar(hi[0:CHUNK, :], srcf[0:CHUNK, :], -62.0, 1.0 / NP, ALU.add, ALU.mult))
            link(v.tensor_scalar(rel[0:CHUNK, :], hi[0:CHUNK, :], MAGIC, None, ALU.add))
            link(v.tensor_scalar(hi[0:CHUNK, :], rel[0:CHUNK, :], -MAGIC, None, ALU.add))
            link(v.scalar_tensor_tensor(out=lo[0:CHUNK, :], in0=hi[0:CHUNK, :], scalar=-float(NP),
                                        in1=srcf[0:CHUNK, :], op0=ALU.mult, op1=ALU.add))
            v.tensor_scalar(neglo[0:CHUNK, :], lo[0:CHUNK, :], -1.0, None, ALU.mult).then_inc(lo_ready, 1)
            dve.wait_ge(base_read, 1)
            v.tensor_copy(wbase_i[0:1, :], PS[0:1, 7, 0:NG]).then_inc(windows_ready, 1)
            link(v.tensor_copy(wbase[:, :], PS[:, 7, 0:NG]))
            three = lambda m: m[0:CHUNK, :].rearrange("p (g j) -> p g j", j=CPG)

            def make_keys(link_to):
                link_to(v.tensor_tensor(three(rel), three(dstf),
                                        wbase[0:CHUNK, :].rearrange("p (g o) -> p g o", o=1).to_broadcast([CHUNK, NG, CPG]),
                                        ALU.subtract))
                link_to(v.tensor_scalar(srcf[0:CHUNK, :], rel[0:CHUNK, :], 0.0, None, ALU.is_ge))
                link_to(v.scalar_tensor_tensor(out=srcf[0:CHUNK, :], in0=rel[0:CHUNK, :], scalar=float(WIN),
                                               in1=srcf[0:CHUNK, :], op0=ALU.is_lt, op1=ALU.mult))
                link_to(v.scalar_tensor_tensor(out=rel[0:CHUNK, :], in0=hi[0:CHUNK, :], scalar=float(WIN),
                                               in1=rel[0:CHUNK, :], op0=ALU.mult, op1=ALU.add))
                link_to(v.scalar_tensor_tensor(out=key[0:CHUNK, :], in0=rel[0:CHUNK, :], scalar=1.0,
                                               in1=srcf[0:CHUNK, :], op0=ALU.add, op1=ALU.mult))
                link_to(v.tensor_scalar(key[0:CHUNK, :], key[0:CHUNK, :], -1.0, None, ALU.add))

            make_keys(link)
            link(v.tensor_reduce(bad[0:CHUNK, 1:2], srcf[0:CHUNK, :], AX.X, ALU.min))
            v.tensor_scalar(bad[0:CHUNK, 0:1], bad[0:CHUNK, 1:2], -1.0, 1.0, ALU.mult, ALU.add).then_inc(bad_ready, 1)
            dve.wait_ge(bad_sum, 1)
            link(v.tensor_scalar(bad[:, 2:3], PS[:, 6, 0:1], 0.5, None, ALU.is_ge))
            last = NG - APART
            link(v.memset(apart[0:1, :, :], 1.0))
            link(v.tensor_tensor(apart[0:1, 0, 0:NG - 1], wbase[0:1, 1:NG], wbase[0:1, 0:NG - 1], ALU.is_ge))
            link(v.tensor_tensor(apart[0:1, 1, 0:last], wbase[0:1, APART:NG], wbase[0:1, 0:last], ALU.subtract))
            link(v.tensor_scalar(apart[0:1, 1, 0:last], apart[0:1, 1, 0:last], float(WIN), None, ALU.is_ge))
            link(v.tensor_reduce(bad[0:1, 3:4], apart[0:1, :, :].rearrange("p a g -> p (a g)"), AX.X, ALU.min))
            link(v.scalar_tensor_tensor(out=bad[0:1, 2:3], in0=bad[0:1, 3:4], scalar=0.5, in1=bad[0:1, 2:3],
                                        op0=ALU.is_lt, op1=ALU.max))
            v.tensor_copy(flag_i[0:1, 0:1], bad[0:1, 2:3]).then_inc(flag_ready, 1)
            dve.wait_ge(const_done, 4)
            link(v.tensor_copy(WH[:, 0, 0:128], ones[:, :]))

            dve.wait_ge(const_done, 4)

            def onehots(k, c, first=0):
                for j in range(CPG):
                    if j >= first:
                        v.tensor_scalar(oh_lo[0:CHUNK, k, j, 0:NP], iota_k[0:CHUNK, 0:NP], lo[0:CHUNK, bass.ds(c + j, 1)],
                                        None, ALU.is_equal)
                    ins = v.tensor_scalar(ohk[k][0:CHUNK, j, :], iota_k[0:CHUNK, :], key[0:CHUNK, bass.ds(c + j, 1)],
                                          None, ALU.is_equal)
                return ins

            for k in range(2):
                onehots(k, k * CPG, ACTJ).then_inc(onehot_ready, 1)
            with dve.Fori(1, NG // 2) as i:
                for k in range(2):
                    dve.wait_ge(group_done, i * 2 + k - 1)
                    onehots(k, (i * 2 + k) * CPG, ACTJ).then_inc(onehot_ready, 1)

            dve.wait_ge(load["x"], 16)
            layer_norm(0)
            dve.wait_ge(added, NG)

            slow = dve.value_load(flag_i[0:1, 0:1], min_val=0, max_val=1)
            with dve.If(slow > 0):
                SLOW0, SLOWK = 2, 7
                v.memset(CT[0:NP, :, :], 0.0).then_inc(slow_step, 1)
                v.memset(wbase[:, :], 0.0).then_inc(slow_step, 1)
                dve.wait_ge(slow_step, SLOW0)
                with dve.Fori(0, PASSES) as w:
                    done = [0]

                    def slow_link(ins):
                        done[0] += 1
                        at = dve.to_reg(w * (SLOWK + NG) + (SLOW0 + done[0]))
                        ins.then_inc(slow_step, 1)
                        dve.wait_ge(flag_ready, 1)
                        dve.wait_ge(slow_step, at)

                    make_keys(slow_link)
                    slow_link(v.tensor_scalar(wbase[:, :], wbase[:, :], float(WIN), None, ALU.add))
                    with dve.Fori(0, NG) as g:
                        onehots(0, g * CPG).then_inc(slow_onehot, 1)
                        dve.wait_ge(slow_group, w * NG + g + 1)
                        dest = CT[0:NP, :, bass.ds(w * WIN, WIN)]
                        v.tensor_tensor(dest, PS[0:NP, 0, 0:KEYS].rearrange("p (t w) -> p t w", t=NT), dest, ALU.add
                                        ).then_inc(slow_step, 1)
                        dve.wait_ge(slow_step, w * (SLOWK + NG) + g + (SLOW0 + SLOWK + 1))

            dve.wait_ge(const_done, CONSTS)

            def self_loops(op, signal):
                for table, on in ((CTR, slow < 1), (CT, slow > 0)):
                    with dve.If(on):
                        for t in range(NT):
                            dest = table[0:NP, t, t * NP:(t + 1) * NP]
                            ins = v.tensor_tensor(dest, f32(dest) if table is CTR else dest, ident[0:NP, 0:NP], op)
                        ins.then_inc(signal, 1)

            self_loops(ALU.add, counts_ready)

            for s, (c0, w) in enumerate(SPLITS):
                dve.wait_ge(deg_ready, s + 1)
                ins = v.tensor_copy(invc[:, c0:c0 + w], PS[:, s, 0:w])
            ins.then_inc(deg_copied, 1)
            dve.wait_ge(sd_ready, 2)
            link(v.reciprocal(dis[0:NP, :], dis[0:NP, :]))
            link(v.tensor_tensor(rdis[0:NP, :], rstd[0:NP, :], dis[0:NP, :], ALU.mult))
            def low_part(m, t, source):
                dve.wait_ge(yh_ready, m + 1)
                v.tensor_tensor(YL[0:NP, t, :], source, f32(YH[0:NP, t, :]), ALU.subtract).then_inc(y_ready, 1)

            def split_weight(k, raw):
                dve.wait_ge(wh_ready, k + 1)
                v.tensor_tensor(WL[:, :, :], raw, f32(WH[:, :, :]), ALU.subtract).then_inc(w_ready, 1)

            for t in range(NT + 1):
                if t < NT:
                    if t >= 2:
                        dve.wait_ge(yh_ready, t - 1)
                        dve.wait_ge(y_ready, t - 1)
                    v.tensor_scalar(val[0:NP, t % 2, :], X[0:NP, t, :], mv[0:NP, t, 0:1], rdis[0:NP, t:t + 1],
                                    ALU.subtract, ALU.mult).then_inc(val_ready, 1)
                if t:
                    dve.wait_ge(val_ready, t)
                    low_part(t - 1, t - 1, val[0:NP, (t - 1) % 2, :])
            split_weight(0, WRAW[:, :, :])
            dve.wait_ge(degcol_ready, 1)
            link(v.tensor_scalar(invc[:, :], invc[:, :], -1.0, 1.0, ALU.add, ALU.max))
            link(v.reciprocal(invc[:, :], invc[:, :]))
            dve.wait_ge(load["gb"], 16 * LAYERS)

            n = 0
            for l in range(LAYERS):
                if l:
                    dve.wait_ge(lin_ready, NT * l)
                    split_weight(l, WNEXT[:, l - 1, :, :])
                for s, (c0, w) in enumerate(SPLITS):
                    for f in range(FT):
                        dve.wait_ge(zh_ready, n + 1)
                        v.tensor_tensor(ZL[:, f, c0:c0 + w], PS[:, n % 6, 0:w], f32(ZH[:, f, c0:c0 + w]), ALU.subtract
                                        ).then_inc(zl_ready, 1)
                        n += 1
                for t in range(NT + 1):
                    m = l * NT + t
                    if t < NT:
                        dve.wait_ge(lin_ready, m + 1)
                        if l < LAYERS - 1 and m >= 2:
                            dve.wait_ge(val_ready, NT + m - 1)
                        if l == LAYERS - 1 and t < 2:
                            dve.wait_ge(val_ready, NT * LAYERS)
                        ins = v.scalar_tensor_tensor(out=tmp[0:NP, t % 2, :], in0=PS[0:NP, 6 + m % 2, :],
                                                     scalar=dis[0:NP, t:t + 1], in1=bias[0:NP, l, :],
                                                     op0=ALU.mult, op1=ALU.add)
                        ins.then_inc(pre_ready if l < LAYERS - 1 else lin_read, 1)
                    if l < LAYERS - 1 and t:
                        low_part(NT + m - 1, t - 1, val[0:NP, (t - 1) % 2, :])
                    if l == LAYERS - 1 and t < NT:
                        dve.wait_ge(lin_read, t + 1)
                        link(v.scalar_tensor_tensor(out=X[0:NP, t, :], in0=tmp[0:NP, t % 2, :], scalar=0.0,
                                                    in1=X[0:NP, t, :], op0=ALU.max, op1=ALU.add))
                        ins = v.bn_stats(stats[0:NP, t, :], X[0:NP, t, :])
            link(ins)

            layer_norm(1, stats_done=True)
            nib = XN[0:NP, :, 16:80].rearrange("p t (g j) -> p t g j", j=16)
            link(v.tensor_scalar(fk[0:NP, :, :, :], nib, 0.5, None, ALU.is_gt))
            wjb = wj[0:NP, :].rearrange("p (a j) -> p a j", a=1)
            link(v.tensor_tensor(fk[0:NP, :, :, :].rearrange("p t g j -> p (t g) j"),
                                 fk[0:NP, :, :, :].rearrange("p t g j -> p (t g) j"),
                                 wjb.to_broadcast([NP, NT * 4, 16]), ALU.mult))
            link(v.tensor_reduce(fm[0:NP, :, :], fk[0:NP, :, :, :], AX.X, ALU.max))
            link(v.tensor_scalar(fg[0:NP, :, :], fm[0:NP, :, :], -1.0, 16.0, ALU.mult, ALU.add))
            link(v.scalar_tensor_tensor(out=fg[0:NP, :, :], in0=fm[0:NP, :, :], scalar=0.0, in1=fg[0:NP, :, :],
                                        op0=ALU.is_gt, op1=ALU.mult))
            for pos in range(POS):
                v.tensor_copy(feats[0:NP, pos, :, 0], fg[0:NP, :, pos])
                v.tensor_copy(feats[0:NP, pos, :, 1], fg[0:NP, :, 2 + pos])
                ins = v.tensor_copy(feats[0:NP, pos, :, 2:4], XN[0:NP, :, 105:107])
            ins.then_inc(feat_ready, 1)
            for c in range(3):
                ins = v.tensor_scalar(msk[0:NP, c, :], XN[0:NP, :, c], 0.5, None, ALU.is_gt)
            link(ins)
            v.tensor_tensor(msk[0:NP, 3, :], msk[0:NP, 0, :], msk[0:NP, 1, :], ALU.mult)
            link(v.tensor_tensor(msk[0:NP, 4, :], msk[0:NP, 0, :], msk[0:NP, 2, :], ALU.mult))
            link(v.tensor_tensor(msk[0:NP, 7, :], msk[0:NP, 4, :], msk[0:NP, 1, :], ALU.mult))
            link(v.tensor_tensor(msk[0:NP, 5, :], msk[0:NP, 4, :], msk[0:NP, 7, :], ALU.subtract))
            link(v.tensor_tensor(msk[0:NP, 6, :], msk[0:NP, 3, :], msk[0:NP, 5, :], ALU.add))
            for c in range(NRC):
                w = min(4, POS * NT - 4 * c) * NP
                dve.wait_ge(feat_t, 1)
                ins = v.tensor_copy(ft[:, c * RC:c * RC + w], PS[0:FK, c, 0:w])
            ins.then_inc(ft_ready, 1)
            def h1_copy(c):
                net, r = c // NRC, c % NRC
                dve.wait_ge(f1_ready, 2 * c + 2)
                if net:
                    dve.wait_ge(f2_ready, 2 * (r + 1))
                v.tensor_scalar(h1t[:, 1, r * RC:(r + 1) * RC], PS[0:GH, 2 * (c % 2) + 1, 0:RC], 0.0, None, ALU.max
                                ).then_inc(h1_dve, 1)

            def h2_copy(c):
                net, r = c // NRC, c % NRC
                dve.wait_ge(f2_ready, 2 * c + 2)
                if net:
                    dve.wait_ge(f3_ready, r + 1)
                v.tensor_scalar(h2t[:, 1, r * RC:(r + 1) * RC], PS[0:GH, 5, 0:RC], b2f[:, net, 1:2], 0.0,
                                ALU.add, ALU.max).then_inc(h2_dve, 1)

            h1_copy(0)
            for c in range(2 * NRC):
                if c + 1 < 2 * NRC:
                    h1_copy(c + 1)
                h2_copy(c)
                v.tensor_tensor(X[0:NP, c, :], X[0:NP, c, :], XN[0:NP, c, :], ALU.add)
            dve.wait_ge(f3_ready, 2 * NRC)
            for net in range(2):
                o = net * POS * NT * 2
                link(v.tensor_tensor(yv[0:NP, net, :, :],
                                     PS[0:NP, 6, o:o + POS * NT * 2].rearrange("p (t c) -> p t c", c=2),
                                     b3f[0:NP, net, :].rearrange("p (a c) -> p a c", a=1).to_broadcast([NP, POS * NT, 2]),
                                     ALU.add))
                m = msk[0:NP, 3 if net == 0 else 5, :].rearrange("p (t o) -> p t o", o=1).to_broadcast([NP, NT, 2])
                for pos in range(POS):
                    view = yv[0:NP, net, pos * NT:(pos + 1) * NT, :]
                    ins = v.tensor_tensor(view, view, m, ALU.mult)
                link(ins)
            link(v.tensor_tensor(res[0:NP, :, :], yv[0:NP, 0, :, :], yv[0:NP, 1, :, :], ALU.add))
            link(v.tensor_scalar(msk[0:NP, 7, :], res[0:NP, NT:2 * NT, 1], 0.5, None, ALU.is_gt))
            link(v.tensor_tensor(msk[0:NP, 7, :], msk[0:NP, 7, :], msk[0:NP, 6, :], ALU.mult))
            link(v.tensor_scalar(res[0:NP, :, :], res[0:NP, :, :], 0.0, 15.0, ALU.max, ALU.min))
            link(v.tensor_scalar(res[0:NP, :, :], res[0:NP, :, :], MAGIC, None, ALU.add))
            link(v.tensor_scalar(res[0:NP, :, :], res[0:NP, :, :], -MAGIC, None, ALU.add))
            link(v.tensor_scalar(msk[0:NP, 6, :], msk[0:NP, 6, :], 2.0, None, ALU.mult))
            wide = lambda m: m.rearrange("p (t o) -> p t o", o=1).to_broadcast([NP, NT, 16])
            cjb = cj[0:NP, :].rearrange("p (a j) -> p a j", a=1).to_broadcast([NP, NT, 16])
            for pos in range(POS):
                link(v.tensor_tensor(oh2[0:NP, :, :], cjb,
                                     res[0:NP, pos * NT:(pos + 1) * NT, 0:1].to_broadcast([NP, NT, 16]), ALU.is_equal))
                link(v.tensor_tensor(oh2[0:NP, :, :], oh2[0:NP, :, :], wide(msk[0:NP, 6, :]), ALU.mult))
                view = X[0:NP, :, 128 + 16 * pos:144 + 16 * pos]
                link(v.tensor_tensor(view, view, oh2[0:NP, :, :], ALU.add))
            link(v.tensor_tensor(X[0:NP, :, 160], X[0:NP, :, 160], msk[0:NP, 7, :], ALU.add))

            self_loops(ALU.subtract, minus_ready)
            layer_norm(2)
            for t in range(NT):
                low_part(LAYERS * NT + t, t, XN[0:NP, t, :])
            for n, (s, f) in enumerate(SF):
                c0, w = SPLITS[s]
                dve.wait_ge(sxt_hi, n + 1)
                v.tensor_tensor(ZL[:, f, c0:c0 + w], PS[:, n % 4, 0:w], f32(ZH[:, f, c0:c0 + w]), ALU.subtract
                                ).then_inc(sxt_ready, 1)
            split_weight(3, WRAW[:, :, :])
            for t in range(NT):
                v.tensor_tensor(X[0:NP, t, :], X[0:NP, t, :], XN[0:NP, t, :], ALU.add).then_inc(xn_added, 1)
            for n in range(len(SF) + 1):
                if n < len(SF):
                    s, f = SF[n]
                    c0, w = SPLITS[s]
                    dve.wait_ge(mean_ps, n + 1)
                    if n >= 2:
                        dve.wait_ge(mean_ready, n - 1)
                    v.tensor_tensor(tmp[:, n % 2, 0:w], PS[:, n % 4, 0:w], invc[:, c0:c0 + w], ALU.mult
                                    ).then_inc(mean_f32, 1)
                if n:
                    s, f = SF[n - 1]
                    c0, w = SPLITS[s]
                    dve.wait_ge(mean_hi, n)
                    v.tensor_tensor(ZL[:, f, c0:c0 + w], tmp[:, (n - 1) % 2, 0:w], f32(ZH[:, f, c0:c0 + w]),
                                    ALU.subtract).then_inc(mean_ready, 1)
            split_weight(4, WRAW[:, :, :])
            for n in range(FT * len(SPLITS)):
                f, s = n // len(SPLITS), n % len(SPLITS)
                c0, w = SPLITS[s]
                dve.wait_ge(hp_ready, n + 1)
                dve.wait_ge(hr_ready, n + 1)
                v.tensor_tensor(ht[:, f, c0:c0 + w], PS[:, 4 + n % 4, 0:w], ht[:, f, c0:c0 + w], ALU.add
                                ).then_inc(h_ready, 1)
                dve.wait_ge(h_ready, n + 1)
                ins = v.bn_stats(hst[:, f, s, :], ht[:, f, c0:c0 + w])
            link(ins)
            for f in range(FT):
                ins = v.bn_aggr(hmv[:, f, :], hst[:, f, :, :].rearrange("p s k -> p (s k)"))
            link(ins)
            v.tensor_scalar(hs[:, 0, :], hmv[:, :, 1], EPS, None, ALU.add).then_inc(hstat, 1)
            dve.wait_ge(hsd, 1)
            dve.wait_ge(load["sage"], 48)
            link(v.reciprocal(hs[:, 2, :], hs[:, 1, :]))
            link(v.tensor_tensor(hs[:, 2, :], hs[:, 2, :], sage[:, 1, :], ALU.mult))
            link(v.tensor_tensor(hs[:, 3, :], hmv[:, :, 0], hs[:, 2, :], ALU.mult))
            v.tensor_tensor(hs[:, 3, :], sage[:, 2, :], hs[:, 3, :], ALU.subtract).then_inc(hscale, 1)
            for t in range(NT):
                dve.wait_ge(back_ready, t + 1)
                v.tensor_tensor(X[0:NP, t, :], PS[0:NP, 2 + t % 2, :], X[0:NP, t, :], ALU.add).then_inc(back_read, 1)
                dve.wait_ge(back_read, t + 1)
                ins = v.bn_stats(stats[0:NP, t, :], X[0:NP, t, :])
            link(ins)

            layer_norm(3, stats_done=True)
            for n, (s, f) in enumerate(SF):
                c0, w = SPLITS[s]
                if f % 2 == 1:
                    dve.wait_ge(xtp_ready, n + 1)
                    v.tensor_copy(xt[:, f, c0:c0 + w], PS[:, n % 2, 0:w]).then_inc(xt_dve, 1)
            R = lambda m: m[0:NP, :, :]
            col = lambda c: rsmall[0:NP, c, :]
            over = lambda m: m.rearrange("p (t o) -> p t o", o=1).to_broadcast([NP, NT, NEXP])
            wjt = wj[0:NP, :].rearrange("p (a j) -> p a j", a=1).to_broadcast([NP, NT, NEXP])
            dve.wait_ge(const_done, CONSTS + 6)
            dve.wait_ge(logit_ready, 1)
            logits = PS[0:NP, 5, 0:NT * NEXP].rearrange("p (t e) -> p t e", t=NT)
            link(v.tensor_reduce(col(0), logits, AX.X, ALU.max))
            v.tensor_tensor(R(q), logits, over(col(0)), ALU.subtract).then_inc(zmax_ready, 1)
            dve.wait_ge(exp_ready, 1)
            link(v.tensor_reduce(col(1), R(pr), AX.X, ALU.add))
            link(v.reciprocal(col(1), col(1)))
            link(v.tensor_tensor(R(pr), R(pr), over(col(1)), ALU.mult))
            for k in range(TOPK):
                link(v.tensor_reduce(col(2 + k), R(pr), AX.X, ALU.max))
                link(v.tensor_tensor(R(q), R(pr), over(col(2 + k)), ALU.is_equal))
                link(v.tensor_tensor(R(q), R(q), wjt, ALU.mult))
                link(v.tensor_reduce(col(4), R(q), AX.X, ALU.max))
                link(v.tensor_tensor(R(oh[k]), wjt, over(col(4)), ALU.is_equal))
                if k == 0:
                    link(v.scalar_tensor_tensor(out=R(pr), in0=R(oh[0]), scalar=-4.0, in1=R(pr),
                                                op0=ALU.mult, op1=ALU.add))
            link(v.tensor_tensor(col(5), col(2), col(3), ALU.add))
            link(v.reciprocal(col(5), col(5)))
            v.tensor_tensor(wsel[0:NP, 0, :], col(2), col(5), ALU.mult)
            link(v.tensor_tensor(wsel[0:NP, 1, :], col(3), col(5), ALU.mult))
            for k in range(TOPK):
                link(v.tensor_tensor(R(pr) if k else cw[0:NP, :, 0:NEXP], R(oh[k]), over(wsel[0:NP, k, :]), ALU.mult))
            link(v.tensor_tensor(cw[0:NP, :, 0:NEXP], cw[0:NP, :, 0:NEXP], R(pr), ALU.add))
            link(v.memset(cw[0:NP, :, NEXP:NEXP + 1], 1.0))
            link(v.tensor_tensor(R(q), R(oh[0]), R(oh[1]), ALU.add))
            for t in range(NT):
                ins = v.tensor_tensor(cum[0:NP, t + 1, :], cum[0:NP, t, :], q[0:NP, t, :], ALU.add)
                if t < NT - 1:
                    link(ins)
            ins.then_inc(sel_ready, 1)

            def rows_copy(k, b):
                dve.wait_ge(xt_ps, b + 1)
                v.tensor_copy(xgt[:, k, :, :], PS[:, 4, :].rearrange("p (f n) -> p f n", f=FT)).then_inc(xgt_ready, 1)

            def units(k, p, b=None, then=None):
                if b is None:
                    rows, one_e, b1 = NP, slice(NEXP, NEXP + 1), SW[0:NP, O_B1:WBUF]
                else:
                    e = dve.value_load(eb_i[0:1, 0, bass.ds(b, 1)], min_val=0, max_val=NEXP - 1)
                    off = dve.value_load(eb_i[0:1, 1, bass.ds(b, 1)], min_val=0, max_val=(NWB - 1) * WBUF)
                    rows, one_e, b1 = 128, bass.ds(e, 1), WB[:, bass.ds(off + O_B1, H2)]
                hi_g, lo_g = clampv[0:rows, 0, one_e, 0], clampv[0:rows, 1, one_e, 0]
                hi_u, lo_u = clampv[0:rows, 0, one_e, 1], clampv[0:rows, 1, one_e, 1]
                gate, upv = hb[k][0:rows, 0:H2:2], hb[k][0:rows, 1:H2:2]
                dve.wait_ge(hb_ready, p + 1)
                if not (isinstance(p, int) and p < 2):
                    dve.wait_ge(t_ready, p - 1)
                v.tensor_tensor(hb[k][0:rows].rearrange("p (h c) -> p h c", h=2), PS[0:rows, 2 * k:2 * k + 2, 0:INTER],
                                b1.rearrange("p (h c) -> p h c", h=2), ALU.add).then_inc(clip_done, 1)
                dve.wait_ge(clip_done, p + 1)
                v.tensor_scalar(gate, gate, lo_g, hi_g, ALU.max, ALU.min).then_inc(clip_g, 1)
                v.tensor_scalar(upv, upv, lo_u, hi_u, ALU.max, ALU.min).then_inc(clip_u, 1)
                if then is not None:
                    then()
                dve.wait_ge(gate_sig, p + 1)
                v.scalar_tensor_tensor(out=ss[k][0:rows], in0=gate, scalar=acts[0:rows, one_e, 1], in1=ss[k][0:rows],
                                       op0=ALU.mult, op1=ALU.mult).then_inc(t_gs, 1)
                dve.wait_ge(t_gs, p + 1)
                dve.wait_ge(clip_u, p + 1)
                if not (isinstance(p, int) and p < 2):
                    dve.wait_ge(tt_ps, p - 1)
                v.scalar_tensor_tensor(out=tb[0:rows, k, :], in0=upv, scalar=acts[0:rows, one_e, 2], in1=ss[k][0:rows],
                                       op0=ALU.add, op1=ALU.mult).then_inc(t_ready, 1)

            def z_add(t, p):
                dve.wait_ge(y_done, p + 1)
                v.tensor_tensor(X[0:NP, t, :], PS[0:NP, 6 + t % 2, :], X[0:NP, t, :], ALU.add).then_inc(z_added, 1)

            dve.wait_ge(load["sw"], 48)
            units(0, 0)
            units(1, 1)
            dve.wait_ge(xn_stored, 16)
            dve.wait_ge(const_done, CONSTS + 9)
            dve.wait_ge(rank_ready, 1)
            BC = lambda c: blkc[:, c, :]
            link(v.tensor_copy(BC(0), PS[:, 4, NT * NEXP:(NT + 1) * NEXP]))
            link(v.tensor_tensor(prod[:, :, 0:NT], BC(0).rearrange("p (e o) -> p e o", o=1).to_broadcast([128, NEXP, NT]),
                                 thr[:, :].rearrange("p (o k) -> p o k", o=1).to_broadcast([128, NEXP, NT]), ALU.is_gt))
            link(v.tensor_reduce(BC(1), prod[:, :, 0:NT], AX.X, ALU.add))
            link(v.tensor_tensor(prod[:, :, :], BC(1).rearrange("p (o e) -> p o e", o=1).to_broadcast([128, NEXP, NEXP]),
                                 le[:, :, :], ALU.mult))
            link(v.tensor_reduce(BC(2), prod[:, :, :], AX.X, ALU.add))
            link(v.tensor_tensor(BC(3), BC(2), BC(1), ALU.subtract))
            link(v.tensor_scalar(BC(3), BC(3), float(BS), None, ALU.mult))
            link(v.tensor_tensor(R(posn), PS[0:NP, 4, 0:NT * NEXP].rearrange("p (t e) -> p t e", t=NT),
                                 blkc[0:NP, 3, :].rearrange("p (o e) -> p o e", o=1).to_broadcast([NP, NT, NEXP]), ALU.add))
            for k in range(TOPK):
                link(v.tensor_tensor(R(pr), R(oh[k]), R(posn), ALU.mult))
                link(v.tensor_reduce(slotf[0:NP, k, :], R(pr), AX.X, ALU.add))
            link(v.tensor_copy(slot_i[0:NP, :, :], slotf[0:NP, :, :]))
            flat = slot_i[0:NP, :, :].rearrange("p k t -> p (k t)")
            v.tensor_scalar(slot_b[0:NP, 0, :], flat, 7, None, ALU.logical_shift_right)
            link(v.tensor_scalar(slot_b[0:NP, 1, :], flat, BS - 1, None, ALU.bitwise_and))
            link(v.tensor_copy(slotp[0:NP, 0:2, :], slot_b[0:NP, :, :]))
            A2 = [NP, ASSIGN, BS]
            v.tensor_tensor(ohr[0:NP, :, :], iota_b[0:NP, :].rearrange("p (o n) -> p o n", o=1).to_broadcast(A2),
                            slotp[0:NP, 1, :].rearrange("p (a o) -> p a o", o=1).to_broadcast(A2), ALU.is_equal)
            A3 = [NP, ASSIGN, NB]
            link(v.tensor_tensor(ohb[0:NP, :, 1, :], iota_b[0:NP, 0:NB].rearrange("p (o n) -> p o n", o=1).to_broadcast(A3),
                                 slotp[0:NP, 0, :].rearrange("p (a o) -> p a o", o=1).to_broadcast(A3), ALU.is_equal))
            for k in range(TOPK):
                rows = slice(k * NT, (k + 1) * NT)
                link(v.tensor_tensor(ohb[0:NP, rows, 0, :], ohb[0:NP, rows, 1, :],
                                     nodef[0:NP, :].rearrange("p (a o) -> p a o", o=1).to_broadcast([NP, NT, NB]), ALU.mult))
            ins = v.tensor_tensor(ohb[0:NP, :, 1, :], ohb[0:NP, :, 1, :],
                                  wsel[0:NP, :, :].rearrange("p k (t o) -> p (k t) o", o=1).to_broadcast(A3), ALU.mult)
            ins.then_inc(slots_ready, 1)
            one = lambda c: ebf[0:1, c, :]
            link(v.tensor_tensor(cnt_e[0:1, :, :], cnt_e[0:1, :, :],
                                 blkc[0:1, 2, :].rearrange("p (o e) -> p o e", o=1).to_broadcast([1, NB, NEXP]), ALU.is_ge))
            link(v.tensor_reduce(ebf[0:1, 0, 0:NB], cnt_e[0:1, :, :], AX.X, ALU.add))
            link(v.tensor_scalar(ebf[0:1, 0, 0:NB], ebf[0:1, 0, 0:NB], float(NEXP - 1), None, ALU.min))
            link(v.memset(ebf[0:1, 1, 0:1], 1.0))
            link(v.tensor_tensor(ebf[0:1, 1, 1:NB], ebf[0:1, 0, 1:NB], ebf[0:1, 0, 0:NB - 1], ALU.not_equal))
            link(v.tensor_tensor(prodb[0:1, :, :], prodb[0:1, :, :],
                                 one(1).rearrange("p (o b) -> p o b", o=1).to_broadcast([1, NB, NB]), ALU.mult))
            link(v.tensor_reduce(one(2), prodb[0:1, :, :], AX.X, ALU.add))
            link(v.tensor_scalar(one(3), one(2), -1.0, 1.0 / NWB, ALU.add, ALU.mult))
            link(v.tensor_scalar(one(3), one(3), MAGIC, None, ALU.add))
            link(v.tensor_scalar(one(3), one(3), -MAGIC, None, ALU.add))
            link(v.scalar_tensor_tensor(out=one(4), in0=one(3), scalar=-float(NWB), in1=one(2), op0=ALU.mult, op1=ALU.add))
            link(v.tensor_scalar(one(4), one(4), float(WBUF), None, ALU.mult))
            v.tensor_copy(eb_i[0:1, 0, :], one(0))
            v.tensor_copy(eb_i[0:1, 1, :], one(4))
            v.tensor_copy(eb_i[0:1, 2, :], one(1))
            link(v.tensor_scalar(ebf[0:1, 3, 0:1], blkc[0:1, 2, NEXP - 1:NEXP], 0.5, -0.75, ALU.mult, ALU.add))
            link(v.tensor_scalar(ebf[0:1, 3, 0:1], ebf[0:1, 3, 0:1], MAGIC, None, ALU.add))
            link(v.tensor_scalar(ebf[0:1, 3, 0:1], ebf[0:1, 3, 0:1], -MAGIC, None, ALU.add))
            link(v.tensor_copy(eb_i[0:1, 3, 0:1], ebf[0:1, 3, 0:1]))
            z_add(0, 0)
            units(0, 2)
            z_add(1, 1)
            units(1, 3)
            dve.wait_ge(table_ps, 1)
            v.tensor_copy(tok[:, :], PS[:, 4, 0:NB])
            v.tensor_copy(wslot[:, :], PS[:, 4, NB:2 * NB]).then_inc(tables_ready, 1)
            dve.wait_ge(tables_ready, 1)
            last = last_pair(dve)
            z_add(2, 2)
            units(0, 4)
            z_add(3, 3)

            units(1, EARLY - 1)
            rows_copy(0, 0)
            z_add(EARLY - 2, EARLY - 2)
            units(0, EARLY, 0)
            rows_copy(1, 1)
            z_add(EARLY - 1, EARLY - 1)
            units(1, EARLY + 1, 1)
            rows_copy(0, 2)
            with dve.Fori(1, NB // 2) as i:
                with dve.If(i < last + 1):
                    units(0, i * 2 + EARLY, i * 2, lambda: rows_copy(1, i * 2 + 1))

                    def next_rows():
                        with dve.If(i < last):
                            rows_copy(0, i * 2 + 2)
                    units(1, i * 2 + (EARLY + 1), i * 2 + 1, next_rows)
            for j in range(NT - EARLY):
                units(j % 2, last * 2 + (EARLY + 2 + j))
                if j:
                    z_add(EARLY + j - 1, last * 2 + (EARLY + 1 + j))
            z_add(NT - 1, last * 2 + (NT + 1))

            for t in range(NT):
                dve.wait_ge(back_in[t // 2], 16 * 4)
                link(v.tensor_tensor(GA[0:NP, t, :], GA[0:NP, t, :], GB[0:NP, t, :], ALU.add))
                v.tensor_tensor(X[0:NP, t, :], X[0:NP, t, :], GA[0:NP, t, :], ALU.add).then_inc(sum_ready, 1)


def kernel(**inputs):
    import numpy as np
    import concourse.bacc as bacc
    from concourse.bass_utils import run_bass_kernel_spmd

    g = {k: np.asarray(v) for k, v in inputs.items()}
    edges = lambda e: e.reshape(NG * CPG, CHUNK).T
    arrays = {
        "x": g["x"], "src": edges(g["src"]), "dst": edges(g["dst"]),
        "W": g["L0_gnn_W"], "gnn_b": g["L0_gnn_b"],
        "WaT": g["L0_ffn_Wa"].transpose(0, 2, 1), "ba": g["L0_ffn_ba"],
        "WsT": g["L0_ffn_Ws"].transpose(0, 2, 1), "bs": g["L0_ffn_bs"],
        "WlT": g["L1_gnn_W_l"].T, "WrT": g["L1_gnn_W_r"].T, "b_l": g["L1_gnn_b_l"],
        "gamma": g["L1_gnn_gamma"], "beta": g["L1_gnn_beta"],
        "gate_w": g["L1_ffn_gate_w"], "gate_b": g["L1_ffn_gate_b"],
        "w1": np.concatenate([g["L1_ffn_expert_w1"], g["L1_ffn_shared_w1"][None]]),
        "b1": np.concatenate([g["L1_ffn_expert_b1"], g["L1_ffn_shared_b1"][None]]),
        "w2": np.concatenate([g["L1_ffn_expert_w2"], g["L1_ffn_shared_w2"][None]]),
        "b2": np.concatenate([g["L1_ffn_expert_b2"], g["L1_ffn_shared_b2"][None]]),
        "act": np.concatenate([g["L1_ffn_expert_act"], g["L1_ffn_shared_act"][None]]),
    }
    arrays = {k: np.ascontiguousarray(v) for k, v in arrays.items()}
    nc = bacc.Bacc("TRN2", target_bir_lowering=False, num_devices=1)
    aps = {k: nc.dram_tensor("in_" + k, v.shape, mybir.dt.from_np(v.dtype), kind="ExternalInput").ap()
           for k, v in arrays.items()}
    out = nc.dram_tensor("out", (N, D), F32, kind="ExternalOutput").ap()
    build(nc, aps, out)
    r = run_bass_kernel_spmd(nc, [{"in_" + k: v for k, v in arrays.items()}], core_ids=[0])
    return r.results[0]["out"]
```

```python
from contextlib import ExitStack

import concourse.bass as bass
from concourse import mybir

ALU = mybir.AluOpType
ACT = mybir.ActivationFunctionType
AX = mybir.AxisListType
F32 = mybir.dt.float32
F16 = mybir.dt.float16
F32R = mybir.dt.float32r
I32 = mybir.dt.int32

N = 1250
D = 512
E = 41250
NP = 125
NT = N // NP
FT = D // 128
LAYERS = 3
EPS = 1e-5
SPLITS = [(0, 500), (500, 500), (1000, 250)]

CHUNK = 125
CPG = 5
ACTJ = 2
NG = E // (CHUNK * CPG)
STEPS = 6
WIN = 24
KEYS = NT * WIN
CW = N + WIN
PASSES = (N + WIN - 1) // WIN

GE = 160
GU = 107
GR = GE - GU
FK = 5
IN1 = 108
OUT0, OUT1 = 128, 161
POS = 2
ROWS = POS * N
RC = 500
NRC = ROWS // RC
EXACT = 4096
APART = EXACT // (CHUNK * CPG)
MAGIC = 12582912.0

NEXP = 16
TOPK = 2
INTER = 384
H2 = 2 * INTER
BS = 128
NB = 36
O_W2 = FT * H2
O_B1 = O_W2 + (INTER // 128) * D
WBUF = O_B1 + H2
EARLY = 6
NWB = 3
ASSIGN = TOPK * NT


def build(nc, a, out):
    ctx = ExitStack()
    with ctx:
        def sb(name, shape, dt=F32):
            return ctx.enter_context(nc.sbuf_tensor(name, shape, dt))

        def sem(name):
            return ctx.enter_context(nc.semaphore(name))

        PS = ctx.enter_context(nc.psum_tensor("PS", [128, 8, 512], F32))

        ROWB = NT * D * 4
        WB_BYTES = FT * D * 4
        CTB = (NT * CW * 4 + 31) // 32 * 32
        BASE = (nc.sbuf_base + 31) // 32 * 32
        nc.alloc_sbuf_tensor("arena", [128, (BASE - nc.sbuf_base + 6 * ROWB + CTB + 2 * WB_BYTES) // 4], F32)

        def at(name, offset, shape, dt=F32):
            return nc.alloc_sbuf_tensor_at(name, shape, dt, offset=BASE + offset)

        R_X, R_XN, R_YH, R_YL, R_ZH, R_ZL, R_CT = [k * ROWB for k in range(7)]
        R_WH = R_CT + CTB
        R_WL = R_WH + WB_BYTES

        X = at("X", R_X, [128, NT, D])
        XN = at("XN", R_XN, [128, NT, D])
        WNEXT = at("WNEXT", R_XN, [128, 2, FT, D])
        val = at("val", R_XN + 2 * WB_BYTES, [128, 2, D])
        CTR = at("CTR", R_CT, [128, NT, CW], F32R)
        CT = at("CT", R_CT, [128, NT, CW])
        YH = at("YH", R_YH, [128, NT, D], F32R)
        YL = at("YL", R_YL, [128, NT, D], F32R)
        ZH = at("ZH", R_ZH, [128, FT, N], F32R)
        ZL = at("ZL", R_ZL, [128, FT, N], F32R)
        WH = at("WH", R_WH, [128, FT, D], F32R)
        WL = at("WL", R_WL, [128, FT, D], F32R)
        WRAW = at("WRAW", R_WL, [128, FT, D])
        ht = at("HT", R_XN, [128, FT, N])
        h1t = at("H1T", R_ZH, [GU, 2, 3, RC])
        h2t = at("H2T", R_YH, [GU, 2, 3, RC])
        y3 = at("Y3", R_YL, [4, ROWS])
        ft = at("FTT", R_ZL, [FK, ROWS])
        assert ROWS * 4 <= ROWB // 2 and FT * N * 4 <= ROWB
        FS = at("FS", R_ZL + ROWB // 2, [128, 2560])
        f32 = lambda m: m.bitcast(F32)
        ET = at("ET", R_YH, [128, 2 * NT * D])
        XT = at("XTF", R_ZH, [128, NT * D])
        xt = XT[:, 0:FT * N].rearrange("p (f n) -> p f n", f=FT)
        YF = at("YF", R_YH, [128, NT * D])
        RT = at("RT", R_YL, [128, NT * D])
        QX = at("QX", R_XN, [128, NT * D])
        WB = at("WB", R_ZL, [128, NWB * WBUF])
        R_SW = R_WL + WB_BYTES - WBUF * 4
        SW = at("SW", R_SW, [128, WBUF])
        assert R_ZL + NWB * WBUF * 4 <= R_SW and 2 * ROWB <= NWB * WBUF * 4
        GA, GB = [at(n, r, [128, NT, D]) for n, r in (("GA", R_ZL), ("GB", R_ZL + ROWB))]

        used = [0]

        def carve(width, dt=F32):
            w = width if dt is not F16 else (width + 1) // 2
            v = ET[:, used[0]:used[0] + w]
            used[0] += w
            assert used[0] <= 2 * NT * D
            return v if dt is F32 else v.bitcast(dt)

        NCH = NG * CPG
        src_i, dst_i = carve(NCH, I32), carve(NCH, I32)
        srcf, dstf, hi, lo, neglo, rel, key = [carve(NCH) for _ in range(7)]
        dist = carve(2 * ACTJ * 128, F16).rearrange("p (b j n) -> p b j n", b=2, j=ACTJ)
        oh_lo = carve(2 * CPG * 128, F16).rearrange("p (b j n) -> p b j n", b=2, j=CPG)
        ohk = [carve(CPG * KEYS, F16).rearrange("p (j n) -> p j n", j=CPG) for _ in range(2)]
        counts = carve(2 * KEYS).rearrange("p (b n) -> p b n", b=2)
        iota_k = carve(KEYS, F16)
        wbase = sb("wbase", [128, NG])
        wbase_i = sb("wbase_i", [1, NG], I32)
        bad = sb("bad", [128, 4])
        flag_i = sb("flag_i", [1, 1], I32)
        apart = carve(2 * NG).rearrange("p (a g) -> p a g", a=2)

        ident = sb("ident", [128, 128])
        ones = sb("ones", [128, 128])
        below = sb("below", [128, 128])
        stats = sb("stats", [128, NT, 3, 6])
        mv = sb("mv", [128, NT, 2])
        sd = sb("sd", [128, NT])
        rstd = sb("rstd", [128, NT])
        dis = sb("dis", [128, NT])
        rdis = sb("rdis", [128, NT])
        invc = sb("invc", [128, N])
        bias = sb("bias", [128, LAYERS, D])
        tmp = sb("tmp", [128, 2, D])

        load = {}

        def loaded(name):
            load[name] = sem("in_" + name)
            return load[name]

        for name in ("sw", "b2", "x", "edges", "w0", "w12", "wl", "wr", "gb", "ffn", "sage", "gate", "acts"):
            loaded(name)
        const_done = sem("const_done")
        step = sem("dve_step")
        var_ready, sd_ready, xn_ready = sem("var_ready"), sem("sd_ready"), sem("xn_ready")
        base_ready, base_read = sem("base_ready"), sem("base_read")
        onehot_ready, group_done = sem("onehot_ready"), sem("group_done")
        lo_ready, dist_ready, onehot_act = sem("lo_ready"), sem("dist_ready"), sem("onehot_act")
        windows_ready, counted, added = sem("windows_ready"), sem("counted"), sem("added")
        bad_ready, bad_sum, flag_ready = sem("bad_ready"), sem("bad_sum"), sem("flag_ready")
        slow_onehot, slow_group = sem("slow_onehot"), sem("slow_group")
        slow_step = sem("slow_step")
        counts_ready = sem("counts_ready")
        deg_ready, deg_copied, degcol_ready = sem("deg_ready"), sem("deg_copied"), sem("degcol_ready")
        y_ready = sem("y_ready")
        agg_ready = sem("agg_ready")
        zh_ready, zl_ready = sem("zh_ready"), sem("zl_ready")
        val_ready, yh_ready = sem("val_ready"), sem("yh_ready")
        wh_ready, w_ready = sem("wh_ready"), sem("w_ready")
        xn_added = sem("xn_added")
        lin_ready = sem("lin_ready")
        lin_read = sem("lin_read")
        pre_ready = sem("pre_ready")
        feat_ready, feat_t, ft_ready = sem("feat_ready"), sem("feat_t"), sem("ft_ready")
        f1_ready, f2_ready = sem("f1_ready"), sem("f2_ready")
        h1_act, h1_dve, h2_act, h2_dve = sem("h1_act"), sem("h1_dve"), sem("h2_act"), sem("h2_dve")
        ffn_zero = sem("ffn_zero")
        gate_ps, lgt_ready = sem("gate_ps"), sem("lgt_ready")
        f3_ready, y3_ready, y3_turned = sem("f3_ready"), sem("y3_ready"), sem("y3_turned")
        xtp_ready, xt_act, xt_dve = sem("xtp_ready"), sem("xt_act"), sem("xt_dve")
        sxt_ps, sxt_hi, sxt_ready = sem("sxt_ps"), sem("sxt_hi"), sem("sxt_ready")
        minus_ready = sem("minus_ready")
        mean_ps, mean_f32 = sem("mean_ps"), sem("mean_f32")
        mean_hi, mean_ready = sem("mean_hi"), sem("mean_ready")
        hr_ps, hr_ready = sem("hr_ps"), sem("hr_ready")
        hp_ready, h_ready = sem("hp_ready"), sem("h_ready")
        hstat, hsd, hscale, hn_ready = sem("hstat"), sem("hsd"), sem("hscale"), sem("hn_ready")
        back_ready, back_read = sem("back_ready"), sem("back_read")
        xn_stored = sem("xn_stored")
        logit_ready, zmax_ready, exp_ready = sem("logit_ready"), sem("zmax_ready"), sem("exp_ready")
        sel_ready, rank_ready = sem("sel_ready"), sem("rank_ready")
        slots_ready, table_ps, tables_ready = sem("slots_ready"), sem("table_ps"), sem("tables_ready")
        sp_ready, sp_exp, sp_one, sp_ln = sem("sp_ready"), sem("sp_exp"), sem("sp_one"), sem("sp_ln")
        gathered = [sem("gathered0"), sem("gathered1")]
        w1_in = [sem("w1_in0"), sem("w1_in1")]
        w2_in = [sem("w2_in0"), sem("w2_in1")]
        xt_ps, xgt_ready = sem("xt_ps"), sem("xgt_ready")
        hb_ready, clip_done, clip_g, gate_sig, t_gs, t_ready = (
            sem("hb_ready"), sem("clip_done"), sem("clip_g"), sem("gate_sig"), sem("t_gs"), sem("t_ready"))
        clip_u = sem("clip_u")
        tt_ps, tt_ready, y_done, yo_ready = sem("tt_ps"), sem("tt_ready"), sem("y_done"), sem("yo_ready")
        stored = [sem("stored0"), sem("stored1")]
        zeroed = sem("zeroed")
        z_added = sem("z_added")
        cw_ps, cwt_ready = sem("cw_ps"), sem("cwt_ready")
        back_in = [sem(f"back_in{g}") for g in range(NT // 2)]
        sum_ready, out_stored = sem("sum_ready"), sem("out_stored")

        xn_dram = nc.dram_tensor("xn_dram", [N, D], F32, kind="Internal")
        y_dram = nc.dram_tensor("y_dram", [NB * BS, D], F32, kind="Internal")

        w1f = FS[0:FK, 1040:1040 + 2 * GE]
        w2f = FS[0:GU, 1360:1360 + 6 * GE].rearrange("p (k n) -> p k n", k=3)
        b2f = sb("b2f", [GU, 3])
        w3f = sb("w3f", [GU, 3, 4])
        b3f = sb("b3f", [128, 2, 2])
        wj = sb("wj", [128, NEXP])
        cj = sb("cj", [128, NEXP])
        fk = FS[:, 0:NT * 64].rearrange("p (t g j) -> p t g j", t=NT, g=4)
        fm = FS[:, 960:1000].rearrange("p (t g) -> p t g", g=4)
        fg = FS[:, 1000:1040].rearrange("p (t g) -> p t g", g=4)
        feats = sb("feats", [128, POS, NT, FK])
        msk = sb("msk", [128, 8, NT])
        yv = FS[:, 640:640 + 80].rearrange("p (a t c) -> p a t c", a=2, c=2)
        res = FS[:, 720:720 + 40].rearrange("p (t c) -> p t c", c=2)
        oh2 = FS[:, 800:800 + 160].rearrange("p (t j) -> p t j", j=16)
        sage = sb("sage", [128, 3, FT])
        hst = sb("hst", [128, FT, 3, 6])
        hmv = sb("hmv", [128, FT, 2])
        hs = sb("hs", [128, 4, FT])
        gw = sb("gw", [128, FT, NEXP])
        gb = sb("gb", [NEXP, 1])
        acts = sb("acts", [128, NEXP + 1, 5])
        clampv = sb("clampv", [128, 5, NEXP + 1, 2])

        xg = YF[:, 0:2 * D].rearrange("p (b d) -> p b d", b=2)
        xgt = YF[:, 1024:1024 + 2 * D].rearrange("p (b f n) -> p b f n", b=2, f=FT)
        tt = YF[:, 2048:2048 + 2 * INTER].rearrange("p (b i n) -> p b i n", b=2, i=3)
        yo = YF[:, 2816:2816 + 2 * D].rearrange("p (b d) -> p b d", b=2)
        spare = bias[:, :, :].rearrange("p l n -> p (l n)")
        hb = [YF[:, 3840:3840 + H2], spare[:, 0:H2]]
        ss = [YF[:, 3840 + H2:3840 + H2 + INTER], spare[:, H2:H2 + INTER]]
        lgt = spare[0:NEXP, 0:N]
        tb = RT[:, 0:2 * INTER].rearrange("p (b i) -> p b i", b=2)
        b2m = invc[0:NEXP + 1, 0:D]
        cw = invc[:, D:D + NT * (NEXP + 1)].rearrange("p (t e) -> p t e", t=NT)
        rat = [2 * INTER]

        def rcarve(*dims):
            n = 1
            for d in dims:
                n *= d
            v = RT[:, rat[0]:rat[0] + n]
            rat[0] += n
            assert rat[0] <= NT * D, rat[0]
            names = "abcd"[:len(dims)]
            return v if len(dims) == 1 else v.rearrange(
                f"p ({' '.join(names)}) -> p {' '.join(names)}", **{c: d for c, d in zip(names, dims)})

        pr = rcarve(NT, NEXP)
        q = rcarve(NT, NEXP)
        oh = [rcarve(NT, NEXP), rcarve(NT, NEXP)]
        cum = rcarve(NT + 1, NEXP)
        posn = rcarve(NT, NEXP)
        rsmall = rcarve(10, NT)
        blkc = rcarve(6, NEXP)
        thr = rcarve(NT)
        le = rcarve(NEXP, NEXP)
        prod = rcarve(NEXP, NEXP)
        slotf = rcarve(TOPK, NT)
        slotp = rcarve(3, TOPK * NT)
        wsel = rcarve(TOPK, NT)
        nodef = rcarve(NT)
        ohb = rcarve(ASSIGN, 2, NB)
        cnt_e = rcarve(NB, NEXP)
        iota_b = rcarve(BS)
        ohr = QX[:, 0:ASSIGN * BS].rearrange("p (a n) -> p a n", a=ASSIGN)
        prodb = QX[:, 2560:2560 + NB * NB].rearrange("p (a b) -> p a b", a=NB)
        cwt = QX[0:NEXP + 1, 3860:3860 + N]
        slot_i = sb("slot_i", [128, TOPK, NT], I32)
        slot_b = sb("slot_b", [128, 2, TOPK * NT], I32)
        idx = sb("idx", [128, 2], I32)
        idx_ready = sem("idx_ready")
        tok = sb("tok", [128, NB], I32)
        wslot = sb("wslot", [128, NB])
        ebf = rcarve(5, NB)
        eb_i = sb("eb_i", [1, 4, NB], I32)

        block = ctx.enter_context(nc.Block())

        def counting(eng, s):
            seen = [0]

            def link(ins):
                seen[0] += 1
                ins.then_inc(s, 1)
                eng.wait_ge(s, seen[0])
            link.seen = seen
            return link

        CONSTS = 11
        SURE = TOPK * N // BS

        def last_pair(eng):
            return eng.value_load(eb_i[0:1, 3, 0:1], min_val=(SURE + 1) // 2 - 1, max_val=NB // 2 - 1)

        CWT_BANKS = ((6, 0), (7, 0), (4, 200))
        FFN_LOADS = 2 * (2 * (3 + 2 + 2) + 1)
        TILE = (GU, GU, 2 * GR)
        FS_SECOND = [(f, 0) for f in range(FT)] + [(f, s) for f in range(FT) for s in range(1, len(SPLITS))]
        SF = [(s, f) for s in range(len(SPLITS)) for f in range(FT)]

        @block.sync
        def _(sp):
            sp.dma_start(src_i[0:CHUNK, :], a["src"]).then_inc(load["edges"], 16)
            sp.dma_start(dst_i[0:CHUNK, :], a["dst"]).then_inc(load["edges"], 16)
            sp.dma_start(X[0:NP, :, :], a["x"].rearrange("(t p) d -> p t d", p=NP)).then_inc(load["x"], 16)
            sp.dma_start(WRAW[:, :, :], a["W"][0].rearrange("(f p) n -> p f n", p=128)).then_inc(load["w0"], 16)
            for l in range(LAYERS):
                if l:
                    sp.dma_start(WNEXT[:, l - 1, :, :], a["W"][l].rearrange("(f p) n -> p f n", p=128)
                                 ).then_inc(load["w12"], 16)
                sp.dma_start(bias[:, l, :], a["gnn_b"][l:l + 1, :].to_broadcast([128, D])).then_inc(load["gb"], 16)
            with nc.allow_non_contiguous_dma(reason="small tables"):
                for k, name in enumerate(("b_l", "gamma", "beta")):
                    sp.dma_start(sage[:, k, :], a[name].rearrange("(f p) -> p f", p=128)).then_inc(load["sage"], 16)
            sp.dma_start(gw[:, :, :], a["gate_w"].rearrange("(f p) n -> p f n", p=128)).then_inc(load["gate"], 16)
            with nc.allow_non_contiguous_dma(reason="small table"):
                sp.dma_start(gb[:, :], a["gate_b"].rearrange("(n o) -> n o", o=1)).then_inc(load["gate"], 16)
            sp.dma_start(acts[:, :, :], a["act"].rearrange("(o e) k -> o e k", o=1).to_broadcast([128, NEXP + 1, 5])
                         ).then_inc(load["acts"], 16)
            sp.wait_ge(const_done, 5)
            sp.dma_start(y_dram[SURE * BS:NB * BS, :].rearrange("(b p) d -> p b d", p=BS),
                         XT[:, 0:D].rearrange("p (o d) -> p o d", o=1).to_broadcast([128, NB - SURE, D])
                         ).then_inc(zeroed, 16)
            sp.wait_ge(lin_ready, NT * LAYERS)
            sp.wait_ge(ffn_zero, 2)
            for n, (w, b) in enumerate((("WaT", "ba"), ("WsT", "bs"))):
                places = ((n, slice(0, GU), slice(0, GU), slice(n * GU, (n + 1) * GU)),
                          (2, slice(n * GR, (n + 1) * GR), slice(GU, GE), slice(2 * GU + n * GR, 2 * GU + (n + 1) * GR)))
                for tile, rows, there, cols in places:
                    sp.dma_start(w1f[0:2, cols], a[w][0, 0:2, there]).then_inc(load["ffn"], 16)
                    sp.dma_start(w1f[2:4, cols], a[w][0, 35:37, there]).then_inc(load["ffn"], 16)
                    sp.dma_start(w1f[4:5, cols], a[b][0:1, there]).then_inc(load["ffn"], 16)
                    for _, _, out_there, out_cols in places:
                        sp.dma_start(w2f[rows, tile, out_cols], a[w][1, there, out_there]).then_inc(load["ffn"], 16)
                    with nc.allow_non_contiguous_dma(reason="small tables"):
                        sp.dma_start(b2f[rows, tile:tile + 1], a[b][1, there].rearrange("(p o) -> p o", o=1)
                                     ).then_inc(load["ffn"], 16)
                        sp.dma_start(w3f[rows, tile, 2 * n:2 * n + 2], a[w][2, there, 100:102]).then_inc(load["ffn"], 16)
                sp.dma_start(b3f[:, n, :], a[b][2:3, 100:102].to_broadcast([128, 2])).then_inc(load["ffn"], 16)
            sp.dma_start(WRAW[:, :, :], a["WrT"].rearrange("(f p) n -> p f n", p=128)).then_inc(load["wr"], 16)
            sp.wait_ge(hr_ps, FT * len(SPLITS))
            sp.dma_start(WRAW[:, :, :], a["WlT"].rearrange("(f p) n -> p f n", p=128)).then_inc(load["wl"], 16)
            sp.wait_ge(mean_ready, FT * len(SPLITS))
            sp.dma_start(b2m, a["b2"]).then_inc(load["b2"], 16)
            sp.wait_ge(hp_ready, FT * len(SPLITS))
            sp.dma_start(SW[:, 0:O_W2].rearrange("p (f n) -> p f n", f=FT),
                         a["w1"][NEXP].rearrange("(f p) n -> p f n", p=128)).then_inc(load["sw"], 16)
            sp.dma_start(SW[:, O_W2:O_B1].rearrange("p (f n) -> p f n", f=INTER // 128),
                         a["w2"][NEXP].rearrange("(f p) n -> p f n", p=128)).then_inc(load["sw"], 16)
            sp.dma_start(SW[:, O_B1:WBUF], a["b1"][NEXP:NEXP + 1, :].to_broadcast([128, H2])).then_inc(load["sw"], 16)
            sp.wait_ge(xn_ready, 3 * NT)
            sp.dma_start(xn_dram[:, :].rearrange("(t p) d -> p t d", p=NP), XN[0:NP, :, :]).then_inc(xn_stored, 16)

            sp.wait_ge(tables_ready, 1)

            def load_weights(i, k, b):
                e = sp.value_load(eb_i[0:1, 0, bass.ds(b, 1)], min_val=0, max_val=NEXP)
                off = sp.value_load(eb_i[0:1, 1, bass.ds(b, 1)], min_val=0, max_val=(NWB - 1) * WBUF)
                new = sp.value_load(eb_i[0:1, 2, bass.ds(b, 1)], min_val=0, max_val=1)
                if isinstance(b, int):
                    ahead, landed1, landed2 = b + EARLY - NWB + 1, 32 * i, 16 * i
                else:
                    ahead, landed1, landed2 = sp.to_reg(b + (EARLY - NWB + 1)), sp.to_reg(i * 32), sp.to_reg(i * 16)
                sp.wait_ge(tables_ready, 1)
                if not (isinstance(b, int) and b < 2):
                    sp.wait_ge(w1_in[k], landed1)
                    sp.wait_ge(w2_in[k], landed2)
                if not (isinstance(b, int) and b < NWB):
                    sp.wait_ge(y_done, ahead)
                w1v = a["w1"][bass.ds(e, 1), :, :].rearrange("o (f p) n -> p (o f) n", p=128)
                sp.dma_start(WB[:, bass.ds(off, FT * H2)].rearrange("p (f n) -> p f n", f=FT), w1v,
                             cond=new).then_inc(w1_in[k], 16)
                sp.dma_start(WB[:, bass.ds(off + O_B1, H2)], a["b1"][bass.ds(e, 1), :].to_broadcast([128, H2]),
                             cond=new).then_inc(w1_in[k], 16)
                w2v = a["w2"][bass.ds(e, 1), :, :].rearrange("o (f p) n -> p (o f) n", p=128)
                sp.dma_start(WB[:, bass.ds(off + O_W2, (INTER // 128) * D)].rearrange("p (f n) -> p f n", f=INTER // 128),
                             w2v, cond=new).then_inc(w2_in[k], 16)

            last = last_pair(sp)
            for b in range(4):
                load_weights(b // 2, b % 2, b)
            with sp.Fori(2, NB // 2) as i:
                with sp.If(i < last + 1):
                    for k in range(2):
                        load_weights(i, k, i * 2 + k)
            for t in range(NT):
                sp.wait_ge(sum_ready, t + 1)
                sp.dma_start(out[t * NP:(t + 1) * NP, :], X[0:NP, t, :]).then_inc(out_stored, 16)
            sp.wait_ge(out_stored, 16 * NT)

        @block.gpsimd
        def _(pool):
            pool.memset(ident[:, :], 0.0).then_inc(const_done, 1)
            pool.memset(ones[:, :], 1.0).then_inc(const_done, 1)
            pool.memset(below[:, :], 1.0).then_inc(const_done, 1)
            pool.iota(iota_k[:, :], pattern=[[1, KEYS]], base=0, channel_multiplier=0,
                      allow_small_or_imprecise_dtypes=True).then_inc(const_done, 1)
            pool.memset(XT[:, 0:D], 0.0).then_inc(const_done, 1)
            pool.iota(wj[:, :], pattern=[[-1, NEXP]], base=16, channel_multiplier=0,
                      allow_small_or_imprecise_dtypes=True).then_inc(const_done, 1)
            pool.iota(cj[:, :], pattern=[[1, NEXP]], base=0, channel_multiplier=0,
                      allow_small_or_imprecise_dtypes=True).then_inc(const_done, 1)
            pool.wait_ge(const_done, 7)
            pool.affine_select(out=ident[:, :], in_=ident[:, :], compare_op=ALU.not_equal, fill=1.0, base=0,
                               pattern=[[-1, 128]], channel_multiplier=1).then_inc(const_done, 1)
            pool.affine_select(out=below[:, :], in_=below[:, :], compare_op=ALU.is_gt, fill=0.0, base=0,
                               pattern=[[1, 128]], channel_multiplier=-1).then_inc(const_done, 1)
            pool.memset(feats[:, :, :, :], 1.0).then_inc(const_done, 1)
            pool.memset(f32(CTR[:, :, :]), 0.0).then_inc(const_done, 1)

            pool.wait_ge(windows_ready, 1)
            pool.wait_ge(const_done, CONSTS)

            def add_counts(k, g):
                w0 = pool.value_load(wbase_i[0:1, bass.ds(g, 1)], min_val=0, max_val=N - 1)
                pool.wait_ge(counted, g + 1)
                if not isinstance(g, int) or g:
                    pool.wait_ge(added, g)
                dest = CTR[0:NP, :, bass.ds(w0, WIN)]
                pool.tensor_tensor(dest, counts[0:NP, k, :].rearrange("p (t w) -> p t w", t=NT), f32(dest), ALU.add
                                   ).then_inc(added, 1)

            add_counts(0, 0)
            add_counts(1, 1)
            with pool.Fori(1, NG // 2) as i:
                for k in range(2):
                    add_counts(k, i * 2 + k)

            pool.wait_ge(lin_ready, NT * LAYERS)
            pool.memset(w2f[:, :, :], 0.0).then_inc(ffn_zero, 1)
            pool.memset(w3f[:, :, :], 0.0).then_inc(ffn_zero, 1)
            pool.wait_ge(hp_ready, FT * len(SPLITS))
            pool.iota(thr[:, :], pattern=[[BS, NT]], base=0, channel_multiplier=0,
                      allow_small_or_imprecise_dtypes=True).then_inc(const_done, 1)
            pool.memset(le[:, :, :], 1.0).then_inc(const_done, 1)
            pool.iota(nodef[:, :], pattern=[[NP, NT]], base=0, channel_multiplier=1,
                      allow_small_or_imprecise_dtypes=True).then_inc(const_done, 1)
            pool.memset(cum[:, 0, :], 0.0).then_inc(const_done, 1)
            pool.iota(cnt_e[:, :, :], pattern=[[1, NB], [0, NEXP]], base=0, channel_multiplier=0,
                      allow_small_or_imprecise_dtypes=True).then_inc(const_done, 1)
            pool.wait_ge(const_done, CONSTS + 5)
            pool.affine_select(out=le[:, :, :], in_=le[:, :, :], compare_op=ALU.is_ge, fill=0.0, base=0,
                               pattern=[[1, NEXP], [-1, NEXP]], channel_multiplier=0).then_inc(const_done, 1)
            pool.wait_ge(logit_ready, 1)
            pool.wait_ge(xn_stored, 16)
            pool.iota(iota_b, pattern=[[1, BS]], base=0, channel_multiplier=0,
                      allow_small_or_imprecise_dtypes=True).then_inc(const_done, 1)
            pool.memset(prodb[0:1, :, :], 1.0).then_inc(const_done, 1)
            pool.wait_ge(const_done, CONSTS + 8)
            pool.affine_select(out=prodb[0:1, :, :], in_=prodb[0:1, :, :], compare_op=ALU.is_ge, fill=0.0, base=0,
                               pattern=[[1, NB], [-1, NB]], channel_multiplier=0).then_inc(const_done, 1)

            pool.wait_ge(tables_ready, 1)

            def gather(i, k, b):
                if not (isinstance(b, int) and b < 2):
                    pool.wait_ge(xt_ps, b - 1)
                turn = b + 1 if isinstance(b, int) else pool.to_reg(b + 1)
                pool.tensor_copy(idx[:, k:k + 1], tok[:, bass.ds(b, 1)]).then_inc(idx_ready, 1)
                pool.wait_ge(xn_stored, 16)
                pool.wait_ge(idx_ready, turn)
                pool.indirect_dma_start(xg[:, k, :], None, xn_dram[:, :],
                                        bass.IndirectOffsetOnAxis(idx[:, k:k + 1], 0)
                                        ).then_inc(gathered[k], 16)

            for b in range(2):
                gather(0, b, b)
            last = last_pair(pool)
            with pool.Fori(1, NB // 2) as i:
                with pool.If(i < last + 1):
                    for k in range(2):
                        gather(i, k, i * 2 + k)
            all_stored = pool.to_reg(last * 16 + 16)
            pool.wait_ge(tables_ready, 1)
            pool.wait_ge(stored[0], all_stored)
            pool.wait_ge(stored[1], all_stored)
            for t in range(NT):
                for k, dest in enumerate((GA, GB)):
                    pool.indirect_dma_start(dest[0:NP, t, :], None, y_dram[:, :],
                                            bass.IndirectOffsetOnAxis(slot_i[0:NP, k, t:t + 1], 0)
                                            ).then_inc(back_in[t // 2], 16)
            for g in range(NT // 2):
                pool.wait_ge(back_in[g], 16 * 4)

        @block.scalar
        def _(act):
            def sqrt_of_var(k):
                act.wait_ge(var_ready, k + 1)
                nc.scalar.activation(sd[0:NP, :], mv[0:NP, :, 1], ACT.Sqrt).then_inc(sd_ready, 1)

            act.wait_ge(lo_ready, 1)
            act.wait_ge(const_done, 4)

            def onehots_act(i, k, b):
                for j in range(ACTJ):
                    nc.scalar.activation(dist[0:CHUNK, k, j, 0:NP], iota_k[0:CHUNK, 0:NP], ACT.Abs,
                                         bias=neglo[0:CHUNK, bass.ds(b * CPG + j, 1)]).then_inc(dist_ready, 1)
                act.wait_ge(dist_ready, b * ACTJ + ACTJ)
                ins = nc.scalar.activation(oh_lo[0:CHUNK, k, 0:ACTJ, 0:NP], dist[0:CHUNK, k, :, 0:NP], ACT.Relu,
                                           scale=-1.0, bias=ones[0:CHUNK, 0:1])
                ins.then_inc(onehot_act, 1)

            def counts_copy(k, b):
                act.wait_ge(group_done, b + 1)
                if not (isinstance(b, int) and b < 2):
                    act.wait_ge(added, b - 1)
                nc.scalar.copy(counts[0:NP, k, :], PS[0:NP, k, 0:KEYS]).then_inc(counted, 1)

            onehots_act(0, 0, 0)
            onehots_act(0, 1, 1)
            for g in range(STEPS):
                counts_copy(g % 2, g)
                onehots_act(0, g % 2, g + 2)
            with act.Fori(1, NG // STEPS - 1) as i:
                for g in range(STEPS):
                    counts_copy(g % 2, i * STEPS + g)
                    onehots_act(i, g % 2, i * STEPS + (g + 2))
            for g in range(NG - STEPS, NG):
                counts_copy(g % 2, g)
                if g + 2 < NG:
                    onehots_act(0, g % 2, g + 2)
            act.wait_ge(sp_ready, 1)
            nc.scalar.activation(clampv[:, 2, :, :], clampv[:, 1, :, :], ACT.Exp).then_inc(sp_exp, 1)
            act.wait_ge(sp_one, 1)
            nc.scalar.activation(clampv[:, 4, :, :], clampv[:, 3, :, :], ACT.Ln).then_inc(sp_ln, 1)
            sqrt_of_var(0)
            act.wait_ge(degcol_ready, 1)
            nc.scalar.activation(dis[0:NP, :], PS[0:NP, 3, 0:NT], ACT.Sqrt).then_inc(sd_ready, 1)

            def split_weight(k, raw, name, count):
                act.wait_ge(load[name], count)
                nc.scalar.copy(WH[:, :, :], raw).then_inc(wh_ready, 1)

            act.wait_ge(zeroed, 16)
            act.wait_ge(deg_ready, len(SPLITS))
            split_weight(0, WRAW[:, :, :], "w0", 16)
            act.wait_ge(load["w12"], 32)
            for t in range(NT):
                act.wait_ge(val_ready, t + 1)
                nc.scalar.copy(YH[0:NP, t, :], val[0:NP, t % 2, :]).then_inc(yh_ready, 1)

            n = 0
            for l in range(LAYERS):
                def relu_tiles(tiles):
                    for t in tiles:
                        m = (l + 1) * NT + t
                        act.wait_ge(pre_ready, l * NT + t + 1)
                        if t < 2:
                            act.wait_ge(agg_ready, FT * len(SPLITS) * (l + 1))
                        act.wait_ge(y_ready, m - 1)
                        nc.scalar.activation(val[0:NP, t % 2, :], tmp[0:NP, t % 2, :], ACT.Relu,
                                             scale=dis[0:NP, t:t + 1]).then_inc(val_ready, 1)
                        act.wait_ge(val_ready, m + 1)
                        nc.scalar.copy(YH[0:NP, t, :], val[0:NP, t % 2, :]).then_inc(yh_ready, 1)

                if l:
                    act.wait_ge(lin_ready, NT * l)
                    split_weight(l, WNEXT[:, l - 1, :, :], "w12", 32)
                for s, (c0, w) in enumerate(SPLITS):
                    for f in range(FT):
                        act.wait_ge(agg_ready, n + 1)
                        if s == 0 and l:
                            act.wait_ge(lin_ready, NT * l)
                        nc.scalar.copy(ZH[:, f, c0:c0 + w], PS[:, n % 6, 0:w]).then_inc(zh_ready, 1)
                        n += 1
                if l < LAYERS - 1:
                    relu_tiles(range(NT))
            sqrt_of_var(1)

            act.wait_ge(load["ffn"], 16 * FFN_LOADS)
            def h1_copy(c):
                for j in (0, 2):
                    act.wait_ge(f1_ready, 3 * c + j + 1)
                    if c >= 2:
                        act.wait_ge(f2_ready, 3 * (c - 1))
                    n = TILE[j]
                    nc.scalar.activation(h1t[0:n, c % 2, j, :], PS[0:n, j, 0:RC], ACT.Relu).then_inc(h1_act, 1)

            def h2_copy(c):
                act.wait_ge(f2_ready, 3 * c + 1)
                if c >= 2:
                    act.wait_ge(f3_ready, c - 1)
                nc.scalar.activation(h2t[:, c % 2, 0, :], PS[0:GU, 3, 0:RC], ACT.Relu, bias=b2f[:, 0:1]
                                     ).then_inc(h2_act, 1)

            def y3_copy(c):
                act.wait_ge(f3_ready, c + 1)
                nc.scalar.copy(y3[:, c * RC:(c + 1) * RC], PS[0:4, 7, 0:RC]).then_inc(y3_ready, 1)

            for c in range(NRC):
                act.wait_ge(feat_t, c + 1)
                nc.scalar.copy(ft[:, c * RC:(c + 1) * RC], PS[0:FK, c, 0:RC]).then_inc(ft_ready, 1)
            h1_copy(0)
            for c in range(NRC):
                if c + 1 < NRC:
                    h1_copy(c + 1)
                h2_copy(c)
                if c >= 1:
                    y3_copy(c - 1)
                if c == 2:
                    split_weight(3, WRAW[:, :, :], "wr", 16)
            y3_copy(NRC - 1)
            sqrt_of_var(2)
            for n, (s, f) in enumerate(SF):
                c0, w = SPLITS[s]
                act.wait_ge(sxt_ps, n + 1)
                nc.scalar.copy(ZH[:, f, c0:c0 + w], PS[:, n % 4, 0:w]).then_inc(sxt_hi, 1)
            for t in range(NT):
                act.wait_ge(xn_ready, NT + t + 1)
                nc.scalar.copy(YH[0:NP, t, :], XN[0:NP, t, :]).then_inc(yh_ready, 1)
            act.wait_ge(y_ready, NT * (LAYERS + 1))
            act.wait_ge(xn_added, NT)
            for n, (s, f) in enumerate(SF):
                c0, w = SPLITS[s]
                act.wait_ge(hr_ps, n + 1)
                nc.scalar.activation(ht[:, f, c0:c0 + w], PS[:, 4 + n % 4, 0:w], ACT.Identity,
                                     bias=sage[:, 0, f:f + 1]).then_inc(hr_ready, 1)
            split_weight(4, WRAW[:, :, :], "wl", 16)
            for n, (s, f) in enumerate(SF):
                c0, w = SPLITS[s]
                act.wait_ge(mean_f32, n + 1)
                nc.scalar.copy(ZH[:, f, c0:c0 + w], tmp[:, n % 2, 0:w]).then_inc(mean_hi, 1)
            for f in range(FT):
                act.wait_ge(hstat, f + 1)
                nc.scalar.activation(hs[:, 1, f:f + 1], hs[:, 0, f:f + 1], ACT.Sqrt).then_inc(hsd, 1)
                act.wait_ge(hscale, f + 1)
                nc.scalar.activation(ht[:, f, :], ht[:, f, :], ACT.Relu, scale=hs[:, 2, f:f + 1],
                                     bias=hs[:, 3, f:f + 1]).then_inc(hn_ready, 1)
            sqrt_of_var(3)
            for n, (s, f) in enumerate(SF):
                c0, w = SPLITS[s]
                if f % 2 == 0:
                    act.wait_ge(xtp_ready, n + 1)
                    nc.scalar.copy(xt[:, f, c0:c0 + w], PS[:, n % 4, 0:w]).then_inc(xt_act, 1)
            for s, (c0, w) in enumerate(SPLITS):
                act.wait_ge(gate_ps, s + 1)
                nc.scalar.activation(lgt[:, c0:c0 + w], PS[0:NEXP, 5 + s, 0:w], ACT.Identity, bias=gb[:, 0:1]
                                     ).then_inc(lgt_ready, 1)
            act.wait_ge(zmax_ready, 1)
            nc.scalar.activation(pr[0:NP, :, :], q[0:NP, :, :], ACT.Exp).then_inc(exp_ready, 1)

            act.wait_ge(cw_ps, 1)
            act.wait_ge(xn_stored, 16)
            for s, (c0, w) in enumerate(SPLITS):
                ins = nc.scalar.copy(cwt[:, c0:c0 + w], PS[0:NEXP + 1, CWT_BANKS[s][0], CWT_BANKS[s][1]:CWT_BANKS[s][1] + w])
            ins.then_inc(cwt_ready, 1)

            def turn_t(k, p, rows=128):
                act.wait_ge(tt_ps, p + 1)
                nc.scalar.copy(tt[:, k, :, 0:rows], PS[:, 5, 0:INTER].rearrange("p (i n) -> p i n", i=3)[:, :, 0:rows]
                               ).then_inc(tt_ready, 1)

            def sigmoid(k, p, b=None):
                shared = b is None
                if not shared:
                    e = act.value_load(eb_i[0:1, 0, bass.ds(b, 1)], min_val=0, max_val=NEXP - 1)
                    alpha, rows = acts[:, bass.ds(e, 1), 0], 128
                else:
                    alpha, rows = acts[0:NP, NEXP:NEXP + 1, 0], NP
                act.wait_ge(clip_g, p + 1)
                if not (isinstance(p, int) and p < 2):
                    act.wait_ge(t_ready, p - 1)
                nc.scalar.activation(ss[k][0:rows], hb[k][0:rows, 0:H2:2], ACT.Sigmoid, scale=alpha).then_inc(gate_sig, 1)

            def store(i, k, b):
                act.wait_ge(yo_ready, b + 1)
                act.dma_start(y_dram[bass.ds(b * BS, BS), :], yo[:, k, :]).then_inc(stored[k], 16)

            def result(i, k, b, first=False):
                act.wait_ge(y_done, b + (EARLY + 1))
                if not first:
                    act.wait_ge(stored[k], i * 16)
                nc.scalar.activation(yo[:, k, :], PS[:, 6 + k, :], ACT.Copy,
                                     scale=wslot[:, bass.ds(b, 1)]).then_inc(yo_ready, 1)

            sigmoid(0, 0)
            for p in range(1, EARLY):
                turn_t((p - 1) % 2, p - 1, NP)
                sigmoid(p % 2, p)
            act.wait_ge(tables_ready, 1)
            last = last_pair(act)
            turn_t(1, EARLY - 1, NP)
            sigmoid(0, EARLY, 0)
            turn_t(0, EARLY)
            sigmoid(1, EARLY + 1, 1)
            result(0, 0, 0, first=True)
            with act.Fori(1, NB // 2) as i:
                with act.If(i < last + 1):
                    store(i, 0, i * 2 - 2)
                    turn_t(1, i * 2 + (EARLY - 1))
                    sigmoid(0, i * 2 + EARLY, i * 2)
                    with act.If(i < 2):
                        result(0, 1, 1, first=True)
                    with act.If(i > 1):
                        result(i - 1, 1, i * 2 - 1)
                    store(i, 1, i * 2 - 1)
                    turn_t(0, i * 2 + EARLY)
                    sigmoid(1, i * 2 + (EARLY + 1), i * 2 + 1)
                    result(i, 0, i * 2)
            store(0, 0, last * 2)
            turn_t(1, last * 2 + (EARLY + 1))
            sigmoid(0, last * 2 + (EARLY + 2))
            result(last, 1, last * 2 + 1)
            store(0, 1, last * 2 + 1)
            for j in range(NT - EARLY):
                turn_t(j % 2, last * 2 + (EARLY + 2 + j), NP)
                if j + 1 < NT - EARLY:
                    sigmoid((j + 1) % 2, last * 2 + (EARLY + j + 3))

        @block.tensor
        def _(pe):
            pe.wait_ge(const_done, 4)
            pe.wait_ge(base_ready, 1)
            nc.tensor.matmul(PS[:, 7, 0:NG], ones[0:1, :], dstf[0:1, 0:NCH:CPG],
                             start=True, stop=True).then_inc(base_read, 1)
            pe.wait_ge(bad_ready, 1)
            nc.tensor.matmul(PS[:, 6, 0:1], ones[0:NP, :], bad[0:NP, 0:1], start=True, stop=True).then_inc(bad_sum, 1)

            def group(k, eng_lo, eng_key):
                for j in range(CPG):
                    mm = nc.tensor.matmul(PS[0:NP, k, 0:KEYS], eng_lo[0:CHUNK, k, j, 0:NP], eng_key[0:CHUNK, j, :],
                                          start=(j == 0), stop=(j == CPG - 1))
                return mm

            for g in range(STEPS):
                pe.wait_ge(onehot_act, g + 1)
                pe.wait_ge(onehot_ready, g + 1)
                if g >= 2:
                    pe.wait_ge(counted, g - 1)
                group(g % 2, oh_lo, ohk[g % 2]).then_inc(group_done, 1)
            with pe.Fori(1, NG // STEPS) as i:
                for g in range(STEPS):
                    pe.wait_ge(onehot_act, i * STEPS + (g + 1))
                    pe.wait_ge(onehot_ready, i * STEPS + (g + 1))
                    pe.wait_ge(counted, i * STEPS + (g - 1))
                    group(g % 2, oh_lo, ohk[g % 2]).then_inc(group_done, 1)

            pe.wait_ge(const_done, CONSTS)
            pe.wait_ge(flag_ready, 1)
            slow = pe.value_load(flag_i[0:1, 0:1], min_val=0, max_val=1)
            with pe.If(slow > 0):
                with pe.Fori(0, PASSES) as w:
                    with pe.Fori(0, NG) as g:
                        pe.wait_ge(slow_onehot, w * NG + g + 1)
                        group(0, oh_lo, ohk[0]).then_inc(slow_group, 1)

            pe.wait_ge(counts_ready, 1)

            def degrees(unit, table):
                for s, (c0, w) in enumerate(SPLITS):
                    for t in range(NT):
                        mm = nc.tensor.matmul(PS[:, s, 0:w], unit, table[0:NP, t, c0:c0 + w],
                                              start=(t == 0), stop=(t == NT - 1))
                    mm.then_inc(deg_ready, 1)

            with pe.If(slow < 1):
                degrees(WH[0:NP, 0, 0:128], CTR)
            with pe.If(slow > 0):
                degrees(ones[0:NP, :], CT)
            pe.wait_ge(deg_copied, 1)
            for t in range(NT):
                mm = nc.tensor.matmul(PS[0:NP, 3, t:t + 1], invc[0:1, t * NP:(t + 1) * NP], ones[0:1, 0:1],
                                      start=True, stop=True)
            mm.then_inc(degcol_ready, 1)

            def aggregate(dest, f, c0, w, exact, tile_wait=None):
                for t in range(NT):
                    if tile_wait is not None:
                        tile_wait(t)
                    for h, part in enumerate((YH, YL)):
                        lhs, rhs = part[0:NP, t, f * 128:(f + 1) * 128], CTR[0:NP, t, c0:c0 + w]
                        if not exact:
                            lhs, rhs = f32(lhs), CT[0:NP, t, c0:c0 + w]
                        mm = nc.tensor.matmul(dest, lhs, rhs, start=(t == 0 and h == 0),
                                              stop=(t == NT - 1 and h == 1))
                return mm

            PRODUCTS = ((ZH, WH), (ZH, WL), (ZL, WH))

            def gcn(exact):
                n_agg = 0
                for l in range(LAYERS):
                    for s, (c0, w) in enumerate(SPLITS):
                        for f in range(FT):
                            if n_agg >= 6:
                                pe.wait_ge(zl_ready, n_agg - 5)
                            tile_wait = None
                            if s == 0 and f == 0:
                                tile_wait = lambda t: pe.wait_ge(y_ready, NT * l + t + 1)
                            aggregate(PS[:, n_agg % 6, 0:w], f, c0, w, exact, tile_wait).then_inc(agg_ready, 1)
                            n_agg += 1
                    pe.wait_ge(w_ready, l + 1)
                    for t in range(NT):
                        n = l * NT + t
                        pe.wait_ge(zl_ready, n_agg - FT * (2 - min(t // 4, 2)))
                        if n >= 2 + NT * (LAYERS - 1):
                            pe.wait_ge(lin_read, n - 1 - NT * (LAYERS - 1))
                        elif n >= 2:
                            pe.wait_ge(pre_ready, n - 1)
                        for f in range(FT):
                            for h, (z, w) in enumerate(PRODUCTS):
                                mm = nc.tensor.matmul(PS[0:NP, 6 + n % 2, :], z[:, f, t * NP:(t + 1) * NP], w[:, f, :],
                                                      start=(f == 0 and h == 0), stop=(f == FT - 1 and h == 2))
                        mm.then_inc(lin_ready, 1)

            with pe.If(slow < 1):
                gcn(True)
            with pe.If(slow > 0):
                gcn(False)

            pe.wait_ge(feat_ready, 1)
            pe.wait_ge(load["ffn"], 16 * FFN_LOADS)
            for pos in range(POS):
                for t in range(NT):
                    i = pos * NT + t
                    mm = nc.tensor.transpose(PS[0:FK, i // 4, (i % 4) * NP:(i % 4 + 1) * NP], feats[0:NP, pos, t, :],
                                             ident[0:NP, 0:NP])
                    if i % 4 == 3:
                        mm.then_inc(feat_t, 1)
            def first(c):
                pe.wait_ge(ft_ready, NRC if c else 1)
                for j in range(3):
                    if c == 0:
                        pe.wait_ge(ft_ready, j + 1)
                    if c >= 1:
                        pe.wait_ge(*((h1_dve, c) if j == 1 else (h1_act, 2 * c - 1 + j // 2)))
                    nc.tensor.matmul(PS[0:TILE[j], j, 0:RC], w1f[:, j * GU:j * GU + TILE[j]],
                                     ft[:, c * RC:(c + 1) * RC], start=True, stop=True).then_inc(f1_ready, 1)

            def second(c):
                pe.wait_ge(h1_act, 2 * c + 2)
                pe.wait_ge(h1_dve, c + 1)
                for j, tiles in enumerate(((0, 2), (1, 2), (0, 1, 2))):
                    if c >= 1:
                        pe.wait_ge(*((h2_act, c) if j == 0 else (h2_dve, 2 * c - 2 + j)))
                    for k in tiles:
                        mm = nc.tensor.matmul(PS[0:TILE[j], 3 + j, 0:RC], w2f[0:TILE[k], k, j * GU:j * GU + TILE[j]],
                                              h1t[0:TILE[k], c % 2, k, :], start=(k == tiles[0]), stop=(k == 2))
                    mm.then_inc(f2_ready, 1)

            def third(c):
                pe.wait_ge(h2_act, c + 1)
                pe.wait_ge(h2_dve, 2 * c + 2)
                if c >= 1:
                    pe.wait_ge(y3_ready, c)
                for k in range(3):
                    mm = nc.tensor.matmul(PS[0:4, 7, 0:RC], w3f[0:TILE[k], k, :], h2t[0:TILE[k], c % 2, k, :],
                                          start=(k == 0), stop=(k == 2))
                mm.then_inc(f3_ready, 1)

            for c in range(NRC + 2):
                if c < NRC:
                    first(c)
                if 1 <= c <= NRC:
                    second(c - 1)
                if c >= 2:
                    third(c - 2)
            pe.wait_ge(y3_ready, NRC)
            for t in range(POS * NT):
                mm = nc.tensor.transpose(PS[0:NP, 6, 4 * t:4 * t + 4], y3[:, t * NP:(t + 1) * NP], ident[0:4, 0:4])
            mm.then_inc(y3_turned, 1)

            pe.wait_ge(f3_ready, NRC)
            for n, (s, f) in enumerate(SF):
                c0, w = SPLITS[s]
                if f == 0:
                    pe.wait_ge(xn_ready, NT + (c0 + w) // NP)
                if n >= 4:
                    pe.wait_ge(sxt_ready, n - 3)
                for j in range(w // NP):
                    mm = nc.tensor.transpose(PS[:, n % 4, j * NP:(j + 1) * NP],
                                             XN[0:NP, c0 // NP + j, f * 128:(f + 1) * 128], ident[0:NP, 0:NP])
                mm.then_inc(sxt_ps, 1)

            def sage_linear(order, wait, signal, inputs):
                for n, (fo, s) in enumerate(order):
                    c0, w = SPLITS[s]
                    pe.wait_ge(inputs, FT * (s + 1))
                    if n >= 4:
                        pe.wait_ge(wait, n - 3)
                    for f in range(FT):
                        for h, (z, wt) in enumerate(PRODUCTS):
                            mm = nc.tensor.matmul(PS[:, 4 + n % 4, 0:w], wt[:, f, fo * 128:(fo + 1) * 128],
                                                  z[:, f, c0:c0 + w], start=(f == 0 and h == 0),
                                                  stop=(f == FT - 1 and h == 2))
                    mm.then_inc(signal, 1)

            pe.wait_ge(w_ready, LAYERS + 1)
            sage_linear([(f, s) for s, f in SF], hr_ready, hr_ps, sxt_ready)
            pe.wait_ge(minus_ready, 1)
            pe.wait_ge(y_ready, NT * (LAYERS + 1))

            def sage_sums(exact):
                for n, (s, f) in enumerate(SF):
                    c0, w = SPLITS[s]
                    if n >= 4:
                        pe.wait_ge(mean_f32, n - 3)
                    aggregate(PS[:, n % 4, 0:w], f, c0, w, exact).then_inc(mean_ps, 1)

            with pe.If(slow < 1):
                sage_sums(True)
            with pe.If(slow > 0):
                sage_sums(False)
            pe.wait_ge(hr_ready, FT * len(SPLITS))
            pe.wait_ge(w_ready, LAYERS + 2)
            sage_linear(FS_SECOND, h_ready, hp_ready, mean_ready)
            pe.wait_ge(hn_ready, FT)
            for t in range(NT):
                if t >= 2:
                    pe.wait_ge(back_read, t - 1)
                for f in range(FT):
                    mm = nc.tensor.transpose(PS[0:NP, 2 + t % 2, f * 128:(f + 1) * 128], ht[:, f, t * NP:(t + 1) * NP],
                                             ident[:, :])
                mm.then_inc(back_ready, 1)

            pe.wait_ge(load["gate"], 32)

            def gate(s):
                c0, w = SPLITS[s]
                pe.wait_ge(xt_act, 2 * (s + 1))
                pe.wait_ge(xt_dve, 2 * (s + 1))
                for f in range(FT):
                    mm = nc.tensor.matmul(PS[0:NEXP, 5 + s, 0:w], gw[:, f, :], xt[:, f, c0:c0 + w],
                                          start=(f == 0), stop=(f == FT - 1))
                mm.then_inc(gate_ps, 1)

            for n, (s, f) in enumerate(SF):
                c0, w = SPLITS[s]
                if f == 0:
                    pe.wait_ge(xn_ready, 2 * NT + (c0 + w) // NP)
                if n >= 4:
                    pe.wait_ge(xt_act if n % 2 == 0 else xt_dve, (n - 4) // 2 + 1)
                for j in range(w // NP):
                    mm = nc.tensor.transpose(PS[:, n % 4, j * NP:(j + 1) * NP],
                                             XN[0:NP, c0 // NP + j, f * 128:(f + 1) * 128], ident[0:NP, 0:NP])
                mm.then_inc(xtp_ready, 1)
                if f == FT - 1 and s:
                    gate(s - 1)
            gate(len(SPLITS) - 1)
            for t in range(NT):
                if t % 4 == 0:
                    pe.wait_ge(lgt_ready, t // 4 + 1)
                mm = nc.tensor.transpose(PS[0:NP, 4, t * NEXP:(t + 1) * NEXP], lgt[:, t * NP:(t + 1) * NP],
                                         ident[0:NEXP, 0:NEXP])
            mm.then_inc(logit_ready, 1)
            def turn_rows(i, k, b):
                pe.wait_ge(gathered[k], i * 16 + 16)
                for f in range(FT):
                    mm = nc.tensor.transpose(PS[:, 4, f * 128:(f + 1) * 128], xg[:, k, f * 128:(f + 1) * 128], ident[:, :])
                mm.then_inc(xt_ps, 1)

            def up_bank_free(p):
                if not (isinstance(p, int) and p < 2):
                    pe.wait_ge(clip_done, p - 1)

            def shared_up(k, p, t):
                up_bank_free(p)
                for h in range(2):
                    for f in range(FT):
                        mm = nc.tensor.matmul(PS[0:NP, 2 * k + h, 0:INTER], xt[:, f, t * NP:(t + 1) * NP],
                                              SW[:, f * H2 + h * INTER:f * H2 + (h + 1) * INTER],
                                              start=(f == 0), stop=(f == FT - 1))
                mm.then_inc(hb_ready, 1)

            def up(i, k, b):
                off = pe.value_load(eb_i[0:1, 1, bass.ds(b, 1)], min_val=0, max_val=(NWB - 1) * WBUF)
                pe.wait_ge(w1_in[k], i * 32 + 32)
                pe.wait_ge(xgt_ready, b + 1)
                up_bank_free(b + EARLY)
                for h in range(2):
                    for f in range(FT):
                        mm = nc.tensor.matmul(PS[:, 2 * k + h, 0:INTER], xgt[:, k, f, :],
                                              WB[:, bass.ds(off + (f * H2 + h * INTER), INTER)],
                                              start=(f == 0), stop=(f == FT - 1))
                mm.then_inc(hb_ready, 1)

            def turn_act(k, p, rows=128):
                pe.wait_ge(t_ready, p + 1)
                if not (isinstance(p, int) and p < 1):
                    pe.wait_ge(tt_ready, p)
                for j in range(3):
                    mm = nc.tensor.transpose(PS[:, 5, j * 128:j * 128 + rows], tb[0:rows, k, j * 128:(j + 1) * 128],
                                             ident[0:rows, 0:rows])
                mm.then_inc(tt_ps, 1)

            def shared_down(k, p, t):
                pe.wait_ge(tt_ready, p + 1)
                for j in range(3):
                    nc.tensor.matmul(PS[0:NP, 6 + k, :], tt[:, k, j, 0:NP], SW[:, O_W2 + j * D:O_W2 + (j + 1) * D],
                                     start=(j == 0), stop=False)
                nc.tensor.matmul(PS[0:NP, 6 + k, :], cwt[:, t * NP:(t + 1) * NP], b2m, start=False, stop=True
                                 ).then_inc(y_done, 1)

            def down(i, k, b):
                off = pe.value_load(eb_i[0:1, 1, bass.ds(b, 1)], min_val=0, max_val=(NWB - 1) * WBUF)
                pe.wait_ge(w2_in[k], i * 16 + 16)
                pe.wait_ge(tt_ready, b + (EARLY + 1))
                if isinstance(b, int) and b < 2:
                    pe.wait_ge(z_added, EARLY - 1 + b)
                else:
                    pe.wait_ge(yo_ready, b - 1)
                for j in range(3):
                    mm = nc.tensor.matmul(PS[:, 6 + k, :], tt[:, k, j, :], WB[:, bass.ds(off + (O_W2 + j * D), D)],
                                          start=(j == 0), stop=(j == 2))
                mm.then_inc(y_done, 1)

            pe.wait_ge(load["sw"], 48)
            shared_up(0, 0, 0)
            shared_up(1, 1, 1)
            pe.wait_ge(sel_ready, 1)
            pe.wait_ge(const_done, CONSTS + 9)
            nc.tensor.matmul(PS[0:NP, 4, 0:NT * NEXP], below[0:NP, 0:NP], q[0:NP, :, :].rearrange("p t e -> p (t e)"),
                             start=True, stop=False)
            nc.tensor.matmul(PS[0:NP, 4, 0:NT * NEXP], ones[0:NP, 0:NP],
                             cum[0:NP, 0:NT, :].rearrange("p t e -> p (t e)"), start=False, stop=True)
            nc.tensor.matmul(PS[:, 4, NT * NEXP:(NT + 1) * NEXP], ones[0:NP, :], cum[0:NP, NT, :], start=True, stop=True
                             ).then_inc(rank_ready, 1)
            for t in range(NT):
                s = min(t // 4, 2)
                n, o = CWT_BANKS[s]
                mm = nc.tensor.transpose(PS[0:NEXP + 1, n, o + t * NP - SPLITS[s][0]:o + (t + 1) * NP - SPLITS[s][0]],
                                         cw[0:NP, t, :], ident[0:NP, 0:NP])
            mm.then_inc(cw_ps, 1)
            pe.wait_ge(load["b2"], 16)
            turn_act(0, 0, NP)
            pe.wait_ge(cwt_ready, 1)
            shared_down(0, 0, 0)
            for p in range(2, EARLY):
                shared_up(p % 2, p, p)
                if p == EARLY - 3:
                    pe.wait_ge(slots_ready, 1)
                    for i in range(ASSIGN):
                        mm = nc.tensor.matmul(PS[:, 4, 0:2 * NB], ohr[0:NP, i, :],
                                              ohb[0:NP, i, :, :].rearrange("p a b -> p (a b)"),
                                              start=(i == 0), stop=(i == ASSIGN - 1))
                    mm.then_inc(table_ps, 1)
                turn_act((p - 1) % 2, p - 1, NP)
                if p >= 3:
                    pe.wait_ge(z_added, p - 2)
                shared_down((p - 1) % 2, p - 1, p - 1)

            pe.wait_ge(tables_ready, 1)
            last = last_pair(pe)
            turn_rows(0, 0, 0)
            up(0, 0, 0)
            turn_act(1, EARLY - 1, NP)
            turn_rows(0, 1, 1)
            pe.wait_ge(z_added, EARLY - 2)
            shared_down(1, EARLY - 1, EARLY - 1)
            up(0, 1, 1)
            turn_act(0, EARLY)
            pe.wait_ge(xgt_ready, 2)
            turn_rows(1, 0, 2)
            down(0, 0, 0)
            with pe.Fori(1, NB // 2) as i:
                with pe.If(i < last + 1):
                    up(i, 0, i * 2)
                    turn_act(1, i * 2 + (EARLY - 1))
                    turn_rows(i, 1, i * 2 + 1)
                    with pe.If(i < 2):
                        down(0, 1, 1)
                    with pe.If(i > 1):
                        down(i - 1, 1, i * 2 - 1)
                    up(i, 1, i * 2 + 1)
                    turn_act(0, i * 2 + EARLY)
                    with pe.If(i < last):
                        turn_rows(i + 1, 0, i * 2 + 2)
                    down(i, 0, i * 2)
            shared_up(0, last * 2 + (EARLY + 2), EARLY)
            turn_act(1, last * 2 + (EARLY + 1))
            down(last, 1, last * 2 + 1)
            for j in range(NT - EARLY):
                if j + 1 < NT - EARLY:
                    shared_up((j + 1) % 2, last * 2 + (EARLY + j + 3), EARLY + j + 1)
                turn_act(j % 2, last * 2 + (EARLY + 2 + j), NP)
                if j < 2:
                    pe.wait_ge(yo_ready, last * 2 + (j + 1))
                else:
                    pe.wait_ge(z_added, EARLY + j - 1)
                shared_down(j % 2, last * 2 + (EARLY + 2 + j), EARLY + j)

        @block.vector
        def _(dve):
            v = nc.vector
            link = counting(dve, step)

            def deviations(k):
                v.tensor_scalar(mv[0:NP, :, 1], mv[0:NP, :, 1], EPS, None, ALU.add).then_inc(var_ready, 1)
                dve.wait_ge(sd_ready, k + 1 if k == 0 else k + 2)
                link(v.reciprocal(rstd[0:NP, :], sd[0:NP, :]))

            def normalise(t, c0=0, c1=D):
                return v.tensor_scalar(XN[0:NP, t, c0:c1], X[0:NP, t, c0:c1], mv[0:NP, t, 0:1], rstd[0:NP, t:t + 1],
                                       ALU.subtract, ALU.mult)

            def layer_norm(k):
                deviations(k)
                for t in range(NT):
                    normalise(t).then_inc(xn_ready, 1)
                dve.wait_ge(xn_ready, k * NT)

            dve.wait_ge(load["edges"], 32)
            v.tensor_copy(dstf[0:CHUNK, :], dst_i[0:CHUNK, :]).then_inc(base_ready, 1)
            link(v.tensor_copy(srcf[0:CHUNK, :], src_i[0:CHUNK, :]))
            link(v.tensor_scalar(hi[0:CHUNK, :], srcf[0:CHUNK, :], -62.0, 1.0 / NP, ALU.add, ALU.mult))
            link(v.tensor_scalar(rel[0:CHUNK, :], hi[0:CHUNK, :], MAGIC, None, ALU.add))
            link(v.tensor_scalar(hi[0:CHUNK, :], rel[0:CHUNK, :], -MAGIC, None, ALU.add))
            link(v.scalar_tensor_tensor(out=lo[0:CHUNK, :], in0=hi[0:CHUNK, :], scalar=-float(NP),
                                        in1=srcf[0:CHUNK, :], op0=ALU.mult, op1=ALU.add))
            v.tensor_scalar(neglo[0:CHUNK, :], lo[0:CHUNK, :], -1.0, None, ALU.mult).then_inc(lo_ready, 1)
            dve.wait_ge(base_read, 1)
            v.tensor_copy(wbase_i[0:1, :], PS[0:1, 7, 0:NG]).then_inc(windows_ready, 1)
            link(v.tensor_copy(wbase[:, :], PS[:, 7, 0:NG]))
            three = lambda m: m[0:CHUNK, :].rearrange("p (g j) -> p g j", j=CPG)

            def make_keys(link_to):
                link_to(v.tensor_tensor(three(rel), three(dstf),
                                        wbase[0:CHUNK, :].rearrange("p (g o) -> p g o", o=1).to_broadcast([CHUNK, NG, CPG]),
                                        ALU.subtract))
                link_to(v.tensor_scalar(srcf[0:CHUNK, :], rel[0:CHUNK, :], 0.0, None, ALU.is_ge))
                link_to(v.scalar_tensor_tensor(out=srcf[0:CHUNK, :], in0=rel[0:CHUNK, :], scalar=float(WIN),
                                               in1=srcf[0:CHUNK, :], op0=ALU.is_lt, op1=ALU.mult))
                link_to(v.scalar_tensor_tensor(out=rel[0:CHUNK, :], in0=hi[0:CHUNK, :], scalar=float(WIN),
                                               in1=rel[0:CHUNK, :], op0=ALU.mult, op1=ALU.add))
                link_to(v.scalar_tensor_tensor(out=key[0:CHUNK, :], in0=rel[0:CHUNK, :], scalar=1.0,
                                               in1=srcf[0:CHUNK, :], op0=ALU.add, op1=ALU.mult))
                link_to(v.tensor_scalar(key[0:CHUNK, :], key[0:CHUNK, :], -1.0, None, ALU.add))

            make_keys(link)
            link(v.tensor_reduce(bad[0:CHUNK, 1:2], srcf[0:CHUNK, :], AX.X, ALU.min))
            v.tensor_scalar(bad[0:CHUNK, 0:1], bad[0:CHUNK, 1:2], -1.0, 1.0, ALU.mult, ALU.add).then_inc(bad_ready, 1)
            dve.wait_ge(bad_sum, 1)
            link(v.tensor_scalar(bad[:, 2:3], PS[:, 6, 0:1], 0.5, None, ALU.is_ge))
            last = NG - APART
            link(v.memset(apart[0:1, :, :], 1.0))
            link(v.tensor_tensor(apart[0:1, 0, 0:NG - 1], wbase[0:1, 1:NG], wbase[0:1, 0:NG - 1], ALU.is_ge))
            link(v.tensor_tensor(apart[0:1, 1, 0:last], wbase[0:1, APART:NG], wbase[0:1, 0:last], ALU.subtract))
            link(v.tensor_scalar(apart[0:1, 1, 0:last], apart[0:1, 1, 0:last], float(WIN), None, ALU.is_ge))
            link(v.tensor_reduce(bad[0:1, 3:4], apart[0:1, :, :].rearrange("p a g -> p (a g)"), AX.X, ALU.min))
            link(v.scalar_tensor_tensor(out=bad[0:1, 2:3], in0=bad[0:1, 3:4], scalar=0.5, in1=bad[0:1, 2:3],
                                        op0=ALU.is_lt, op1=ALU.max))
            v.tensor_copy(flag_i[0:1, 0:1], bad[0:1, 2:3]).then_inc(flag_ready, 1)
            dve.wait_ge(const_done, 4)
            link(v.tensor_copy(WH[:, 0, 0:128], ones[:, :]))

            dve.wait_ge(const_done, 4)

            def onehots(k, c, first=0):
                for j in range(CPG):
                    if j >= first:
                        v.tensor_scalar(oh_lo[0:CHUNK, k, j, 0:NP], iota_k[0:CHUNK, 0:NP], lo[0:CHUNK, bass.ds(c + j, 1)],
                                        None, ALU.is_equal)
                    ins = v.tensor_scalar(ohk[k][0:CHUNK, j, :], iota_k[0:CHUNK, :], key[0:CHUNK, bass.ds(c + j, 1)],
                                          None, ALU.is_equal)
                return ins

            for g in range(STEPS):
                if g >= 2:
                    dve.wait_ge(group_done, g - 1)
                onehots(g % 2, g * CPG, ACTJ).then_inc(onehot_ready, 1)
            with dve.Fori(1, NG // STEPS) as i:
                for g in range(STEPS):
                    dve.wait_ge(group_done, i * STEPS + (g - 1))
                    onehots(g % 2, i * (STEPS * CPG) + g * CPG, ACTJ).then_inc(onehot_ready, 1)

            dve.wait_ge(added, NG)

            slow = dve.value_load(flag_i[0:1, 0:1], min_val=0, max_val=1)
            with dve.If(slow > 0):
                SLOW0, SLOWK = 2, 7
                v.memset(CT[0:NP, :, :], 0.0).then_inc(slow_step, 1)
                v.memset(wbase[:, :], 0.0).then_inc(slow_step, 1)
                dve.wait_ge(slow_step, SLOW0)
                with dve.Fori(0, PASSES) as w:
                    done = [0]

                    def slow_link(ins):
                        done[0] += 1
                        at = dve.to_reg(w * (SLOWK + NG) + (SLOW0 + done[0]))
                        ins.then_inc(slow_step, 1)
                        dve.wait_ge(flag_ready, 1)
                        dve.wait_ge(slow_step, at)

                    make_keys(slow_link)
                    slow_link(v.tensor_scalar(wbase[:, :], wbase[:, :], float(WIN), None, ALU.add))
                    with dve.Fori(0, NG) as g:
                        onehots(0, g * CPG).then_inc(slow_onehot, 1)
                        dve.wait_ge(slow_group, w * NG + g + 1)
                        dest = CT[0:NP, :, bass.ds(w * WIN, WIN)]
                        v.tensor_tensor(dest, PS[0:NP, 0, 0:KEYS].rearrange("p (t w) -> p t w", t=NT), dest, ALU.add
                                        ).then_inc(slow_step, 1)
                        dve.wait_ge(slow_step, w * (SLOWK + NG) + g + (SLOW0 + SLOWK + 1))

            dve.wait_ge(const_done, CONSTS)

            def self_loops(op, signal):
                for table, on in ((CTR, slow < 1), (CT, slow > 0)):
                    with dve.If(on):
                        for t in range(NT):
                            dest = table[0:NP, t, t * NP:(t + 1) * NP]
                            ins = v.tensor_tensor(dest, f32(dest) if table is CTR else dest, ident[0:NP, 0:NP], op)
                        ins.then_inc(signal, 1)

            self_loops(ALU.add, counts_ready)

            dve.wait_ge(load["acts"], 16)
            link(v.tensor_scalar(clampv[:, 0, :, :], acts[:, :, 3:5], -1.0, None, ALU.mult))
            v.tensor_tensor(clampv[:, 1, :, :], clampv[:, 0, :, :], acts[:, :, 3:5], ALU.min).then_inc(sp_ready, 1)
            dve.wait_ge(sp_exp, 1)
            v.tensor_scalar(clampv[:, 3, :, :], clampv[:, 2, :, :], 1.0, None, ALU.add).then_inc(sp_one, 1)
            dve.wait_ge(sp_ln, 1)
            link(v.tensor_scalar(clampv[:, 2, :, :], acts[:, :, 3:5], 0.0, None, ALU.max))
            link(v.tensor_tensor(clampv[:, 0, :, :], clampv[:, 2, :, :], clampv[:, 4, :, :], ALU.add))
            link(v.tensor_scalar(clampv[:, 1, :, :], clampv[:, 0, :, :], -1.0, None, ALU.mult))

            dve.wait_ge(load["x"], 16)
            for t in range(NT):
                ins = v.bn_stats(stats[0:NP, t, 0, :], X[0:NP, t, :])
            link(ins)
            for t in range(NT):
                ins = v.bn_aggr(mv[0:NP, t, :], stats[0:NP, t, 0, :])
            link(ins)
            deviations(0)

            for s, (c0, w) in enumerate(SPLITS):
                dve.wait_ge(deg_ready, s + 1)
                ins = v.tensor_copy(invc[:, c0:c0 + w], PS[:, s, 0:w])
            ins.then_inc(deg_copied, 1)
            dve.wait_ge(sd_ready, 2)
            link(v.reciprocal(dis[0:NP, :], dis[0:NP, :]))
            link(v.tensor_tensor(rdis[0:NP, :], rstd[0:NP, :], dis[0:NP, :], ALU.mult))
            def low_part(m, t, source):
                dve.wait_ge(yh_ready, m + 1)
                v.tensor_tensor(YL[0:NP, t, :], source, f32(YH[0:NP, t, :]), ALU.subtract).then_inc(y_ready, 1)

            def split_weight(k, raw):
                dve.wait_ge(wh_ready, k + 1)
                v.tensor_tensor(WL[:, :, :], raw, f32(WH[:, :, :]), ALU.subtract).then_inc(w_ready, 1)

            for t in range(NT + 1):
                if t < NT:
                    if t >= 2:
                        dve.wait_ge(yh_ready, t - 1)
                        dve.wait_ge(y_ready, t - 1)
                    v.tensor_scalar(val[0:NP, t % 2, :], X[0:NP, t, :], mv[0:NP, t, 0:1], rdis[0:NP, t:t + 1],
                                    ALU.subtract, ALU.mult).then_inc(val_ready, 1)
                if t:
                    dve.wait_ge(val_ready, t)
                    low_part(t - 1, t - 1, val[0:NP, (t - 1) % 2, :])
            split_weight(0, WRAW[:, :, :])
            dve.wait_ge(degcol_ready, 1)
            link(v.tensor_scalar(invc[:, :], invc[:, :], -1.0, 1.0, ALU.add, ALU.max))
            link(v.reciprocal(invc[:, :], invc[:, :]))
            dve.wait_ge(load["gb"], 16 * LAYERS)

            n = 0
            for l in range(LAYERS):
                if l:
                    dve.wait_ge(lin_ready, NT * l)
                    split_weight(l, WNEXT[:, l - 1, :, :])
                for s, (c0, w) in enumerate(SPLITS):
                    for f in range(FT):
                        dve.wait_ge(zh_ready, n + 1)
                        v.tensor_tensor(ZL[:, f, c0:c0 + w], PS[:, n % 6, 0:w], f32(ZH[:, f, c0:c0 + w]), ALU.subtract
                                        ).then_inc(zl_ready, 1)
                        n += 1
                for t in range(NT + 1):
                    m = l * NT + t
                    if t < NT:
                        dve.wait_ge(lin_ready, m + 1)
                        if l < LAYERS - 1 and m >= 2:
                            dve.wait_ge(val_ready, NT + m - 1)
                        if l == LAYERS - 1 and t < 2:
                            dve.wait_ge(val_ready, NT * LAYERS)
                        ins = v.scalar_tensor_tensor(out=tmp[0:NP, t % 2, :], in0=PS[0:NP, 6 + m % 2, :],
                                                     scalar=dis[0:NP, t:t + 1], in1=bias[0:NP, l, :],
                                                     op0=ALU.mult, op1=ALU.add)
                        ins.then_inc(pre_ready if l < LAYERS - 1 else lin_read, 1)
                    if l < LAYERS - 1 and t:
                        low_part(NT + m - 1, t - 1, val[0:NP, (t - 1) % 2, :])
                    if l == LAYERS - 1 and t < NT:
                        dve.wait_ge(lin_read, t + 1)
                        link(v.scalar_tensor_tensor(out=X[0:NP, t, :], in0=tmp[0:NP, t % 2, :], scalar=0.0,
                                                    in1=X[0:NP, t, :], op0=ALU.max, op1=ALU.add))
                        link(v.bn_stats(stats[0:NP, t, 0, :], X[0:NP, t, :]))
                        ins = v.bn_aggr(mv[0:NP, t, :], stats[0:NP, t, 0, :])
            link(ins)

            deviations(1)
            for t in range(NT):
                ins = normalise(t, 0, IN1)
            link(ins)
            nib = XN[0:NP, :, 16:80].rearrange("p t (g j) -> p t g j", j=16)
            link(v.tensor_scalar(fk[0:NP, :, :, :], nib, 0.5, None, ALU.is_gt))
            wjb = wj[0:NP, :].rearrange("p (a j) -> p a j", a=1)
            link(v.tensor_tensor(fk[0:NP, :, :, :].rearrange("p t g j -> p (t g) j"),
                                 fk[0:NP, :, :, :].rearrange("p t g j -> p (t g) j"),
                                 wjb.to_broadcast([NP, NT * 4, 16]), ALU.mult))
            link(v.tensor_reduce(fm[0:NP, :, :], fk[0:NP, :, :, :], AX.X, ALU.max))
            link(v.tensor_scalar(fg[0:NP, :, :], fm[0:NP, :, :], -1.0, 16.0, ALU.mult, ALU.add))
            link(v.scalar_tensor_tensor(out=fg[0:NP, :, :], in0=fm[0:NP, :, :], scalar=0.0, in1=fg[0:NP, :, :],
                                        op0=ALU.is_gt, op1=ALU.mult))
            for pos in range(POS):
                v.tensor_copy(feats[0:NP, pos, :, 0], fg[0:NP, :, pos])
                v.tensor_copy(feats[0:NP, pos, :, 1], fg[0:NP, :, 2 + pos])
                ins = v.tensor_copy(feats[0:NP, pos, :, 2:4], XN[0:NP, :, 105:107])
            ins.then_inc(feat_ready, 1)
            for c in range(3):
                ins = v.tensor_scalar(msk[0:NP, c, :], XN[0:NP, :, c], 0.5, None, ALU.is_gt)
            link(ins)
            v.tensor_tensor(msk[0:NP, 3, :], msk[0:NP, 0, :], msk[0:NP, 1, :], ALU.mult)
            link(v.tensor_tensor(msk[0:NP, 4, :], msk[0:NP, 0, :], msk[0:NP, 2, :], ALU.mult))
            link(v.tensor_tensor(msk[0:NP, 7, :], msk[0:NP, 4, :], msk[0:NP, 1, :], ALU.mult))
            link(v.tensor_tensor(msk[0:NP, 5, :], msk[0:NP, 4, :], msk[0:NP, 7, :], ALU.subtract))
            link(v.tensor_tensor(msk[0:NP, 6, :], msk[0:NP, 3, :], msk[0:NP, 5, :], ALU.add))
            for t in range(NT):
                normalise(t, IN1, D).then_inc(xn_ready, 1)
            dve.wait_ge(xn_ready, NT)
            def h1_copy(c):
                dve.wait_ge(f1_ready, 3 * c + 2)
                if c >= 2:
                    dve.wait_ge(f2_ready, 3 * (c - 1))
                v.tensor_scalar(h1t[:, c % 2, 1, :], PS[0:GU, 1, 0:RC], 0.0, None, ALU.max).then_inc(h1_dve, 1)

            def h2_copy(c):
                for j in (1, 2):
                    dve.wait_ge(f2_ready, 3 * c + j + 1)
                    if c >= 2:
                        dve.wait_ge(f3_ready, c - 1)
                    n = TILE[j]
                    v.tensor_scalar(h2t[0:n, c % 2, j, :], PS[0:n, 3 + j, 0:RC], b2f[0:n, j:j + 1], 0.0,
                                    ALU.add, ALU.max).then_inc(h2_dve, 1)

            dve.wait_ge(load["ffn"], 16 * FFN_LOADS)
            h1_copy(0)
            for c in range(NRC):
                if c + 1 < NRC:
                    h1_copy(c + 1)
                h2_copy(c)
                for t in (2 * c, 2 * c + 1):
                    ins = v.tensor_tensor(X[0:NP, t, :], X[0:NP, t, :], XN[0:NP, t, :], ALU.add)
                link(ins)
                for t in (2 * c, 2 * c + 1):
                    v.bn_stats(stats[0:NP, t, 0, :], X[0:NP, t, 0:OUT0])
                    v.bn_stats(stats[0:NP, t, 1, :], X[0:NP, t, OUT1:D])
                if c == 3:
                    split_weight(3, WRAW[:, :, :])
                if c == NRC - 1:
                    self_loops(ALU.subtract, minus_ready)
            dve.wait_ge(y3_turned, 1)
            for net in range(2):
                link(v.tensor_tensor(yv[0:NP, net, :, :],
                                     PS[0:NP, 6, 0:POS * NT * 4].rearrange("p (t n c) -> p n t c", n=2, c=2)[:, net],
                                     b3f[0:NP, net, :].rearrange("p (a c) -> p a c", a=1).to_broadcast([NP, POS * NT, 2]),
                                     ALU.add))
                m = msk[0:NP, 3 if net == 0 else 5, :].rearrange("p (t o) -> p t o", o=1).to_broadcast([NP, NT, 2])
                for pos in range(POS):
                    view = yv[0:NP, net, pos * NT:(pos + 1) * NT, :]
                    ins = v.tensor_tensor(view, view, m, ALU.mult)
                link(ins)
            link(v.tensor_tensor(res[0:NP, :, :], yv[0:NP, 0, :, :], yv[0:NP, 1, :, :], ALU.add))
            link(v.tensor_scalar(msk[0:NP, 7, :], res[0:NP, NT:2 * NT, 1], 0.5, None, ALU.is_gt))
            link(v.tensor_tensor(msk[0:NP, 7, :], msk[0:NP, 7, :], msk[0:NP, 6, :], ALU.mult))
            link(v.tensor_scalar(res[0:NP, :, :], res[0:NP, :, :], 0.0, 15.0, ALU.max, ALU.min))
            link(v.tensor_scalar(res[0:NP, :, :], res[0:NP, :, :], MAGIC, None, ALU.add))
            link(v.tensor_scalar(res[0:NP, :, :], res[0:NP, :, :], -MAGIC, None, ALU.add))
            link(v.tensor_scalar(msk[0:NP, 6, :], msk[0:NP, 6, :], 2.0, None, ALU.mult))
            wide = lambda m: m.rearrange("p (t o) -> p t o", o=1).to_broadcast([NP, NT, 16])
            cjb = cj[0:NP, :].rearrange("p (a j) -> p a j", a=1).to_broadcast([NP, NT, 16])
            for pos in range(POS):
                link(v.tensor_tensor(oh2[0:NP, :, :], cjb,
                                     res[0:NP, pos * NT:(pos + 1) * NT, 0:1].to_broadcast([NP, NT, 16]), ALU.is_equal))
                link(v.tensor_tensor(oh2[0:NP, :, :], oh2[0:NP, :, :], wide(msk[0:NP, 6, :]), ALU.mult))
                view = X[0:NP, :, 128 + 16 * pos:144 + 16 * pos]
                link(v.tensor_tensor(view, view, oh2[0:NP, :, :], ALU.add))
            link(v.tensor_tensor(X[0:NP, :, 160], X[0:NP, :, 160], msk[0:NP, 7, :], ALU.add))

            for t in range(NT):
                ins = v.bn_stats(stats[0:NP, t, 2, :], X[0:NP, t, OUT0:OUT1])
            link(ins)
            for t in range(NT):
                ins = v.bn_aggr(mv[0:NP, t, :], stats[0:NP, t, :, :].rearrange("p a k -> p (a k)"))
            link(ins)
            layer_norm(2)
            for n, (s, f) in enumerate(SF):
                c0, w = SPLITS[s]
                dve.wait_ge(sxt_hi, n + 1)
                v.tensor_tensor(ZL[:, f, c0:c0 + w], PS[:, n % 4, 0:w], f32(ZH[:, f, c0:c0 + w]), ALU.subtract
                                ).then_inc(sxt_ready, 1)
            for t in range(NT):
                low_part(LAYERS * NT + t, t, XN[0:NP, t, :])
            for t in range(NT):
                v.tensor_tensor(X[0:NP, t, :], X[0:NP, t, :], XN[0:NP, t, :], ALU.add).then_inc(xn_added, 1)
            for n in range(len(SF) + 1):
                if n < len(SF):
                    s, f = SF[n]
                    c0, w = SPLITS[s]
                    dve.wait_ge(mean_ps, n + 1)
                    if n >= 2:
                        dve.wait_ge(mean_ready, n - 1)
                    v.tensor_tensor(tmp[:, n % 2, 0:w], PS[:, n % 4, 0:w], invc[:, c0:c0 + w], ALU.mult
                                    ).then_inc(mean_f32, 1)
                if n:
                    s, f = SF[n - 1]
                    c0, w = SPLITS[s]
                    dve.wait_ge(mean_hi, n)
                    v.tensor_tensor(ZL[:, f, c0:c0 + w], tmp[:, (n - 1) % 2, 0:w], f32(ZH[:, f, c0:c0 + w]),
                                    ALU.subtract).then_inc(mean_ready, 1)
                if n == len(SF) - FT:
                    split_weight(4, WRAW[:, :, :])
            dve.wait_ge(load["sage"], 48)

            def scale_shift(f):
                one = lambda c: hs[:, c, f:f + 1]
                dve.wait_ge(hsd, f + 1)
                link(v.reciprocal(one(2), one(1)))
                link(v.tensor_tensor(one(2), one(2), sage[:, 1, f:f + 1], ALU.mult))
                link(v.tensor_tensor(one(3), hmv[:, f, 0:1], one(2), ALU.mult))
                v.tensor_tensor(one(3), sage[:, 2, f:f + 1], one(3), ALU.subtract).then_inc(hscale, 1)

            dve.wait_ge(hr_ready, len(SF))
            for n, (f, s) in enumerate(FS_SECOND):
                c0, w = SPLITS[s]
                dve.wait_ge(hp_ready, n + 1)
                v.tensor_tensor(ht[:, f, c0:c0 + w], PS[:, 4 + n % 4, 0:w], ht[:, f, c0:c0 + w], ALU.add
                                ).then_inc(h_ready, 1)
                dve.wait_ge(h_ready, n + 1)
                ins = v.bn_stats(hst[:, f, s, :], ht[:, f, c0:c0 + w])
                if s == 1 and f:
                    scale_shift(f - 1)
                if s == len(SPLITS) - 1:
                    link(ins)
                    link(v.bn_aggr(hmv[:, f, :], hst[:, f, :, :].rearrange("p s k -> p (s k)")))
                    v.tensor_scalar(hs[:, 0, f:f + 1], hmv[:, f, 1:2], EPS, None, ALU.add).then_inc(hstat, 1)
            scale_shift(FT - 1)
            for t in range(NT):
                dve.wait_ge(back_ready, t + 1)
                v.tensor_tensor(X[0:NP, t, :], PS[0:NP, 2 + t % 2, :], X[0:NP, t, :], ALU.add).then_inc(back_read, 1)
                dve.wait_ge(back_read, t + 1)
                link(v.bn_stats(stats[0:NP, t, 0, :], X[0:NP, t, :]))
                ins = v.bn_aggr(mv[0:NP, t, :], stats[0:NP, t, 0, :])
            link(ins)

            layer_norm(3)
            for n, (s, f) in enumerate(SF):
                c0, w = SPLITS[s]
                if f % 2 == 1:
                    dve.wait_ge(xtp_ready, n + 1)
                    v.tensor_copy(xt[:, f, c0:c0 + w], PS[:, n % 4, 0:w]).then_inc(xt_dve, 1)
            R = lambda m: m[0:NP, :, :]
            col = lambda c: rsmall[0:NP, c, :]
            over = lambda m: m.rearrange("p (t o) -> p t o", o=1).to_broadcast([NP, NT, NEXP])
            wjt = wj[0:NP, :].rearrange("p (a j) -> p a j", a=1).to_broadcast([NP, NT, NEXP])
            dve.wait_ge(const_done, CONSTS + 6)
            dve.wait_ge(logit_ready, 1)
            logits = PS[0:NP, 4, 0:NT * NEXP].rearrange("p (t e) -> p t e", t=NT)
            link(v.tensor_reduce(col(0), logits, AX.X, ALU.max))
            v.tensor_tensor(R(q), logits, over(col(0)), ALU.subtract).then_inc(zmax_ready, 1)
            dve.wait_ge(exp_ready, 1)
            link(v.tensor_reduce(col(1), R(pr), AX.X, ALU.add))
            link(v.reciprocal(col(1), col(1)))
            link(v.tensor_tensor(R(pr), R(pr), over(col(1)), ALU.mult))
            for k in range(TOPK):
                link(v.tensor_reduce(col(2 + k), R(pr), AX.X, ALU.max))
                link(v.tensor_tensor(R(q), R(pr), over(col(2 + k)), ALU.is_equal))
                link(v.tensor_tensor(R(q), R(q), wjt, ALU.mult))
                link(v.tensor_reduce(col(4), R(q), AX.X, ALU.max))
                link(v.tensor_tensor(R(oh[k]), wjt, over(col(4)), ALU.is_equal))
                if k == 0:
                    link(v.scalar_tensor_tensor(out=R(pr), in0=R(oh[0]), scalar=-4.0, in1=R(pr),
                                                op0=ALU.mult, op1=ALU.add))
            link(v.tensor_tensor(col(5), col(2), col(3), ALU.add))
            link(v.reciprocal(col(5), col(5)))
            v.tensor_tensor(wsel[0:NP, 0, :], col(2), col(5), ALU.mult)
            link(v.tensor_tensor(wsel[0:NP, 1, :], col(3), col(5), ALU.mult))
            for k in range(TOPK):
                link(v.tensor_tensor(R(pr) if k else cw[0:NP, :, 0:NEXP], R(oh[k]), over(wsel[0:NP, k, :]), ALU.mult))
            link(v.tensor_tensor(cw[0:NP, :, 0:NEXP], cw[0:NP, :, 0:NEXP], R(pr), ALU.add))
            link(v.memset(cw[0:NP, :, NEXP:NEXP + 1], 1.0))
            link(v.tensor_tensor(R(q), R(oh[0]), R(oh[1]), ALU.add))
            for t in range(NT):
                ins = v.tensor_tensor(cum[0:NP, t + 1, :], cum[0:NP, t, :], q[0:NP, t, :], ALU.add)
                if t < NT - 1:
                    link(ins)
            ins.then_inc(sel_ready, 1)

            def rows_copy(k, b):
                dve.wait_ge(xt_ps, b + 1)
                v.tensor_copy(xgt[:, k, :, :], PS[:, 4, :].rearrange("p (f n) -> p f n", f=FT)).then_inc(xgt_ready, 1)

            def units(k, p, b=None, then=None):
                if b is None:
                    rows, one_e, b1 = NP, slice(NEXP, NEXP + 1), SW[0:NP, O_B1:WBUF]
                else:
                    e = dve.value_load(eb_i[0:1, 0, bass.ds(b, 1)], min_val=0, max_val=NEXP - 1)
                    off = dve.value_load(eb_i[0:1, 1, bass.ds(b, 1)], min_val=0, max_val=(NWB - 1) * WBUF)
                    rows, one_e, b1 = 128, bass.ds(e, 1), WB[:, bass.ds(off + O_B1, H2)]
                hi_g, lo_g = clampv[0:rows, 0, one_e, 0], clampv[0:rows, 1, one_e, 0]
                hi_u, lo_u = clampv[0:rows, 0, one_e, 1], clampv[0:rows, 1, one_e, 1]
                gate, upv = hb[k][0:rows, 0:H2:2], hb[k][0:rows, 1:H2:2]
                dve.wait_ge(hb_ready, p + 1)
                if not (isinstance(p, int) and p < 2):
                    dve.wait_ge(t_ready, p - 1)
                v.tensor_tensor(hb[k][0:rows].rearrange("p (h c) -> p h c", h=2), PS[0:rows, 2 * k:2 * k + 2, 0:INTER],
                                b1.rearrange("p (h c) -> p h c", h=2), ALU.add).then_inc(clip_done, 1)
                dve.wait_ge(clip_done, p + 1)
                v.tensor_scalar(gate, gate, lo_g, hi_g, ALU.max, ALU.min).then_inc(clip_g, 1)
                v.tensor_scalar(upv, upv, lo_u, hi_u, ALU.max, ALU.min).then_inc(clip_u, 1)
                if then is not None:
                    then()
                dve.wait_ge(gate_sig, p + 1)
                v.scalar_tensor_tensor(out=ss[k][0:rows], in0=gate, scalar=acts[0:rows, one_e, 1], in1=ss[k][0:rows],
                                       op0=ALU.mult, op1=ALU.mult).then_inc(t_gs, 1)
                dve.wait_ge(t_gs, p + 1)
                dve.wait_ge(clip_u, p + 1)
                if not (isinstance(p, int) and p < 2):
                    dve.wait_ge(tt_ps, p - 1)
                v.scalar_tensor_tensor(out=tb[0:rows, k, :], in0=upv, scalar=acts[0:rows, one_e, 2], in1=ss[k][0:rows],
                                       op0=ALU.add, op1=ALU.mult).then_inc(t_ready, 1)

            def z_add(t, p):
                dve.wait_ge(y_done, p + 1)
                v.tensor_tensor(X[0:NP, t, :], PS[0:NP, 6 + t % 2, :], X[0:NP, t, :], ALU.add).then_inc(z_added, 1)

            dve.wait_ge(load["sw"], 48)
            units(0, 0)
            units(1, 1)
            dve.wait_ge(xn_stored, 16)
            dve.wait_ge(const_done, CONSTS + 9)
            dve.wait_ge(rank_ready, 1)
            BC = lambda c: blkc[:, c, :]
            link(v.tensor_copy(BC(0), PS[:, 4, NT * NEXP:(NT + 1) * NEXP]))
            link(v.tensor_tensor(prod[:, :, 0:NT], BC(0).rearrange("p (e o) -> p e o", o=1).to_broadcast([128, NEXP, NT]),
                                 thr[:, :].rearrange("p (o k) -> p o k", o=1).to_broadcast([128, NEXP, NT]), ALU.is_gt))
            link(v.tensor_reduce(BC(1), prod[:, :, 0:NT], AX.X, ALU.add))
            link(v.tensor_tensor(prod[:, :, :], BC(1).rearrange("p (o e) -> p o e", o=1).to_broadcast([128, NEXP, NEXP]),
                                 le[:, :, :], ALU.mult))
            link(v.tensor_reduce(BC(2), prod[:, :, :], AX.X, ALU.add))
            link(v.tensor_tensor(BC(3), BC(2), BC(1), ALU.subtract))
            link(v.tensor_scalar(BC(3), BC(3), float(BS), None, ALU.mult))
            link(v.tensor_tensor(R(posn), PS[0:NP, 4, 0:NT * NEXP].rearrange("p (t e) -> p t e", t=NT),
                                 blkc[0:NP, 3, :].rearrange("p (o e) -> p o e", o=1).to_broadcast([NP, NT, NEXP]), ALU.add))
            for k in range(TOPK):
                link(v.tensor_tensor(R(pr), R(oh[k]), R(posn), ALU.mult))
                link(v.tensor_reduce(slotf[0:NP, k, :], R(pr), AX.X, ALU.add))
            link(v.tensor_copy(slot_i[0:NP, :, :], slotf[0:NP, :, :]))
            flat = slot_i[0:NP, :, :].rearrange("p k t -> p (k t)")
            v.tensor_scalar(slot_b[0:NP, 0, :], flat, 7, None, ALU.logical_shift_right)
            link(v.tensor_scalar(slot_b[0:NP, 1, :], flat, BS - 1, None, ALU.bitwise_and))
            link(v.tensor_copy(slotp[0:NP, 0:2, :], slot_b[0:NP, :, :]))
            A2 = [NP, ASSIGN, BS]
            v.tensor_tensor(ohr[0:NP, :, :], iota_b[0:NP, :].rearrange("p (o n) -> p o n", o=1).to_broadcast(A2),
                            slotp[0:NP, 1, :].rearrange("p (a o) -> p a o", o=1).to_broadcast(A2), ALU.is_equal)
            A3 = [NP, ASSIGN, NB]
            link(v.tensor_tensor(ohb[0:NP, :, 1, :], iota_b[0:NP, 0:NB].rearrange("p (o n) -> p o n", o=1).to_broadcast(A3),
                                 slotp[0:NP, 0, :].rearrange("p (a o) -> p a o", o=1).to_broadcast(A3), ALU.is_equal))
            for k in range(TOPK):
                rows = slice(k * NT, (k + 1) * NT)
                link(v.tensor_tensor(ohb[0:NP, rows, 0, :], ohb[0:NP, rows, 1, :],
                                     nodef[0:NP, :].rearrange("p (a o) -> p a o", o=1).to_broadcast([NP, NT, NB]), ALU.mult))
            ins = v.tensor_tensor(ohb[0:NP, :, 1, :], ohb[0:NP, :, 1, :],
                                  wsel[0:NP, :, :].rearrange("p k (t o) -> p (k t) o", o=1).to_broadcast(A3), ALU.mult)
            ins.then_inc(slots_ready, 1)
            one = lambda c: ebf[0:1, c, :]
            link(v.tensor_tensor(cnt_e[0:1, :, :], cnt_e[0:1, :, :],
                                 blkc[0:1, 2, :].rearrange("p (o e) -> p o e", o=1).to_broadcast([1, NB, NEXP]), ALU.is_ge))
            link(v.tensor_reduce(ebf[0:1, 0, 0:NB], cnt_e[0:1, :, :], AX.X, ALU.add))
            link(v.tensor_scalar(ebf[0:1, 0, 0:NB], ebf[0:1, 0, 0:NB], float(NEXP - 1), None, ALU.min))
            link(v.memset(ebf[0:1, 1, 0:1], 1.0))
            link(v.tensor_tensor(ebf[0:1, 1, 1:NB], ebf[0:1, 0, 1:NB], ebf[0:1, 0, 0:NB - 1], ALU.not_equal))
            link(v.tensor_tensor(prodb[0:1, :, :], prodb[0:1, :, :],
                                 one(1).rearrange("p (o b) -> p o b", o=1).to_broadcast([1, NB, NB]), ALU.mult))
            link(v.tensor_reduce(one(2), prodb[0:1, :, :], AX.X, ALU.add))
            link(v.tensor_scalar(one(3), one(2), -1.0, 1.0 / NWB, ALU.add, ALU.mult))
            link(v.tensor_scalar(one(3), one(3), MAGIC, None, ALU.add))
            link(v.tensor_scalar(one(3), one(3), -MAGIC, None, ALU.add))
            link(v.scalar_tensor_tensor(out=one(4), in0=one(3), scalar=-float(NWB), in1=one(2), op0=ALU.mult, op1=ALU.add))
            link(v.tensor_scalar(one(4), one(4), float(WBUF), None, ALU.mult))
            v.tensor_copy(eb_i[0:1, 0, :], one(0))
            v.tensor_copy(eb_i[0:1, 1, :], one(4))
            v.tensor_copy(eb_i[0:1, 2, :], one(1))
            link(v.tensor_scalar(ebf[0:1, 3, 0:1], blkc[0:1, 2, NEXP - 1:NEXP], 0.5, -0.75, ALU.mult, ALU.add))
            link(v.tensor_scalar(ebf[0:1, 3, 0:1], ebf[0:1, 3, 0:1], MAGIC, None, ALU.add))
            link(v.tensor_scalar(ebf[0:1, 3, 0:1], ebf[0:1, 3, 0:1], -MAGIC, None, ALU.add))
            link(v.tensor_copy(eb_i[0:1, 3, 0:1], ebf[0:1, 3, 0:1]))
            z_add(0, 0)
            units(0, 2)
            z_add(1, 1)
            units(1, 3)
            dve.wait_ge(table_ps, 1)
            v.tensor_copy(tok[:, :], PS[:, 4, 0:NB])
            v.tensor_copy(wslot[:, :], PS[:, 4, NB:2 * NB]).then_inc(tables_ready, 1)
            dve.wait_ge(tables_ready, 1)
            last = last_pair(dve)
            z_add(2, 2)
            units(0, 4)
            z_add(3, 3)

            units(1, EARLY - 1)
            rows_copy(0, 0)
            z_add(EARLY - 2, EARLY - 2)
            units(0, EARLY, 0)
            rows_copy(1, 1)
            z_add(EARLY - 1, EARLY - 1)
            units(1, EARLY + 1, 1)
            rows_copy(0, 2)
            with dve.Fori(1, NB // 2) as i:
                with dve.If(i < last + 1):
                    units(0, i * 2 + EARLY, i * 2, lambda: rows_copy(1, i * 2 + 1))

                    def next_rows():
                        with dve.If(i < last):
                            rows_copy(0, i * 2 + 2)
                    units(1, i * 2 + (EARLY + 1), i * 2 + 1, next_rows)

            def gathered_sum(t):
                dve.wait_ge(back_in[t // 2], 16 * 4)
                link(v.tensor_tensor(GA[0:NP, t, :], GA[0:NP, t, :], GB[0:NP, t, :], ALU.add))

            def last_sum(t):
                v.tensor_tensor(X[0:NP, t, :], X[0:NP, t, :], GA[0:NP, t, :], ALU.add).then_inc(sum_ready, 1)

            for j in range(NT - EARLY):
                units(j % 2, last * 2 + (EARLY + 2 + j))
                if j:
                    z_add(EARLY + j - 1, last * 2 + (EARLY + 1 + j))
                if j >= 2:
                    for t in range(3 * (j - 2), 3 * (j - 1)):
                        gathered_sum(t)
                        last_sum(t)
            for t in range(EARLY, NT):
                gathered_sum(t)
            z_add(NT - 1, last * 2 + (NT + 1))
            dve.wait_ge(z_added, NT)
            for t in range(EARLY, NT):
                last_sum(t)


def kernel(**inputs):
    import numpy as np
    import concourse.bacc as bacc
    from concourse.bass_utils import run_bass_kernel_spmd

    g = {k: np.asarray(v) for k, v in inputs.items()}
    edges = lambda e: e.reshape(NG * CPG, CHUNK).T
    arrays = {
        "x": g["x"], "src": edges(g["src"]), "dst": edges(g["dst"]),
        "W": g["L0_gnn_W"], "gnn_b": g["L0_gnn_b"],
        "WaT": g["L0_ffn_Wa"].transpose(0, 2, 1), "ba": g["L0_ffn_ba"],
        "WsT": g["L0_ffn_Ws"].transpose(0, 2, 1), "bs": g["L0_ffn_bs"],
        "WlT": g["L1_gnn_W_l"].T, "WrT": g["L1_gnn_W_r"].T, "b_l": g["L1_gnn_b_l"],
        "gamma": g["L1_gnn_gamma"], "beta": g["L1_gnn_beta"],
        "gate_w": g["L1_ffn_gate_w"], "gate_b": g["L1_ffn_gate_b"],
        "w1": np.concatenate([g["L1_ffn_expert_w1"], g["L1_ffn_shared_w1"][None]]),
        "b1": np.concatenate([g["L1_ffn_expert_b1"], g["L1_ffn_shared_b1"][None]]),
        "w2": np.concatenate([g["L1_ffn_expert_w2"], g["L1_ffn_shared_w2"][None]]),
        "b2": np.concatenate([g["L1_ffn_expert_b2"], g["L1_ffn_shared_b2"][None]]),
        "act": np.concatenate([g["L1_ffn_expert_act"], g["L1_ffn_shared_act"][None]]),
    }
    arrays = {k: np.ascontiguousarray(v) for k, v in arrays.items()}
    nc = bacc.Bacc("TRN2", target_bir_lowering=False, num_devices=1)
    aps = {k: nc.dram_tensor("in_" + k, v.shape, mybir.dt.from_np(v.dtype), kind="ExternalInput").ap()
           for k, v in arrays.items()}
    out = nc.dram_tensor("out", (N, D), F32, kind="ExternalOutput").ap()
    build(nc, aps, out)
    r = run_bass_kernel_spmd(nc, [{"in_" + k: v for k, v in arrays.items()}], core_ids=[0])
    return r.results[0]["out"]
```
